# Optimizing a Trainium2 kernel written in Bass

```python
import numpy as np
import jax
import jax.numpy as jnp

def _softmax(x, axis=-1):
    return jax.nn.softmax(x, axis=axis)

def _gelu(x):
    return jax.nn.gelu(x, approximate=True)

def _silu(x):
    return jax.nn.silu(x)

def _sigmoid(x):
    return jax.nn.sigmoid(x)

def _layernorm(x, axis=-1, eps=1e-05):
    m = jnp.mean(x, axis=axis, keepdims=True)
    v = jnp.var(x, axis=axis, keepdims=True)
    return (x - m) / jnp.sqrt(v + eps)

def _scatter_add(tgt, idx, src, axis=0):
    return tgt.at[idx].add(src)

def _segment_sum(src, seg, n):
    return jax.ops.segment_sum(src, seg, n)
kernel_name = 'mk_seq_preln_d2_jaxref_r8_62e3b0'

def setup_inputs(seed: int=0):
    np.random.seed(seed)
    _w = jnp.asarray

    def _L0_attn_setup():
        import jax, jax.numpy as jnp
        import numpy as np
        D_MODEL, N_HEADS, BATCH, SEQ = (128, 16, 2, 256)

        def get_freqs(seq, n_dim):
            inv_freq = 1.0 / 10000.0 ** (jnp.arange(0, n_dim, 2, dtype=jnp.float32) / n_dim)
            pos = jnp.arange(seq, dtype=jnp.float32)
            return pos[:, None] * inv_freq[None, :]

        def rope(x, freq):
            cos = jnp.cos(freq)[None, :, None, :]
            sin = jnp.sin(freq)[None, :, None, :]
            x1, x2 = (x[..., ::2], x[..., 1::2])
            r1 = x1 * cos - x2 * sin
            r2 = x1 * sin + x2 * cos
            return jnp.stack([r1, r2], axis=-1).reshape(x.shape)
        key = jax.random.key(seed)
        ks = jax.random.split(key, 5)
        w_scale = 0.01
        return {'x': jax.random.normal(ks[0], (BATCH, SEQ, D_MODEL), dtype=jnp.float32), 'qw': jax.random.normal(ks[1], (D_MODEL, D_MODEL), dtype=jnp.float32) * w_scale, 'kw': jax.random.normal(ks[2], (D_MODEL, D_MODEL), dtype=jnp.float32) * w_scale, 'vw': jax.random.normal(ks[3], (D_MODEL, D_MODEL), dtype=jnp.float32) * w_scale, 'ow': jax.random.normal(ks[4], (D_MODEL, D_MODEL), dtype=jnp.float32) * w_scale}
    _L0_attn_in = _L0_attn_setup()

    def _L0_ffn_setup():
        import jax, jax.numpy as jnp
        import numpy as np
        B, N, D, E, R, K = (4, 256, 128, 8, 32, 2)
        key = jax.random.key(seed)
        ks = jax.random.split(key, 5)
        scale = 0.02
        return {'x': jax.random.normal(ks[0], (B, N, D), dtype=jnp.float32), 'gate_w': jax.random.normal(ks[1], (D, E), dtype=jnp.float32) * scale, 'Wu': jax.random.normal(ks[2], (E, D, R), dtype=jnp.float32) * scale, 'Wv': jax.random.normal(ks[3], (E, D, R), dtype=jnp.float32) * scale, 'Wo': jax.random.normal(ks[4], (E, R, D), dtype=jnp.float32) * scale}
    _L0_ffn_in = _L0_ffn_setup()

    def _L1_attn_setup():
        import jax, jax.numpy as jnp
        import numpy as np
        L, B, E, H = (256, 8, 128, 16)
        D = E // H
        EPS = 0.001
        key = jax.random.key(seed)
        k1, k2, k3 = jax.random.split(key, 3)
        scale_in = (2.0 / (3 * E + E)) ** 0.5
        scale_out = (2.0 / (E + E)) ** 0.5
        return {'query': jax.random.normal(k1, (L, B, E), dtype=jnp.float32), 'in_proj_weight': jax.random.normal(k2, (3 * E, E), dtype=jnp.float32) * scale_in, 'in_proj_bias': jnp.zeros((3 * E,), dtype=jnp.float32), 'out_w': jax.random.normal(k3, (E, E), dtype=jnp.float32) * scale_out, 'out_b': jnp.zeros((E,), dtype=jnp.float32)}
    _L1_attn_in = _L1_attn_setup()

    def _L1_ffn_setup():
        import jax, jax.numpy as jnp
        import numpy as np
        ALPHA = 2.0
        TOP_K = 2
        key = jax.random.key(seed)
        ks = jax.random.split(key, 8)
        B, S, D, H, E = (2, 256, 128, 512, 8)
        Er = E - 1
        s_in = 1.0 / np.sqrt(D)
        s_hid = 1.0 / np.sqrt(H)
        return {'x': jax.random.normal(ks[0], (B, S, D), dtype=jnp.float32), 'router_w': jax.random.normal(ks[1], (D, E), dtype=jnp.float32) * s_in, 'up_w': jax.random.normal(ks[2], (Er, D, H), dtype=jnp.float32) * s_in, 'gate_w': jax.random.normal(ks[3], (Er, D, H), dtype=jnp.float32) * s_in, 'down_w': jax.random.normal(ks[4], (Er, H, D), dtype=jnp.float32) * s_hid * 0.1, 'shared_up_w': jax.random.normal(ks[5], (D, H), dtype=jnp.float32) * s_in, 'shared_gate_w': jax.random.normal(ks[6], (D, H), dtype=jnp.float32) * s_in, 'shared_down_w': jax.random.normal(ks[7], (H, D), dtype=jnp.float32) * s_hid * 0.1}
    _L1_ffn_in = _L1_ffn_setup()
    _d = {'L0_attn_x': _L0_attn_in['x'], 'L0_attn_qw': _L0_attn_in['qw'], 'L0_attn_kw': _L0_attn_in['kw'], 'L0_attn_vw': _L0_attn_in['vw'], 'L0_attn_ow': _L0_attn_in['ow'], 'L0_ffn_gate_w': _L0_ffn_in['gate_w'], 'L0_ffn_Wu': _L0_ffn_in['Wu'], 'L0_ffn_Wv': _L0_ffn_in['Wv'], 'L0_ffn_Wo': _L0_ffn_in['Wo'], 'L1_attn_in_proj_weight': _L1_attn_in['in_proj_weight'], 'L1_attn_in_proj_bias': _L1_attn_in['in_proj_bias'], 'L1_attn_out_w': _L1_attn_in['out_w'], 'L1_attn_out_b': _L1_attn_in['out_b'], 'L1_ffn_router_w': _L1_ffn_in['router_w'], 'L1_ffn_up_w': _L1_ffn_in['up_w'], 'L1_ffn_gate_w': _L1_ffn_in['gate_w'], 'L1_ffn_down_w': _L1_ffn_in['down_w'], 'L1_ffn_shared_up_w': _L1_ffn_in['shared_up_w'], 'L1_ffn_shared_gate_w': _L1_ffn_in['shared_gate_w'], 'L1_ffn_shared_down_w': _L1_ffn_in['shared_down_w']}
    _x0 = _d['L0_attn_x']
    _d['L0_attn_x'] = jax.random.normal(jax.random.fold_in(jax.random.key(seed), 1), (4, 1024, 128), dtype=_x0.dtype)
    del _x0
    return _d

def reference(L0_attn_x, L0_attn_qw, L0_attn_kw, L0_attn_vw, L0_attn_ow, L0_ffn_gate_w, L0_ffn_Wu, L0_ffn_Wv, L0_ffn_Wo, L1_attn_in_proj_weight, L1_attn_in_proj_bias, L1_attn_out_w, L1_attn_out_b, L1_ffn_router_w, L1_ffn_up_w, L1_ffn_gate_w, L1_ffn_down_w, L1_ffn_shared_up_w, L1_ffn_shared_gate_w, L1_ffn_shared_down_w):

    def _L0_attn_ref(x, qw, kw, vw, ow):
        import jax, jax.numpy as jnp
        import numpy as np
        D_MODEL, N_HEADS, BATCH, SEQ = (128, 16, 2, 256)

        def get_freqs(seq, n_dim):
            inv_freq = 1.0 / 10000.0 ** (jnp.arange(0, n_dim, 2, dtype=jnp.float32) / n_dim)
            pos = jnp.arange(seq, dtype=jnp.float32)
            return pos[:, None] * inv_freq[None, :]

        def rope(x, freq):
            cos = jnp.cos(freq)[None, :, None, :]
            sin = jnp.sin(freq)[None, :, None, :]
            x1, x2 = (x[..., ::2], x[..., 1::2])
            r1 = x1 * cos - x2 * sin
            r2 = x1 * sin + x2 * cos
            return jnp.stack([r1, r2], axis=-1).reshape(x.shape)
        batch, seq, dim = x.shape
        n_heads = N_HEADS
        n_dim = dim // n_heads
        Q = (x @ qw).astype(jnp.float32).reshape(batch, seq, n_heads, n_dim)
        K = (x @ kw).astype(jnp.float32).reshape(batch, seq, n_heads, n_dim)
        V = (x @ vw).astype(jnp.float32).reshape(batch, seq, n_heads, n_dim)
        freq = get_freqs(seq, n_dim)
        Q = rope(Q, freq)
        K = rope(K, freq)
        Q = jnp.transpose(Q, (0, 2, 1, 3))
        K = jnp.transpose(K, (0, 2, 1, 3))
        V = jnp.transpose(V, (0, 2, 1, 3))
        scale = jnp.sqrt(jnp.float32(n_dim))
        score = jnp.einsum('bhqd,bhkd->bhqk', Q, K) / scale
        causal = jnp.tril(jnp.ones((1, 1, seq, seq), dtype=jnp.float32))
        score = score - 10000000000.0 * (1.0 - causal)
        score = score - jnp.max(score, axis=-1, keepdims=True)
        weights = jax.nn.softmax(score, axis=-1)
        attn = jnp.einsum('bhqk,bhkd->bhqd', weights, V)
        merged = jnp.transpose(attn, (0, 2, 1, 3)).reshape(batch, seq, dim)
        return (merged @ ow).astype(x.dtype)

    def _L0_ffn_ref(x, gate_w, Wu, Wv, Wo):
        import jax, jax.numpy as jnp
        import numpy as np
        B, N, D, E, R, K = (4, 256, 128, 8, 32, 2)
        logits = jnp.einsum('bnd,de->bne', x, gate_w)
        topv, topi = jax.lax.top_k(logits, K)
        w = jax.nn.softmax(topv, axis=-1)
        u = jnp.einsum('bnd,edr->bner', x, Wu)
        v = jnp.einsum('bnd,edr->bner', x, Wv)
        s = jax.nn.silu(u) * v
        Y = jnp.einsum('bner,erd->bned', s, Wo)
        y_sel = jnp.take_along_axis(Y, topi[..., None], axis=2)
        out = jnp.einsum('bnkd,bnk->bnd', y_sel, w)
        return out

    def _L1_attn_ref(query, in_proj_weight, in_proj_bias, out_w, out_b):
        import jax, jax.numpy as jnp
        import numpy as np
        L, B, E, H = (256, 8, 128, 16)
        D = E // H
        EPS = 0.001
        tgt_len, bsz, embed_dim = query.shape
        qkv = query @ in_proj_weight.T + in_proj_bias
        q, k, v = jnp.split(qkv, 3, axis=-1)

        def to_heads(x):
            return x.reshape(tgt_len, bsz, H, D).transpose(1, 0, 2, 3)
        q = jax.nn.relu(to_heads(q))
        k = jax.nn.relu(to_heads(k))
        v = to_heads(v)
        idx = jnp.pi / 2 * jnp.arange(1, tgt_len + 1, dtype=jnp.float32)
        theta = (idx / tgt_len)[None, :, None, None]
        sin_t, cos_t = (jnp.sin(theta), jnp.cos(theta))
        q_ = jnp.concatenate([q * sin_t, q * cos_t], axis=-1)
        k_ = jnp.concatenate([k * sin_t, k * cos_t], axis=-1)
        kv = jnp.einsum('bshd,bshm->bhmd', k_, v)
        z = 1.0 / jnp.maximum(jnp.einsum('blhd,bhd->blh', q_, k_.sum(axis=1)), EPS)
        attn = jnp.einsum('blhd,bhmd,blh->blhm', q_, kv, z)
        attn = attn.transpose(1, 0, 2, 3).reshape(tgt_len, bsz, embed_dim)
        return attn @ out_w.T + out_b

    def _L1_ffn_ref(x, router_w, up_w, gate_w, down_w, shared_up_w, shared_gate_w, shared_down_w):
        import jax, jax.numpy as jnp
        import numpy as np
        ALPHA = 2.0
        TOP_K = 2
        logits = jnp.einsum('bsd,de->bse', x, router_w)
        probs = jax.nn.softmax(logits, axis=-1)
        topk_vals, topk_idx = jax.lax.top_k(probs, TOP_K)
        top1_val = topk_vals[..., 0]
        top1_idx = topk_idx[..., 0]
        hid = jnp.einsum('bsd,edh->ebsh', x, up_w) * jax.nn.silu(jnp.einsum('bsd,edh->ebsh', x, gate_w))
        Er = up_w.shape[0]
        mask = (top1_idx[None, :, :] == jnp.arange(Er)[:, None, None]).astype(x.dtype)
        routed = jnp.einsum('ebsh,ehd,ebs->bsd', hid, down_w, mask)
        shid = jnp.einsum('bsd,dh->bsh', x, shared_up_w) * jax.nn.silu(jnp.einsum('bsd,dh->bsh', x, shared_gate_w))
        shared = jnp.einsum('bsh,hd->bsd', shid, shared_down_w)
        return ALPHA * top1_val[..., None] * routed + shared
    x = L0_attn_x
    x = x + _L0_attn_ref(_layernorm(x, axis=-1), L0_attn_qw, L0_attn_kw, L0_attn_vw, L0_attn_ow)
    x = x + _L0_ffn_ref(_layernorm(x, axis=-1), L0_ffn_gate_w, L0_ffn_Wu, L0_ffn_Wv, L0_ffn_Wo)
    x = x + _L1_attn_ref(_layernorm(x, axis=-1), L1_attn_in_proj_weight, L1_attn_in_proj_bias, L1_attn_out_w, L1_attn_out_b)
    x = x + _L1_ffn_ref(_layernorm(x, axis=-1), L1_ffn_router_w, L1_ffn_up_w, L1_ffn_gate_w, L1_ffn_down_w, L1_ffn_shared_up_w, L1_ffn_shared_gate_w, L1_ffn_shared_down_w)
    return x

_drawn_inputs = setup_inputs


def setup_inputs(seed=0):
    import zlib

    import numpy as np

    out = dict(_drawn_inputs(seed))
    spreads = {'L1_attn_in_proj_bias': (0.0, 0.1), 'L1_attn_out_b': (0.0, 0.1)}
    factors = {'L0_attn_qw': 8.0,
     'L0_attn_kw': 8.0,
     'L0_attn_vw': 8.0,
     'L0_attn_ow': 8.0,
     'L0_ffn_gate_w': 8.0,
     'L0_ffn_Wu': 8.0,
     'L0_ffn_Wv': 8.0,
     'L0_ffn_Wo': 8.0,
     'L1_ffn_router_w': 2.673}
    for name, (base, spread) in spreads.items():
        noise = np.random.default_rng([zlib.crc32(name.encode()), seed]).standard_normal(out[name].shape)
        drawn = base * np.exp(spread * noise) if base else spread * noise
        out[name] = jnp.asarray(drawn.astype(out[name].dtype))
    for name, factor in factors.items():
        out[name] = (out[name] * factor).astype(out[name].dtype)
    return out
```

```python
import numpy as np
import concourse.bass as bass
from concourse import mybir
from contextlib import ExitStack

F32 = mybir.dt.float32
BF16 = mybir.dt.bfloat16
I32 = mybir.dt.int32
U32 = mybir.dt.uint32
ALU = mybir.AluOpType
ACT = mybir.ActivationFunctionType
AX = mybir.AxisListType

P = 128
NBATCH, SEQ, D = 4, 1024, 128
TILES = NBATCH * SEQ // P
TPB = SEQ // P
HEADS, HD = 16, 8
QUADS = NBATCH * HEADS // 4
SLOTS = 6
ROWS = SLOTS * HD
EPS = 1e-5
Q_PART = [0, 1, 2, 0, 1, 0]
K_PART = [0, 0, 0, 1, 1, 2]
QSCALE = float(1.0 / np.sqrt(HD))
MASKED = -1.0e30

UNITS = [(h, i, c * 512, min(512, (i + 1) * P - c * 512))
         for h in range(4) for i in range(TPB) for c in range((i * P + P - 1) // 512 + 1)]
NUNITS = len(UNITS) + 1
LATE_T = 4
EARLY = 12


def wait_apart(eng, sem, value, passed):
    eng.wait_ge(sem, value)
    eng.sem_inc(passed, 1)


def tables():
    inv = (np.float32(1.0) / np.power(np.float32(10000.0), np.arange(0, HD, 2, dtype=np.float32) / np.float32(HD))).astype(np.float32)
    freq = np.arange(SEQ, dtype=np.float32)[:, None] * inv[None, :]
    f = np.arange(D)
    ang = freq[:, (f % HD) // 2].T.astype(np.float64)
    sign = np.where(f % 2 == 0, -1.0, 1.0)[:, None]
    return np.cos(ang).astype(np.float32), (np.sin(ang) * sign).astype(np.float32)


def project_and_rotate(nc, X, VS, x, cos, sin, wq, wqs, wk, wks, wv, QD, KD):
    with ExitStack() as ctx:
        def sb(name, shape, dt=F32):
            return ctx.enter_context(nc.sbuf_tensor(name, shape, dt))

        def sem(name):
            return ctx.enter_context(nc.semaphore(name))

        ident = sb("a_ident", [P, P])
        W = sb("a_w", [P, 5, D])
        tab = sb("a_tab", [P, 2, SEQ])
        half, eps = sb("a_minus_half", [P, TPB]), sb("a_eps", [P, TPB])
        stats = sb("a_stats", [P, TPB, 6])
        mv = sb("a_mean_var", [P, TPB, 2])
        rstd = sb("a_rstd", [P, TPB])
        Y = sb("a_y", [P, TPB, D])
        YT = sb("a_yT", [P, SEQ])
        rot = [sb(f"a_rot{k}", [P, 2, 512]) for k in range(2)]
        parts = [sb(f"a_parts{k}", [P, 3, NBATCH * SEQ], BF16) for k in range(2)]
        pT = [ctx.enter_context(nc.psum_tensor(f"a_pT{i}", [P, 4, P], F32)) for i in range(2)]
        pQ = [ctx.enter_context(nc.psum_tensor(f"a_pQ{i}", [P, 512], F32)) for i in range(4)]
        pV = ctx.enter_context(nc.psum_tensor("a_pV", [P, 4, D], F32))

        s_x, s_w, s_id = sem("a_x_loaded"), sem("a_w_loaded"), sem("a_ident_made")
        s_st, s_mv, s_rstd = sem("a_stats_done"), sem("a_mean_var_done"), sem("a_rstd_steps")
        s_y, s_t, s_yt = sem("a_y_done"), sem("a_transposed"), sem("a_yT_done")
        s_qk, s_v, s_vc = sem("a_projected"), sem("a_v_projected"), sem("a_v_copied")
        s_rot, s_hi, s_mid = sem("a_rot_steps"), sem("a_hi_done"), sem("a_mid_done")
        s_part, s_store = sem("a_parts_done"), sem("a_parts_stored")
        s_pass = sem("a_passed")

        with nc.Block() as block:
            @block.sync
            def _(sp):
                sp.dma_start(X[:], x.rearrange("b (t p) d -> p (b t) d", p=P)).then_inc(s_x, 16)
                for k, w in enumerate((wq, wqs, wk, wks, wv)):
                    sp.dma_start(W[:, k, :], w).then_inc(s_w, 16)
                sp.dma_start(tab[:, 0, :], cos).then_inc(s_w, 16)
                sp.dma_start(tab[:, 1, :], sin).then_inc(s_w, 16)
                with sp.Fori(0, NBATCH) as b:
                    sp.wait_ge(s_part, b * 4 + 4)
                    for k, (dst, order) in enumerate(((QD, Q_PART), (KD, K_PART))):
                        for s, part in enumerate(order):
                            sp.dma_start(
                                dst[bass.ts(b, 4), :, s * HD:(s + 1) * HD, :].rearrange("g h d t -> (g h) d t"),
                                parts[k][:, part, bass.ts(b, SEQ)]).then_inc(s_store, 16)
                sp.wait_ge(s_store, NBATCH * 2 * SLOTS * 16)

            @block.gpsimd
            def _(gp):
                gp.memset(half[:], -0.5)
                gp.memset(eps[:], EPS).then_inc(s_id, 1)
                gp.memset(ident[:], 0.0).then_inc(s_id, 1)
                gp.wait_ge(s_id, 2)
                gp.affine_select(out=ident[:], in_=ident[:], compare_op=ALU.not_equal, fill=1.0, base=0,
                                 pattern=[[-1, P]], channel_multiplier=1).then_inc(s_id, 1)
                with gp.Fori(0, NBATCH) as b:
                    gp.wait_ge(s_mv, b + 1)
                    gp.tensor_tensor(rstd[:], mv[:, :, 1], eps[:], ALU.add).then_inc(s_rstd, 1)
                    gp.wait_ge(s_rstd, b * 2 + 1)
                    gp.tensor_tensor(rstd[:], rstd[:], half[:], ALU.pow).then_inc(s_rstd, 1)

            @block.vector
            def _(dve):
                dve.wait_ge(s_x, 16)
                dve.wait_ge(s_w, 16 * 7)
                with dve.Fori(0, NBATCH) as b:
                    for t in range(TPB):
                        ins = dve.bn_stats(stats[:, t, :], X[:, b * TPB + t, :])
                    ins.then_inc(s_st, 1)
                    wait_apart(dve, s_st, b + 1, s_pass)
                    for t in range(TPB):
                        ins = dve.bn_aggr(mv[:, t, :], stats[:, t, :])
                    ins.then_inc(s_mv, 1)
                    dve.wait_ge(s_rstd, b * 2 + 2)
                    dve.wait_ge(s_mv, b + 1)
                    dve.wait_ge(s_t, b * 2)
                    for t in range(TPB):
                        ins = dve.tensor_scalar(Y[:, t, :], X[:, b * TPB + t, :], mv[:, t, 0:1], rstd[:, t:t + 1],
                                                ALU.subtract, ALU.mult)
                        if t % 4 == 3:
                            ins.then_inc(s_y, 1)
                    for half_ in range(2):
                        cols = slice(half_ * 512, half_ * 512 + 512)
                        for k in range(2):
                            n = half_ * 2 + k
                            dve.wait_ge(s_qk, b * 4 + n + 1)
                            dve.tensor_tensor(rot[k][:, 0, :], pQ[2 * k][:], tab[:, 0, cols], ALU.mult)
                            dve.tensor_tensor(rot[k][:, 1, :], pQ[2 * k + 1][:], tab[:, 1, cols],
                                              ALU.mult).then_inc(s_rot, 1)
                            dve.wait_ge(s_rot, b * 12 + n * 3 + 1)
                            dve.tensor_tensor(rot[k][:, 0, :], rot[k][:, 0, :], rot[k][:, 1, :],
                                              ALU.add).then_inc(s_rot, 1)
                            dve.wait_ge(s_rot, b * 12 + n * 3 + 2)
                            dve.wait_ge(s_hi, b * 4 + n + 1)
                            dve.tensor_tensor(rot[k][:, 1, :], rot[k][:, 0, :],
                                              parts[k][:, 0, bass.ds(b * SEQ + half_ * 512, 512)],
                                              ALU.subtract).then_inc(s_rot, 1)
                            dve.wait_ge(s_rot, b * 12 + n * 3 + 3)
                            dve.wait_ge(s_mid, b * 4 + n + 1)
                            dve.tensor_tensor(parts[k][:, 2, bass.ds(b * SEQ + half_ * 512, 512)],
                                              rot[k][:, 1, :],
                                              parts[k][:, 1, bass.ds(b * SEQ + half_ * 512, 512)],
                                              ALU.subtract).then_inc(s_part, 1)

            @block.scalar
            def _(act):
                with act.Fori(0, NBATCH) as b:
                    for i in range(2):
                        act.wait_ge(s_t, b * 2 + i + 1)
                        act.wait_ge(s_v, b * 2 + i)
                        act.activation(YT[:, i * 512:(i + 1) * 512], pT[i][:].rearrange("p a b -> p (a b)"),
                                       ACT.Copy).then_inc(s_yt, 1)
                    for half_ in range(2):
                        for k in range(2):
                            n = half_ * 2 + k
                            span = bass.ds(b * SEQ + half_ * 512, 512)
                            act.wait_ge(s_rot, b * 12 + n * 3 + 2)
                            act.activation(parts[k][:, 0, span], rot[k][:, 0, :], ACT.Copy).then_inc(s_hi, 1)
                            act.wait_ge(s_rot, b * 12 + n * 3 + 3)
                            act.activation(parts[k][:, 1, span], rot[k][:, 1, :], ACT.Copy).then_inc(s_mid, 1)
                        act.wait_ge(s_v, b * 2 + half_ + 1)
                        act.activation(
                            VS[:, bass.ts(b, 4), 4 * half_:4 * half_ + 4, :],
                            pV[:].rearrange("p j (g f) -> p g j f", g=4), ACT.Copy).then_inc(s_vc, 1)

            @block.tensor
            def _(pe):
                pe.wait_ge(s_id, 3)
                pe.wait_ge(s_w, 16 * 7)
                with pe.Fori(0, NBATCH) as b:
                    for i in range(2):
                        pe.wait_ge(s_y, b * 2 + i + 1)
                        for t in range(4):
                            ins = pe.transpose(pT[i][:, t, :], Y[:, 4 * i + t, :], ident[:])
                        ins.then_inc(s_t, 1)
                    for half_ in range(2):
                        cols = slice(half_ * 512, half_ * 512 + 512)
                        pe.wait_ge(s_yt, b * 2 + half_ + 1)
                        for k in range(2):
                            pe.wait_ge(s_rot, b * 12 + (3 * k + 1 if half_ else 0))
                            pe.matmul(pQ[2 * k][:], W[:, 2 * k, :], YT[:, cols], start=True, stop=True)
                            pe.matmul(pQ[2 * k + 1][:], W[:, 2 * k + 1, :], YT[:, cols], start=True,
                                      stop=True).then_inc(s_qk, 1)
                        pe.wait_ge(s_vc, b * 2 + half_)
                        for t in range(4):
                            ins = pe.matmul(pV[:, t, :], YT[:, (4 * half_ + t) * P:(4 * half_ + t + 1) * P],
                                            W[:, 4, :], start=True, stop=True)
                        ins.then_inc(s_v, 1)


def attend(nc, VS, QD, KD, MD, ND):
    with ExitStack() as ctx:
        def sb(name, shape, dt=F32):
            return ctx.enter_context(nc.sbuf_tensor(name, shape, dt))

        def sem(name):
            return ctx.enter_context(nc.semaphore(name))

        def both(name, shape, dt=F32):
            return [sb(f"{name}{i}", shape, dt) for i in range(2)]

        Qz, Kz = both("b_Qz", [P, 4, SEQ], BF16), both("b_Kz", [P, 4, SEQ], BF16)
        Qm, Km = both("b_Qm", [P, 2, SEQ], BF16), both("b_Km", [P, 2, SEQ], BF16)
        ones = sb("b_ones", [3, 2 * SEQ], BF16)
        Vq = both("b_Vq", [P, TPB, 4, 32])
        probs = both("b_probs", [P, 4, SEQ])
        raw = both("b_raw", [P, SEQ])
        identb = sb("b_ident", [P, P], BF16)
        maskb = sb("b_mask", [P, P], BF16)
        mx = both("b_mx", [P, 4, TPB, 2])
        res = sb("b_res", [P, 4, TPB])
        nm = both("b_negmax", [P, 2, 3, 2, TPB], BF16)
        MT = sb("b_negmaxT", [96, P], BF16)
        st = [ctx.enter_context(nc.psum_tensor(f"b_st{i}", [P, SEQ], F32)) for i in range(2)]
        acc = ctx.enter_context(nc.psum_tensor("b_acc", [P, SEQ], F32))
        mb = [ctx.enter_context(nc.psum_tensor(f"b_mb{i}", [P, 512], F32)) for i in range(2)]

        s_zero, s_ones, s_cst = sem("b_zeroed"), sem("b_ones_set"), sem("b_const_steps")
        s_ks, s_qs = [[sem(f"b_{n}_loaded{i}") for i in range(2)] for n in ("max_stacks", "exp_stacks")]
        s_mm, s_red, s_fin = sem("b_unit_made"), sem("b_unit_reduced"), sem("b_negmax_steps")
        s_mt, s_md, s_mrow = sem("b_negmaxT_copied"), sem("b_negmax_stored"), sem("b_negmax_loaded")
        s_st, s_exp, s_mask = sem("b_scores"), sem("b_exp_done"), sem("b_masked")
        s_pv, s_raw, s_nd = sem("b_pv_done"), sem("b_raw_done"), [sem(f"b_raw_stored{i}") for i in range(2)]
        s_vq, s_vone = sem("b_v_ready"), sem("b_v_ones")
        s_pass = sem("b_passed")
        LOAD = 4 * 16
        NT = QUADS

        def number(n):
            return n if n < LATE_T else n + 1

        def stream(first, second):
            out = [(first, n) for n in range(EARLY, len(UNITS))]
            if second:
                out += [(first + 1, n) for n in range(LATE_T)]
            out.append((first, "T"))
            if second:
                out += [(first + 1, n) for n in range(LATE_T, EARLY)]
            return out

        def spread(units):
            cost = [(UNITS[n][3] if n != "T" else P) + 70 for _, n in units]
            lens = [SEQ - P * (k // 4) + 120 for k in range(32)]
            plan, spent, passed, at = [], 0, 0, 0
            for k in range(32):
                passed += lens[k]
                now = []
                while at < len(units) and (spent + cost[at] / 2) * sum(lens) <= passed * sum(cost):
                    spent += cost[at]
                    now.append(units[at])
                    at += 1
                plan.append(now)
            plan[-1] += units[at:]
            return plan

        PROLOGUE = [(0, n) for n in range(EARLY)] + stream(0, True)
        FULL = spread(stream(1, True))
        LAST = spread(stream(1, False))

        def unit_number(u, ahead, n, last):
            if n == "T":
                return (u + ahead + 1) * NUNITS + (0 if last else LATE_T)
            return (u + ahead) * NUNITS + number(n)

        def unit_parity(par, ahead, n, last):
            return unit_number(par, ahead, n, last) % 2

        def skips(u, ahead, n):
            return 2 if u is None and ahead == 0 and n == LATE_T - 1 else 1

        def each_quad(eng, prologue, body, epilogue):
            if prologue:
                prologue()
            body(0, 0, -1, FULL, False)
            with eng.Fori(0, 6) as v:
                body(v * 2 + 1, 1, v, FULL, False)
                body(v * 2 + 2, 0, v, FULL, False)
            body(13, 1, 6, FULL, False)
            body(14, 0, 6, LAST, True)
            body(15, 1, 7, [[]] * 32, True)
            if epilogue:
                epilogue()

        def half_of(u, par, v, ahead):
            return v + (1 + (par + 1) % 2 + ahead) // 2 if not isinstance(u, int) else (u + ahead) // 2

        with nc.Block() as block:
            @block.sync
            def _(sp):
                def stacks(zeroed, moving, src_z, src_m, u, par, s):
                    for e in range(2):
                        rows = slice(64 * e, 64 * e + ROWS)
                        sp.dma_start(zeroed[par][rows, e::2, :], src_z[bass.ds(u, 1), e::2, :, :]
                                     .rearrange("u h r t -> (u r) h t")).then_inc(s[par], 16)
                        sp.dma_start(moving[par][rows, :, :], src_m[bass.ds(u, 1), e::2, :, :]
                                     .rearrange("u h r t -> (u r) h t")).then_inc(s[par], 16)

                def maxima(u, ahead, par, last):
                    sp.wait_ge(s_red, unit_number(u, ahead, "T", last) + 1)
                    sp.dma_start(MD[:, :], MT[:, :]).then_inc(s_md, 16)
                    sp.wait_ge(s_md, (u + ahead) * 16 + 16)
                    for e in range(2):
                        sp.dma_start(Qm[par][64 * e + ROWS:64 * e + ROWS + 3, :, :],
                                     MD[48 * e:48 * e + 48, :].rearrange("(c p i) q -> c p (i q)", c=3, p=2)) \
                          .then_inc(s_mrow, 16)

                def store_raw(u, par, ):
                    sp.wait_ge(s_raw, u + 1)
                    for h in range(4):
                        sp.dma_start(ND[bass.ds(u, 1), h, :, :].rearrange("u r t -> (u r) t"),
                                     raw[par][32 * h:32 * h + 16, :]).then_inc(s_nd[par], 16)

                def prologue():
                    sp.wait_ge(s_zero, 2)
                    for par in range(2):
                        for e in range(2):
                            sp.dma_start(Kz[par][64 * e + ROWS:64 * e + ROWS + 3, e::2, :],
                                         ones[:, :].rearrange("c (h t) -> c h t", h=2)).then_inc(s_ones, 16)
                    stacks(Qz, Km, QD, KD, 0, 0, s_ks)
                    stacks(Kz, Qm, KD, QD, 0, 0, s_qs)
                    stacks(Qz, Km, QD, KD, 1, 1, s_ks)
                    maxima(0, 0, 0, False)

                def body(u, par, v, plan, last):
                    static = isinstance(u, int)
                    if not (static and u + 1 >= NT):
                        if not (static and u == 0):
                            sp.wait_ge(s_exp, u * 32)
                        stacks(Kz, Qm, KD, QD, u + 1, 1 - par, s_qs)
                    if not (static and u + 2 >= NT):
                        sp.wait_ge(s_red, (u + 1) * NUNITS)
                        stacks(Qz, Km, QD, KD, u + 2, par, s_ks)
                    if not (static and u == 0):
                        store_raw(u - 1, 1 - par)
                    if not (static and u + 1 >= NT):
                        maxima(u, 1, 1 - par, last)

                def epilogue():
                    store_raw(NT - 1, (NT - 1) % 2)
                    for par in range(2):
                        sp.wait_ge(s_nd[par], NT // 2 * 64)

                each_quad(sp, prologue, body, epilogue)

            @block.vector
            def _(dve):
                for t in (Qz[0], Qz[1], Km[0], Km[1]):
                    ins = dve.memset(t[:].bitcast(U32), 0)
                ins.then_inc(s_zero, 1)

                def unit(u, ahead, n, par, last):
                    num = unit_number(u, ahead, n, last)
                    bank = mb[unit_parity((par + ahead) % 2, ahead, n, last)]
                    dve.wait_ge(s_mm, num + 1)
                    if n == "T":
                        q = u + ahead
                        if not (isinstance(q, int) and q == 0):
                            dve.wait_ge(s_md, q * 16)
                        dve.tensor_copy(MT[:, :], bank[0:96, 0:P // 2].bitcast(BF16)).then_inc(s_red, 1)
                        return
                    h, i, k0, w = UNITS[n]
                    dve.tensor_reduce(mx[par][:, h, i, k0 // 512:k0 // 512 + 1], bank[:, 0:w], AX.X, ALU.max) \
                       .then_inc(s_red, 2 if isinstance(u, int) and u + ahead == 0 and n == LATE_T - 1 else 1)
                    if n == len(UNITS) - 1:
                        q = u + ahead
                        dve.wait_ge(s_red, num + 1)
                        dve.tensor_tensor(mx[par][:, :, 4:8, 0], mx[par][:, :, 4:8, 0], mx[par][:, :, 4:8, 1],
                                          ALU.max).then_inc(s_fin, 1)
                        dve.wait_ge(s_fin, q * 5 + 1)
                        if not (isinstance(q, int) and q < 2):
                            dve.wait_ge(s_mm, (q - 1) * NUNITS + LATE_T + 1)
                        m = mx[par][:, :, :, 0].rearrange("q (p e) i -> q e p i", e=2)
                        neg = nm[par]
                        r = res[:, :, :].rearrange("q (e p) i -> q e p i", e=2)
                        dve.tensor_scalar(neg[:, :, 0, :, :], m, -1.0, None, ALU.mult).then_inc(s_fin, 1)
                        dve.wait_ge(s_fin, q * 5 + 2)
                        for e in range(2):
                            ins = dve.scalar_tensor_tensor(out=r[:, e], in0=m[:, e], scalar=-1.0, in1=neg[:, e, 0],
                                                           op0=ALU.mult, op1=ALU.subtract)
                        ins.then_inc(s_fin, 1)
                        dve.wait_ge(s_fin, q * 5 + 3)
                        dve.tensor_copy(neg[:, :, 1, :, :], r).then_inc(s_fin, 1)
                        dve.wait_ge(s_fin, q * 5 + 4)
                        dve.tensor_tensor(neg[:, :, 2, :, :], r, neg[:, :, 1, :, :], ALU.subtract).then_inc(s_fin, 1)
                        dve.wait_ge(s_fin, q * 5 + 5)

                def prologue():
                    for ahead, n in PROLOGUE:
                        unit(0, ahead, n, ahead, False)

                def body(u, par, v, plan, last):
                    for units in plan:
                        for ahead, n in units:
                            unit(u, ahead, n, (par + ahead) % 2, last)

                each_quad(dve, prologue, body, None)

            @block.gpsimd
            def _(gp):
                for t in (Kz[0], Kz[1], Qm[0], Qm[1]):
                    ins = gp.memset(t[:].bitcast(U32), 0)
                gp.memset(ones[:], 1.0).then_inc(s_zero, 1)
                gp.memset(identb[:], 0.0)
                gp.memset(maskb[:], 0.0).then_inc(s_cst, 1)
                gp.wait_ge(s_cst, 1)
                gp.affine_select(out=identb[:], in_=identb[:], compare_op=ALU.not_equal, fill=1.0, base=0,
                                 pattern=[[-1, P]], channel_multiplier=1)
                gp.affine_select(out=maskb[:], in_=maskb[:], compare_op=ALU.is_ge, fill=MASKED, base=0,
                                 pattern=[[-1, P]], channel_multiplier=1).then_inc(s_cst, 1)
                for t in Vq:
                    gp.memset(t[:], 0.0).then_inc(s_vone, 1)
                gp.wait_ge(s_vone, 2)
                for t in Vq:
                    gp.memset(t[:, :, :, HD:2 * HD], 1.0).then_inc(s_vone, 1)

                def take_v(u, par):
                    gp.tensor_copy(Vq[par][:, :, :, 0:HD],
                                   VS[:, bass.ds(u, 1), :, :].rearrange("p u j (h f) -> p (u j) h f", h=4)) \
                      .then_inc(s_vq, 1)

                def prologue():
                    gp.wait_ge(s_vone, 4)
                    take_v(0, 0)

                def body(u, par, v, plan, last):
                    static = isinstance(u, int)
                    for j in range(TPB):
                        wait_apart(gp, s_exp, u * 32 + 4 * j + 4, s_pass)
                        diag = probs[j % 2][:, :, P * j:P * j + P]
                        gp.affine_select(out=diag, in_=diag, compare_op=ALU.is_ge, fill=0.0, base=0,
                                         pattern=[[0, 4], [1, P]], channel_multiplier=-1).then_inc(s_mask, 1)
                        if j == 1 and not (static and u + 1 >= NT):
                            if not (static and u == 0):
                                gp.wait_ge(s_pv, u * 8)
                            take_v(u + 1, 1 - par)

                each_quad(gp, prologue, body, None)

            @block.scalar
            def _(act):
                def evacuate(u, par, v):
                    act.wait_ge(s_pv, (u + 1) * 8)
                    if not (isinstance(u, int) and u < 2):
                        act.wait_ge(s_nd[par], v * 64)
                    act.activation(raw[par][:, :], acc[:], ACT.Copy).then_inc(s_raw, 1)

                def body(u, par, v, plan, last):
                    static = isinstance(u, int)
                    for j in range(TPB):
                        for h in range(4):
                            k = 4 * j + h
                            act.wait_ge(s_st, u * 32 + k + 1)
                            if h == 0 and not (static and u == 0 and j < 2):
                                act.wait_ge(s_pv, u * 8 + j - 1)
                            act.activation(probs[j % 2][:, h, P * j:SEQ], st[h % 2][:, P * j:SEQ], ACT.Exp,
                                           scale=QSCALE).then_inc(s_exp, 1)
                        if j == 0 and not (static and u == 0):
                            evacuate(u - 1, 1 - par, v)

                each_quad(act, None, body, lambda: evacuate(NT - 1, 1, 7))

            @block.tensor
            def _(pe):
                def unit(u, ahead, n, par, last):
                    num = unit_number(u, ahead, n, last)
                    bank = mb[unit_parity((par + ahead) % 2, ahead, n, last)]
                    if not (isinstance(num, int) and num < 2):
                        if not (isinstance(num, int) and num == 2):
                            pe.wait_ge(s_red, num - 1)
                        else:
                            pe.wait_ge(s_red, 1)
                    if n == "T":
                        pe.wait_ge(s_fin, (u + ahead) * 5 + 5)
                        pe.transpose(bank[0:96, 0:P // 2].bitcast(BF16),
                                     nm[par][:, :, :, :, :].rearrange("q e c p i -> q (e c p i)"),
                                     identb[:]).then_inc(s_mm, 1)
                        return
                    h, i, k0, w = UNITS[n]
                    if n == 0:
                        pe.wait_ge(s_ks[par], half_index[0](u, ahead) * LOAD + LOAD)
                    diagonal = k0 + w == (i + 1) * P
                    ins = pe.matmul(bank[:, 0:w], Qz[par][:, h, P * i:P * i + P], Km[par][:, h // 2, k0:k0 + w],
                                    start=True, stop=not diagonal)
                    if diagonal:
                        ins = pe.matmul(bank[:, w - P:w], identb[:], maskb[:], start=False, stop=True)
                    ins.then_inc(s_mm, 2 if isinstance(u, int) and u + ahead == 0 and n == LATE_T - 1 else 1)

                half_index = [None]

                def scores(u, par, v, k):
                    j, h = k // 4, k % 4
                    static0 = isinstance(u, int) and u == 0
                    if k == 0:
                        pe.wait_ge(s_qs[par], half_index[0](u, 0) * LOAD + LOAD)
                        pe.wait_ge(s_mrow, u * 32 + 32)
                    if not (static0 and k < 2):
                        pe.wait_ge(s_exp, u * 32 + k - 1)
                    for c in range(2):
                        a = max(P * j, 512 * c)
                        if a < 512 * (c + 1):
                            ins = pe.matmul(st[h % 2][:, a:512 * (c + 1)], Kz[par][:, h, P * j:P * j + P],
                                            Qm[par][:, h // 2, a:512 * (c + 1)], start=True, stop=True)
                    ins.then_inc(s_st, 1)

                def values(u, par, j):
                    pe.wait_ge(s_mask, u * 8 + j + 1)
                    if j == 0:
                        pe.wait_ge(s_vq, u + 1)
                        if not (isinstance(u, int) and u == 0):
                            pe.wait_ge(s_raw, u)
                    for c in range(2):
                        a = max(P * j, 512 * c)
                        for h in range(4):
                            if a < 512 * (c + 1):
                                ins = pe.matmul(acc[32 * h:32 * h + 32, a:512 * (c + 1)], Vq[par][:, j, h, :],
                                                probs[j % 2][:, h, a:512 * (c + 1)], start=(j == 0),
                                                stop=(j == 4 * c + 3))
                    ins.then_inc(s_pv, 1)

                def prologue():
                    pe.wait_ge(s_zero, 2)
                    pe.wait_ge(s_cst, 2)
                    pe.wait_ge(s_ones, 64)
                    half_index[0] = lambda u, ahead: (u + ahead) // 2
                    for ahead, n in PROLOGUE:
                        unit(0, ahead, n, ahead, False)

                def body(u, par, v, plan, last):
                    static = isinstance(u, int)
                    half_index[0] = (lambda u_, ahead: (u_ + ahead) // 2) if static else \
                        (lambda u_, ahead: v + ((1 if par else 2) + ahead) // 2)
                    for k in range(32):
                        scores(u, par, v, k)
                        if k % 4 == 1:
                            if k >= 4:
                                values(u, par, k // 4 - 1)
                            elif not (static and u == 0):
                                values(u - 1, 1 - par, TPB - 1)
                        for ahead, n in plan[k]:
                            unit(u, ahead, n, (par + ahead) % 2, last)

                each_quad(pe, prologue, body, lambda: values(NT - 1, 1, TPB - 1))


def head_sums():
    f = np.arange(D) // HD
    same = (f[:, None] == f[None, :]).astype(np.float64)
    return np.stack([same * np.cos(np.pi / 2 * n / NBATCH) for n in range(NBATCH)]).astype(np.float32)


def middle_layers(nc, X, Y4, L2, ND, w):
    with ExitStack() as ctx:
        def sb(name, shape, dt=F32):
            return ctx.enter_context(nc.sbuf_tensor("c_" + name, shape, dt))

        def sem(name):
            return ctx.enter_context(nc.semaphore("c_" + name))

        def bank(name):
            return ctx.enter_context(nc.psum_tensor("c_" + name, [P, 4, P], F32))

        B = NBATCH
        EXP, R = 8, 32
        HC = 4
        ident, half, eps = sb("ident", [P, P]), sb("half", [P, B]), sb("eps", [P, B])
        ow, gate, Wuv = sb("ow", [P, D]), sb("gate", [P, EXP]), sb("Wuv", [P, 2, EXP, R])
        Wo, Win, outw = sb("Wo", [P, 2, D]), sb("Win", [P, 3, D]), sb("outw", [P, D])
        bias, outb, router = sb("bias", [P, 3]), sb("outb", [P, D]), sb("router", [P, 8])
        sums, tri = sb("sums", [P, B, D]), sb("tri", [P, EXP, EXP])
        num = [sb(f"num{i}", [P, B, P]) for i in range(2)]
        den = [sb(f"den{i}", [P, B, P]) for i in range(2)]
        attT = sb("attT", [P, B, P])
        st1, mv1, rs1 = sb("st1", [P, B, 6]), sb("mv1", [P, B, 2]), sb("rs1", [P, B])
        st2, mv2, rs2 = sb("st2", [P, B, 6]), sb("mv2", [P, B, 2]), sb("rs2", [P, B])
        y, yT = sb("y", [P, B, D]), sb("yT", [P, B, P])
        lg, rank = sb("lg", [P, B, EXP]), sb("rank", [P, B, EXP])
        cmp, eq = sb("cmp", [P, B, EXP, EXP]), sb("eq", [P, B, EXP, EXP])
        hs, th, wt = sb("hs", [P, B]), sb("th", [P, B, EXP]), sb("wt", [P, B, EXP])
        su = [sb(f"su{i}", [P, EXP, R]) for i in range(2)]
        sv = [sb(f"sv{i}", [P, EXP, R]) for i in range(2)]
        sw = [sb(f"sw{i}", [P, 2, P]) for i in range(2)]
        swT = sb("swT", [P, B, 2, P])
        z, zT, xb = sb("z", [P, B, D]), sb("zT", [P, B, P]), sb("xb", [P, B, D])
        qkv = sb("qkv", [P, 3, B, P])
        prod = [sb(f"prod{i}", [P, B, P]) for i in range(2)]
        av = [sb(f"av{i}", [P, B, P]) for i in range(2)]
        nsum, dsum, at = sb("nsum", [P, B, P]), sb("dsum", [P, B, P]), sb("at", [P, B, P])
        yT4, z4 = sb("yT4", [P, B, P]), sb("z4", [P, B, D])
        sg = [sb(f"sg{i}", [P, B, P]) for i in range(2)]
        hid = sb("hid", [P, HC, B, P])
        O1, T1, UV0, UV1 = bank("O1"), bank("T1"), bank("UV0"), bank("UV1")
        O2, T2, A0, A1 = bank("O2"), bank("T2"), bank("A0"), bank("A1")
        UV, A = [UV0, UV1], [A0, A1]

        s_w, s_cst = sem("weights_loaded"), sem("const_steps")
        s_nd = [sem(f"att_loaded{i}") for i in range(2)]
        s_rd, s_att, s_o1 = sem("den_inverted"), sem("attT_done"), sem("O1_made")
        s_x1, s_st, s_mv, s_pw, s_y = sem("x1_steps"), sem("ln1_stats"), sem("ln1_meanvar"), sem("ln1_pow"), sem("y_done")
        s_t1, s_yt, s_uv = sem("T1_made"), sem("T1_copied"), sem("uv_made")
        s_lg, s_rt, s_th, s_wt = sem("logits_copied"), sem("route_steps"), sem("tanh_done"), sem("weights_done")
        s_su, s_sv, s_sw = sem("silu_u"), sem("silu_v"), sem("weighted")
        s_sx, s_sst, s_smv, s_spw, s_z = sem("x2_steps"), sem("ln2_stats"), sem("ln2_meanvar"), sem("ln2_pow"), sem("z_done")
        s_xb, s_t2, s_zt = sem("xb_done"), sem("T2_made"), sem("T2_copied")
        s_pj, s_qk = sem("qkv_made"), sem("qkv_done")
        s_pr, s_a, s_av, s_ds, s_ns = sem("prod_done"), sem("A_made"), sem("Av_done"), sem("den_summed"), sem("num_steps")
        s_zz, s_at, s_o2 = sem("z_steps"), sem("at_done"), sem("O2_made")
        s_l2, s_y4 = sem("L2_copied"), sem("Y4_kept")
        s_gu, s_sg, s_hd = sem("shared_up_made"), sem("shared_silu"), sem("shared_hidden")

        s_pass = sem("passed")

        def xs(i):
            return X[:, :, :].rearrange("p (b i) d -> p i b d", b=B)[:, bass.ds(i, 1), :, :] \
                .rearrange("p i b d -> p (i b) d")

        def flat(t):
            return t[:].rearrange("p a b -> p (a b)")

        def y4(i):
            return Y4[:, bass.ts(i, B), :]

        with nc.Block() as block:
            @block.sync
            def _(sp):
                for dst, src in ((ow[:], w["ow"]), (gate[:], w["gate"]),
                                 (Wuv[:, 0], w["Wu"].rearrange("e d r -> d e r")),
                                 (Wuv[:, 1], w["Wv"].rearrange("e d r -> d e r")),
                                 (Wo[:], w["Wo"].rearrange("(c e) r d -> (e r) c d", c=2)),
                                 (Win[:], w["Win"].rearrange("d (c n) -> d c n", c=3)), (outw[:], w["outw"]),
                                 (bias[:], w["bias"]), (outb[:], w["outb"].partition_broadcast(P)),
                                 (router[:], w["router"]), (sums[:], w["sums"].rearrange("n f g -> f n g")),
                                 (tri[:].rearrange("p e f -> p (e f)"), w["tri"].partition_broadcast(P))):
                    sp.dma_start(dst, src).then_inc(s_w, 16)

                def load(i, par):
                    for b in range(B):
                        for dst, r in ((num[par], 0), (den[par], HD)):
                            sp.dma_start(dst[:, b, :],
                                         ND[4 * b:4 * b + 4, :, r:r + HD, bass.ts(i, P)]
                                         .rearrange("g h r q -> (g h) r q")).then_inc(s_nd[par], 16)

                load(0, 0)
                load(1, 1)
                with sp.Fori(0, 3) as v:
                    sp.wait_ge(s_att, v * 2 + 1)
                    load(v * 2 + 2, 0)
                    sp.wait_ge(s_att, v * 2 + 2)
                    load(v * 2 + 3, 1)

            @block.gpsimd
            def _(gp):
                gp.memset(half[:], -0.5)
                gp.memset(eps[:], EPS).then_inc(s_cst, 1)
                gp.memset(ident[:], 0.0).then_inc(s_cst, 1)
                gp.wait_ge(s_cst, 2)
                gp.affine_select(out=ident[:], in_=ident[:], compare_op=ALU.not_equal, fill=1.0, base=0,
                                 pattern=[[-1, P]], channel_multiplier=1).then_inc(s_cst, 1)
                gp.wait_ge(s_w, 12 * 16)

                def power(i, n, per, mv, rs, made, done):
                    gp.wait_ge(made, i * per + n + 1)
                    gp.tensor_tensor(rs[:], mv[:, :, 1], eps[:], ALU.add).then_inc(done, 1)
                    gp.wait_ge(done, i * 2 * per + 2 * n + 1)
                    gp.tensor_tensor(rs[:], rs[:], half[:], ALU.pow).then_inc(done, 1)

                def first(i):
                    power(i, 0, 1, mv1, rs1, s_mv, s_pw)

                def weigh(i):
                    for b in range(B):
                        gp.wait_ge(s_sv, i * 4 + b + 1)
                        if b == 0:
                            gp.wait_ge(s_wt, i + 1)
                        if b >= 2:
                            gp.wait_ge(s_t1, i * 3 + 2)
                        elif b < 2:
                            gp.wait_ge(s_t1, i * 3)
                        gp.tensor_tensor(sw[b % 2][:].rearrange("p c (e r) -> p (c e) r", r=R), sv[b % 2][:],
                                         wt[:, b, :].unsqueeze(2).broadcast_to([P, EXP, R]),
                                         ALU.mult).then_inc(s_sw, 1)

                def second(i):
                    power(i, 0, 2, mv2, rs2, s_smv, s_spw)
                    gp.wait_ge(s_x1, i * 2 + 2)
                    gp.wait_ge(s_sx, i * 2)
                    gp.tensor_tensor(xb[:], xs(i), outb[:].unsqueeze(1).broadcast_to([P, B, D]),
                                     ALU.add).then_inc(s_xb, 1)

                def sum_up(i, l):
                    n = i * 8 + 2 * l
                    gp.wait_ge(s_av, i * 4 + l + 1)
                    if l == 0:
                        gp.wait_ge(s_at, i)
                    a = av[l % 2]
                    gp.tensor_tensor(a[:, 0:2, :], a[:, 0:2, :], a[:, 2:4, :], ALU.add).then_inc(s_ns, 1)
                    gp.wait_ge(s_ns, n + 1)
                    gp.tensor_tensor(nsum[:, l, :], a[:, 0, :], a[:, 1, :], ALU.add).then_inc(s_ns, 1)

                def third(i):
                    power(i, 1, 2, mv2, rs2, s_smv, s_spw)

                first(0)
                weigh(0)
                with gp.Fori(0, 7) as i:
                    second(i)
                    first(i + 1)
                    sum_up(i, 0)
                    sum_up(i, 1)
                    sum_up(i, 2)
                    sum_up(i, 3)
                    weigh(i + 1)
                    third(i)
                second(7)
                for l in range(B):
                    sum_up(7, l)
                third(7)

            @block.vector
            def _(dve):
                def stats(src, st, mv, s_stats, s_made, n):
                    for b in range(B):
                        ins = dve.bn_stats(st[:, b, :], src(b))
                    ins.then_inc(s_stats, 1)
                    wait_apart(dve, s_stats, n + 1, s_pass)
                    for b in range(B):
                        ins = dve.bn_aggr(mv[:, b, :], st[:, b, :])
                    ins.then_inc(s_made, 1)

                def normalize(dst, src, mv, rs, done):
                    for b in range(B):
                        ins = dve.tensor_scalar(dst(b), src(b), mv[:, b, 0:1], rs[:, b:b + 1],
                                                ALU.subtract, ALU.mult)
                    ins.then_inc(done, 1)

                def xtile(i):
                    return lambda b: X[:, TPB * b + i, :]

                def attT_(i, par, loaded):
                    dve.wait_ge(s_nd[par], loaded)
                    dve.reciprocal(den[par][:], den[par][:]).then_inc(s_rd, 1)
                    dve.wait_ge(s_rd, i + 1)
                    dve.wait_ge(s_o1, i * 3)
                    dve.tensor_tensor(attT[:], num[par][:], den[par][:], ALU.mult).then_inc(s_att, 1)

                def residual1(i):
                    dve.wait_ge(s_o1, i * 3 + 1)
                    dve.tensor_tensor(xs(i), xs(i), O1[:], ALU.add).then_inc(s_x1, 1)
                    wait_apart(dve, s_x1, i * 2 + 1, s_pass)
                    stats(xtile(i), st1, mv1, s_st, s_mv, i)
                    dve.wait_ge(s_mv, i + 1)
                    dve.wait_ge(s_pw, i * 2 + 2)
                    dve.wait_ge(s_t1, i * 3)
                    normalize(lambda b: y[:, b, :], xtile(i), mv1, rs1, s_y)

                def route(i):
                    dve.wait_ge(s_o1, i * 3 + 2)
                    dve.tensor_copy(lg[:], O1[:, 0, 0:B * EXP].rearrange("p (b e) -> p b e", b=B)) \
                       .then_inc(s_lg, 1)
                    dve.wait_ge(s_lg, i + 1)
                    mine = lg[:].unsqueeze(3).broadcast_to([P, B, EXP, EXP])
                    other = lg[:].unsqueeze(2).broadcast_to([P, B, EXP, EXP])
                    n = i * 7
                    dve.tensor_tensor(cmp[:], other, mine, ALU.is_gt)
                    dve.tensor_tensor(eq[:], other, mine, ALU.is_equal).then_inc(s_rt, 1)
                    dve.wait_ge(s_rt, n + 1)
                    dve.tensor_tensor(eq[:], eq[:], tri[:].unsqueeze(1).broadcast_to([P, B, EXP, EXP]),
                                      ALU.mult).then_inc(s_rt, 1)
                    dve.wait_ge(s_rt, n + 2)
                    dve.tensor_tensor(cmp[:], cmp[:], eq[:], ALU.add).then_inc(s_rt, 1)
                    dve.wait_ge(s_rt, n + 3)
                    dve.tensor_reduce(rank[:], cmp[:], AX.X, ALU.add).then_inc(s_rt, 1)
                    dve.wait_ge(s_rt, n + 4)
                    dve.tensor_scalar(rank[:], rank[:], 2.0, 0.5, ALU.is_lt, ALU.mult).then_inc(s_rt, 1)
                    dve.wait_ge(s_rt, n + 5)
                    dve.tensor_tensor(th[:], rank[:], lg[:], ALU.mult).then_inc(s_rt, 1)
                    dve.wait_ge(s_rt, n + 6)
                    dve.tensor_reduce(hs[:], th[:], AX.X, ALU.add).then_inc(s_rt, 1)
                    dve.wait_ge(s_rt, n + 7)
                    dve.wait_ge(s_sw, i * 4)
                    dve.tensor_tensor(th[:], lg[:], hs[:].unsqueeze(2).broadcast_to([P, B, EXP]),
                                      ALU.subtract).then_inc(s_lg if False else s_th, 1)

                def route_end(i):
                    dve.wait_ge(s_wt, i * 1 + 0)
                    dve.wait_ge(s_th, i * 2 + 2)
                    dve.scalar_tensor_tensor(out=wt[:].rearrange("p b e -> p (b e)"),
                                             in0=th[:].rearrange("p b e -> p (b e)"), scalar=1.0,
                                             in1=rank[:].rearrange("p b e -> p (b e)"),
                                             op0=ALU.add, op1=ALU.mult).then_inc(s_wt, 1)

                def gated(i, b):
                    dve.wait_ge(s_su, i * 4 + b + 1)
                    if b >= 2:
                        dve.wait_ge(s_sw, i * 4 + b - 1)
                    elif b < 2:
                        dve.wait_ge(s_sw, i * 4)
                    dve.tensor_tensor(sv[b % 2][:].rearrange("p e r -> p (e r)"),
                                      su[b % 2][:].rearrange("p e r -> p (e r)"),
                                      flat(UV[b % 2])[:, 256:512], ALU.mult).then_inc(s_sv, 1)

                def residual2(i):
                    dve.wait_ge(s_o1, i * 3 + 3)
                    dve.tensor_tensor(xs(i), xs(i), O1[:], ALU.add).then_inc(s_x1, 1)

                def ln2(i):
                    wait_apart(dve, s_x1, i * 2 + 2, s_pass)
                    stats(xtile(i), st2, mv2, s_sst, s_smv, i * 2)
                    dve.wait_ge(s_smv, i * 2 + 1)
                    dve.wait_ge(s_spw, i * 4 + 2)
                    dve.wait_ge(s_t2, i * 2)
                    normalize(lambda b: z[:, b, :], xtile(i), mv2, rs2, s_z)

                def product(i, l):
                    if l == 0:
                        dve.wait_ge(s_qk, i * 3 + 2)
                    dve.wait_ge(s_a, i * 4 + (l - 1 if l >= 2 else 0))
                    dve.tensor_tensor(prod[l % 2][:], qkv[:, 1, :, :],
                                      qkv[:, 0, l, :].unsqueeze(1).broadcast_to([P, B, P]),
                                      ALU.mult).then_inc(s_pr, 1)

                def weigh_values(i, l):
                    dve.wait_ge(s_a, i * 4 + l + 1)
                    if l == 0:
                        dve.wait_ge(s_qk, i * 3 + 3)
                    dve.wait_ge(s_ns, i * 8 + (2 * l - 2 if l >= 2 else 0))
                    dve.tensor_tensor(av[l % 2][:], A[l % 2][:], qkv[:, 2, :, :], ALU.mult).then_inc(s_av, 1)
                    dve.tensor_reduce(dsum[:, l, :], A[l % 2][:].rearrange("p s t -> p t s"), AX.X,
                                      ALU.add).then_inc(s_ds, 1)

                def attend2(i):
                    dve.wait_ge(s_ds, i * 4 + 4)
                    dve.tensor_scalar(dsum[:], dsum[:], 1e-3, None, ALU.max).then_inc(s_zz, 1)
                    dve.wait_ge(s_zz, i * 2 + 1)
                    dve.reciprocal(dsum[:], dsum[:]).then_inc(s_zz, 1)
                    dve.wait_ge(s_zz, i * 2 + 2)
                    dve.wait_ge(s_ns, i * 8 + 8)
                    dve.wait_ge(s_o2, i * 3)
                    dve.tensor_tensor(at[:], nsum[:], dsum[:], ALU.mult).then_inc(s_at, 1)

                def residual3(i):
                    dve.wait_ge(s_o2, i * 3 + 1)
                    dve.wait_ge(s_xb, i + 1)
                    dve.tensor_tensor(xs(i), xb[:], O2[:], ALU.add).then_inc(s_sx, 1)
                    wait_apart(dve, s_sx, i * 2 + 1, s_pass)
                    stats(xtile(i), st2, mv2, s_sst, s_smv, i * 2 + 1)
                    dve.wait_ge(s_smv, i * 2 + 2)
                    dve.wait_ge(s_spw, i * 4 + 4)
                    dve.wait_ge(s_y4, i)
                    normalize(lambda b: z4[:, b, :], xtile(i), mv2, rs2, s_z)

                def shared(i, c):
                    dve.wait_ge(s_sg, i * 4 + c + 1)
                    if c == 0:
                        dve.wait_ge(s_o2, i * 3)
                    dve.tensor_tensor(hid[:, c, :, :], sg[c % 2][:], A[1][:], ALU.mult).then_inc(s_hd, 1)

                def logits2(i):
                    dve.wait_ge(s_o2, i * 3 + 2)
                    dve.tensor_copy(L2[:, bass.ts(i, B), :],
                                    O2[:, 0, 0:B * 8].rearrange("p (b e) -> p b e", b=B)).then_inc(s_l2, 1)

                def residual4(i):
                    dve.wait_ge(s_o2, i * 3 + 3)
                    dve.tensor_tensor(xs(i), xs(i), O2[:], ALU.add).then_inc(s_sx, 1)

                dve.wait_ge(s_w, 12 * 16)

                def head(i, par, loaded):
                    attT_(i, par, loaded)
                    residual1(i)

                def mixture(i):
                    route(i)
                    gated(i, 0)
                    gated(i, 1)
                    route_end(i)
                    gated(i, 2)
                    gated(i, 3)

                head(0, 0, 128)
                mixture(0)
                residual2(0)

                def body(i, par, loaded):
                    ln2(i)
                    head(i + 1, par, loaded)
                    product(i, 0)
                    product(i, 1)
                    weigh_values(i, 0)
                    weigh_values(i, 1)
                    route(i + 1)
                    product(i, 2)
                    product(i, 3)
                    gated(i + 1, 0)
                    gated(i + 1, 1)
                    route_end(i + 1)
                    weigh_values(i, 2)
                    weigh_values(i, 3)
                    gated(i + 1, 2)
                    gated(i + 1, 3)
                    attend2(i)
                    residual2(i + 1)
                    residual3(i)
                    logits2(i)
                    for c in range(HC):
                        shared(i, c)
                    residual4(i)

                body(0, 1, 128)
                with dve.Fori(0, 3) as v:
                    body(v * 2 + 1, 0, v * 128 + 256)
                    body(v * 2 + 2, 1, v * 128 + 256)
                ln2(7)
                for l in range(0, B, 2):
                    product(7, l)
                    product(7, l + 1)
                    weigh_values(7, l)
                    weigh_values(7, l + 1)
                attend2(7)
                residual3(7)
                logits2(7)
                for c in range(HC):
                    shared(7, c)
                residual4(7)

            @block.scalar
            def _(act):
                act.wait_ge(s_w, 12 * 16)

                def transposed1(i):
                    act.wait_ge(s_t1, i * 3 + 1)
                    act.wait_ge(s_uv, i * 4)
                    act.activation(yT[:], T1[:], ACT.Copy).then_inc(s_yt, 1)

                def silu_u(i, b):
                    act.wait_ge(s_uv, i * 4 + b + 1)
                    act.wait_ge(s_sv, i * 4 + (b - 1 if b >= 2 else 0))
                    act.activation(su[b % 2][:].rearrange("p e r -> p (e r)"), flat(UV[b % 2])[:, 0:256],
                                   ACT.Silu).then_inc(s_su, 1)

                def tanh(i):
                    act.wait_ge(s_th, i * 2 + 1)
                    act.activation(th[:], th[:], ACT.Tanh).then_inc(s_th, 1)

                def hidden_T(i, n):
                    act.wait_ge(s_t1, i * 3 + 2 + n)
                    if n == 0:
                        act.wait_ge(s_o1, i * 3)
                    act.activation(swT[:, 2 * n:2 * n + 2, :, :].rearrange("p a b q -> p (a b) q"), T1[:],
                                   ACT.Copy).then_inc(s_yt, 1)

                def transposed2(i):
                    act.wait_ge(s_t2, i * 2 + 1)
                    act.wait_ge(s_pj, i * 3)
                    act.activation(zT[:], T2[:], ACT.Copy).then_inc(s_zt, 1)

                def bias_qkv(i):
                    act.wait_ge(s_pr, i * 4)
                    act.wait_ge(s_av, i * 4)
                    for c, src in enumerate((A0, A1, O2)):
                        act.wait_ge(s_pj, i * 3 + c + 1)
                        act.activation(qkv[:, c, :, :], src[:], ACT.Relu if c < 2 else ACT.Identity,
                                       bias=bias[:, c:c + 1]).then_inc(s_qk, 1)

                def transposed3(i):
                    act.wait_ge(s_t2, i * 2 + 2)
                    act.wait_ge(s_gu, i * 4)
                    act.wait_ge(s_o2, i * 3)
                    act.activation(yT4[:], T2[:], ACT.Copy).then_inc(s_zt, 1)
                    act.activation(y4(i), z4[:], ACT.Copy).then_inc(s_y4, 1)

                def silu_g(i, c):
                    act.wait_ge(s_gu, i * 4 + c + 1)
                    act.wait_ge(s_hd, i * 4 + (c - 1 if c >= 2 else 0))
                    act.activation(sg[c % 2][:], A0[:], ACT.Silu).then_inc(s_sg, 1)

                def mixture(i):
                    silu_u(i, 0)
                    silu_u(i, 1)
                    tanh(i)
                    silu_u(i, 2)
                    silu_u(i, 3)
                    hidden_T(i, 0)
                    hidden_T(i, 1)

                transposed1(0)
                mixture(0)
                with act.Fori(0, 7) as i:
                    transposed2(i)
                    bias_qkv(i)
                    transposed1(i + 1)
                    mixture(i + 1)
                    transposed3(i)
                    for c in range(HC):
                        silu_g(i, c)
                transposed2(7)
                bias_qkv(7)
                transposed3(7)
                for c in range(HC):
                    silu_g(7, c)

            @block.tensor
            def _(pe):
                pe.wait_ge(s_w, 12 * 16)
                pe.wait_ge(s_cst, 3)

                def project1(i):
                    pe.wait_ge(s_att, i + 1)
                    pe.wait_ge(s_x1, i * 2)
                    for b in range(B):
                        ins = pe.matmul(O1[:, b, :], attT[:, b, :], ow[:], start=True, stop=True)
                    ins.then_inc(s_o1, 1)

                def transpose1(i):
                    pe.wait_ge(s_y, i + 1)
                    pe.wait_ge(s_yt, i * 3)
                    for b in range(B):
                        ins = pe.transpose(T1[:, b, :], y[:, b, :], ident[:])
                    ins.then_inc(s_t1, 1)

                def mixture1(i):
                    pe.wait_ge(s_yt, i * 3 + 1)
                    for b in range(B):
                        ins = pe.matmul(O1[:, 0, b * EXP:b * EXP + EXP], yT[:, b, :], gate[:], start=True, stop=True)
                    ins.then_inc(s_o1, 1)
                    for b in range(B):
                        if b >= 2:
                            pe.wait_ge(s_sv, i * 4 + b - 1)
                        pe.matmul(flat(UV[b % 2]), yT[:, b, :], Wuv[:].rearrange("p a e r -> p (a e r)"),
                                  start=True, stop=True).then_inc(s_uv, 1)

                def mixture2(i):
                    for n in range(2):
                        pe.wait_ge(s_yt, i * 3 + 1 + n)
                        for b in range(2):
                            pe.wait_ge(s_sw, i * 4 + 2 * n + b + 1)
                            for c in range(2):
                                ins = pe.transpose(T1[:, 2 * b + c, :], sw[b][:, c, :], ident[:])
                        ins.then_inc(s_t1, 1)
                    pe.wait_ge(s_yt, i * 3 + 3)
                    pe.wait_ge(s_lg, i + 1)
                    for b in range(B):
                        for c in range(2):
                            ins = pe.matmul(O1[:, b, :], swT[:, b, c, :], Wo[:, c, :], start=(c == 0), stop=(c == 1))
                    ins.then_inc(s_o1, 1)

                def project2(i):
                    pe.wait_ge(s_z, i * 2 + 1)
                    pe.wait_ge(s_zt, i * 2)
                    for b in range(B):
                        ins = pe.transpose(T2[:, b, :], z[:, b, :], ident[:])
                    ins.then_inc(s_t2, 1)
                    pe.wait_ge(s_zt, i * 2 + 1)
                    pe.wait_ge(s_sx, i * 2)
                    for c, dst in enumerate((A0, A1, O2)):
                        pe.matmul(flat(dst), Win[:, c, :], flat(zT), start=True, stop=True).then_inc(s_pj, 1)

                def scores(i, l):
                    pe.wait_ge(s_pr, i * 4 + l + 1)
                    pe.wait_ge(s_qk, i * 3 + 2)
                    pe.wait_ge(s_ds, i * 4 + (l - 1 if l >= 2 else 0))
                    for s in range(B):
                        ins = pe.matmul(A[l % 2][:, s, :], sums[:, abs(l - s), :], prod[l % 2][:, s, :],
                                        start=True, stop=True)
                    ins.then_inc(s_a, 1)

                def project3(i):
                    pe.wait_ge(s_at, i + 1)
                    pe.wait_ge(s_qk, i * 3 + 3)
                    for b in range(B):
                        ins = pe.matmul(O2[:, b, :], at[:, b, :], outw[:], start=True, stop=True)
                    ins.then_inc(s_o2, 1)

                def transpose3(i):
                    pe.wait_ge(s_z, i * 2 + 2)
                    for b in range(B):
                        ins = pe.transpose(T2[:, b, :], z4[:, b, :], ident[:])
                    ins.then_inc(s_t2, 1)

                def shared(i):
                    pe.wait_ge(s_zt, i * 2 + 2)
                    pe.wait_ge(s_sx, i * 2 + 1)
                    for b in range(B):
                        ins = pe.matmul(O2[:, 0, b * 8:b * 8 + 8], yT4[:, b, :], router[:], start=True, stop=True)
                    ins.then_inc(s_o2, 1)
                    pe.wait_ge(s_ds, i * 4 + 4)
                    for c in range(HC):
                        if c:
                            pe.wait_ge(s_hd, i * 4 + c)
                        pe.matmul(flat(A0), w["sg"][:, c * P:c * P + P], flat(yT4), start=True, stop=True)
                        pe.matmul(flat(A1), w["su"][:, c * P:c * P + P], flat(yT4), start=True,
                                  stop=True).then_inc(s_gu, 1)
                    pe.wait_ge(s_hd, i * 4 + 4)
                    pe.wait_ge(s_l2, i + 1)
                    for b in range(B):
                        for c in range(HC):
                            ins = pe.matmul(O2[:, b, :], hid[:, c, b, :], w["sd"][:, c, :],
                                            start=(c == 0), stop=(c == HC - 1))
                    ins.then_inc(s_o2, 1)

                project1(0)
                transpose1(0)
                mixture1(0)
                mixture2(0)
                with pe.Fori(0, 7) as i:
                    project2(i)
                    project1(i + 1)
                    transpose1(i + 1)
                    scores(i, 0)
                    scores(i, 1)
                    mixture1(i + 1)
                    scores(i, 2)
                    scores(i, 3)
                    mixture2(i + 1)
                    project3(i)
                    transpose3(i)
                    shared(i)
                project2(7)
                for l in range(B):
                    scores(7, l)
                project3(7)
                transpose3(7)
                shared(7)


RTILES = TILES + 7
NEXP = 8


def order_tokens(nc, Y4, L2, slots, scale, experts, YS, w):
    with ExitStack() as ctx:
        def sb(name, shape, dt=F32):
            return ctx.enter_context(nc.sbuf_tensor("d_" + name, shape, dt))

        def sem(name):
            return ctx.enter_context(nc.semaphore("d_" + name))

        SH = [P, TILES, NEXP]
        zero = sb("zero", [P, D])
        before, ones = sb("before", [P, P]), sb("ones", [P, P])
        rows = sb("rows", [P, NEXP])
        tau = sb("tau", [1, RTILES])
        top, sm = sb("top", [P, TILES]), sb("sm", [P, TILES])
        dl, oh, sc = sb("dl", SH), sb("oh", SH), sb("sc", SH)
        run = [sb(f"run{i}", SH) for i in range(2)]
        ti = sb("ti", [P, NEXP], I32)
        tl = sb("tl", [P, NEXP])
        ends = [sb(f"ends{i}", [P, NEXP]) for i in range(2)]
        ct = sb("ct", [1, RTILES, 6])
        sf = sb("sf", [P, TILES])
        buf = [sb(f"buf{i}", [P, D]) for i in range(2)]
        idx = [sb(f"idx{i}", [P, 1], I32) for i in range(2)]
        pR = ctx.enter_context(nc.psum_tensor("d_pR", SH, F32))
        pC = ctx.enter_context(nc.psum_tensor("d_pC", SH, F32))
        s_c, s_k, s_z0, s_z = sem("const_loaded"), sem("const_steps"), sem("zero_made"), sem("YS_zeroed")
        s_dl, s_ex, s_d, s_oh, s_cnt = sem("shifted"), sem("exp_done"), sem("dve_steps"), sem("onehot"), sem("counted")
        s_pass, s_buf, s_sc = sem("passed"), sem("tile_copied"), [sem(f"scattered{i}") for i in range(2)]

        with nc.Block() as block:
            @block.sync
            def _(sp):
                sp.dma_start(rows[:], w["down8"].partition_broadcast(P)).then_inc(s_c, 16)
                sp.dma_start(tau[:], w["tau"].rearrange("(a n) -> a n", a=1)).then_inc(s_c, 16)
                sp.wait_ge(s_z0, 1)
                sp.dma_start(YS.rearrange("(n p) d -> p n d", p=P),
                             zero[:].unsqueeze(1).broadcast_to([P, RTILES, D])).then_inc(s_z, 16)

            @block.gpsimd
            def _(gp):
                gp.memset(zero[:], 0.0).then_inc(s_z0, 1)
                gp.memset(before[:], 1.0).then_inc(s_k, 1)
                gp.wait_ge(s_k, 1)
                gp.affine_select(out=before[:], in_=before[:], compare_op=ALU.is_gt, fill=0.0, base=0,
                                 pattern=[[1, P]], channel_multiplier=-1).then_inc(s_k, 1)
                gp.memset(ones[:], 1.0).then_inc(s_k, 1)
                gp.wait_ge(s_z, 16)

                def scatter(n, k, count):
                    wait_apart(gp, s_buf, n + 1, s_pass)
                    gp.indirect_dma_start(out=YS, out_offset=bass.IndirectOffsetOnAxis(ap=idx[k][:, 0:1], axis=0),
                                          in_=buf[k][:, :], in_offset=None).then_inc(s_sc[k], 16)

                with gp.Fori(0, TILES // 2) as v:
                    scatter(v * 2, 0, v)
                    scatter(v * 2 + 1, 1, v)
                for k in range(2):
                    gp.wait_ge(s_sc[k], TILES // 2 * 16)

            @block.scalar
            def _(act):
                act.wait_ge(s_dl, 1)
                act.activation(dl[:], dl[:], ACT.Exp).then_inc(s_ex, 1)

            @block.tensor
            def _(pe):
                pe.wait_ge(s_k, 3)
                pe.wait_ge(s_oh, 1)
                pe.matmul(pR[:].rearrange("p t e -> p (t e)"), before[:], oh[:].rearrange("p t e -> p (t e)"),
                          start=True, stop=True)
                pe.matmul(pC[:].rearrange("p t e -> p (t e)"), ones[:], oh[:].rearrange("p t e -> p (t e)"),
                          start=True, stop=True).then_inc(s_cnt, 1)

            @block.vector
            def _(dve):
                steps = [0]

                def step(ins):
                    steps[0] += 1
                    ins.then_inc(s_d, 1)
                    dve.wait_ge(s_d, steps[0])

                def wide(t):
                    return t[:].unsqueeze(2).broadcast_to(SH)

                dve.wait_ge(s_c, 32)
                step(dve.tensor_reduce(top[:], L2[:], AX.X, ALU.max))
                dve.tensor_tensor(dl[:], L2[:], wide(top), ALU.subtract).then_inc(s_dl, 1)
                step(dve.tensor_tensor(sc[:], L2[:], wide(top), ALU.is_equal))
                step(dve.tensor_tensor(sc[:], sc[:], rows[:].unsqueeze(1).broadcast_to(SH), ALU.mult))
                step(dve.tensor_reduce(top[:], sc[:], AX.X, ALU.max))
                dve.tensor_tensor(oh[:], sc[:], wide(top), ALU.is_equal).then_inc(s_oh, 1)
                dve.wait_ge(s_oh, 1)
                dve.wait_ge(s_ex, 1)
                step(dve.tensor_reduce(sm[:], dl[:], AX.X, ALU.add))
                step(dve.reciprocal(sm[:], sm[:]))
                step(dve.tensor_scalar(top[:], oh[:, :, 7], -2.0, 2.0, ALU.mult, ALU.add))
                step(dve.tensor_tensor(scale[:], sm[:], top[:], ALU.mult))
                dve.wait_ge(s_cnt, 1)
                step(dve.tensor_copy(run[0][:], pC[:]))
                k = 0
                for s in (1, 2, 4, 8, 16):
                    a, b = run[k], run[1 - k]
                    dve.tensor_copy(b[:, 0:s, :], a[:, 0:s, :])
                    step(dve.tensor_tensor(b[:, s:, :], a[:, s:, :], a[:, 0:TILES - s, :], ALU.add))
                    k = 1 - k
                step(dve.tensor_scalar(ti[:], run[k][:, TILES - 1, :], float(P - 1), None, ALU.add))
                step(dve.tensor_scalar(ti[:], ti[:], 7, None, ALU.arith_shift_right))
                step(dve.tensor_copy(tl[:], ti[:]))
                step(dve.tensor_copy(ends[0][:], tl[:]))
                j = 0
                for s in (1, 2, 4):
                    a, b = ends[j], ends[1 - j]
                    dve.tensor_copy(b[:, 0:s], a[:, 0:s])
                    step(dve.tensor_tensor(b[:, s:], a[:, s:], a[:, 0:NEXP - s], ALU.add))
                    j = 1 - j
                step(dve.tensor_tensor(ct[:], tau[:].unsqueeze(2).broadcast_to([1, RTILES, 6]),
                                       ends[j][0:1, 0:6].unsqueeze(1).broadcast_to([1, RTILES, 6]), ALU.is_ge))
                step(dve.tensor_reduce(tau[:], ct[:], AX.X, ALU.add))
                step(dve.tensor_copy(experts[:], tau[:]))
                step(dve.tensor_tensor(tl[:], ends[j][:], tl[:], ALU.subtract))
                step(dve.tensor_scalar(tl[:], tl[:], float(P), None, ALU.mult))
                step(dve.tensor_tensor(run[k][:], run[k][:], pC[:], ALU.subtract))
                step(dve.tensor_tensor(run[k][:], run[k][:], pR[:], ALU.add))
                step(dve.tensor_tensor(run[k][:], run[k][:], tl[:].unsqueeze(1).broadcast_to(SH), ALU.add))
                step(dve.tensor_tensor(run[k][:], run[k][:], oh[:], ALU.mult))
                step(dve.tensor_reduce(sf[:], run[k][:], AX.X, ALU.add))
                step(dve.tensor_copy(slots[:], sf[:]))
                with dve.Fori(0, TILES // 2) as v:
                    for k in range(2):
                        dve.wait_ge(s_sc[k], v * 16)
                        dve.tensor_copy(idx[k][:], slots[:, bass.ds(v * 2 + k, 1)])
                        dve.tensor_copy(buf[k][:], Y4[:, v * 2 + k, :]).then_inc(s_buf, 1)


def routed_experts(nc, WG, WU, WD, experts, YS, RO):
    with ExitStack() as ctx:
        def sb(name, shape, dt=F32):
            return ctx.enter_context(nc.sbuf_tensor("e_" + name, shape, dt))

        def sem(name):
            return ctx.enter_context(nc.semaphore("e_" + name))

        def two(name, shape):
            return [sb(f"{name}{i}", shape) for i in range(2)]

        HC = 4
        ident = sb("ident", [P, P])
        xin, xT, sg, h, hT, ro = (two(n, s) for n, s in (
            ("xin", [P, D]), ("xT", [P, P]), ("sg", [P, 512]), ("h", [P, HC, P]), ("hT", [P, HC, P]), ("ro", [P, D])))
        pX = ctx.enter_context(nc.psum_tensor("e_pX", [P, 512], F32))
        pG = [ctx.enter_context(nc.psum_tensor(f"e_pG{i}", [P, 512], F32)) for i in range(2)]
        pU = [ctx.enter_context(nc.psum_tensor(f"e_pU{i}", [P, 512], F32)) for i in range(2)]
        pH = ctx.enter_context(nc.psum_tensor("e_pH", [P, HC, P], F32))
        pO = ctx.enter_context(nc.psum_tensor("e_pO", [P, 512], F32))
        s_k = sem("const_steps")
        s_in, s_ro = [[sem(f"{n}{i}") for i in range(2)] for n in ("tile_loaded", "tile_stored")]
        s_tx, s_xt, s_gu, s_sg, s_h = sem("pX_made"), sem("xT_copied"), sem("gate_up_made"), sem("silu_done"), sem("h_done")
        s_th, s_ht, s_o, s_oc = sem("pH_made"), sem("hT_copied"), sem("pO_made"), sem("ro_copied")

        with nc.Block() as block:
            @block.sync
            def _(sp):
                def load(t, k):
                    sp.dma_start(xin[k][:], YS[bass.ts(t, P), :]).then_inc(s_in[k], 16)

                def store(t, k):
                    sp.wait_ge(s_oc, t + 1)
                    sp.dma_start(RO[bass.ts(t, P), :], ro[k][:]).then_inc(s_ro[k], 16)

                load(0, 0)
                load(1, 1)
                with sp.Fori(0, (RTILES - 3) // 2) as v:
                    for k in range(2):
                        sp.wait_ge(s_tx, v * 2 + k + 1)
                        load(v * 2 + k + 2, k)
                        store(v * 2 + k, k)
                sp.wait_ge(s_tx, RTILES - 2)
                load(RTILES - 1, 0)
                for t in range(RTILES - 3, RTILES):
                    store(t, t % 2)
                sp.wait_ge(s_ro[0], (RTILES + 1) // 2 * 16)
                sp.wait_ge(s_ro[1], RTILES // 2 * 16)

            @block.gpsimd
            def _(gp):
                gp.memset(ident[:], 0.0).then_inc(s_k, 1)
                gp.wait_ge(s_k, 1)
                gp.affine_select(out=ident[:], in_=ident[:], compare_op=ALU.not_equal, fill=1.0, base=0,
                                 pattern=[[-1, P]], channel_multiplier=1).then_inc(s_k, 1)

            @block.tensor
            def _(pe):
                pe.wait_ge(s_k, 2)

                def expand(t, k, loaded):
                    pe.wait_ge(s_in[k], loaded)
                    pe.wait_ge(s_xt, t)
                    pe.transpose(pX[:, 0:P], xin[k][:], ident[:]).then_inc(s_tx, 1)
                    e = pe.value_load(experts[0:1, bass.ds(t, 1)], min_val=0, max_val=6)
                    pe.wait_ge(s_xt, t + 1)
                    if not isinstance(t, int):
                        pe.wait_ge(s_h, t - 1)
                    pe.matmul(pG[k][:], xT[k][:], WG[:, bass.ds(e, 1), :].rearrange("p e n -> p (e n)"),
                              start=True, stop=True)
                    pe.matmul(pU[k][:], xT[k][:], WU[:, bass.ds(e, 1), :].rearrange("p e n -> p (e n)"),
                              start=True, stop=True).then_inc(s_gu, 1)
                    return e

                def reduce(t, k):
                    pe.wait_ge(s_h, t + 1)
                    pe.wait_ge(s_ht, t)
                    for c in range(HC):
                        ins = pe.transpose(pH[:, c, :], h[k][:, c, :], ident[:])
                    ins.then_inc(s_th, 1)
                    e = pe.value_load(experts[0:1, bass.ds(t, 1)], min_val=0, max_val=6)
                    pe.wait_ge(s_ht, t + 1)
                    pe.wait_ge(s_oc, t)
                    for c in range(HC):
                        ins = pe.matmul(pO[:, 0:D], hT[k][:, c, :],
                                        WD[:, bass.ds(e, 1), c, :].rearrange("p e n -> p (e n)"),
                                        start=(c == 0), stop=(c == HC - 1))
                    ins.then_inc(s_o, 1)

                expand(0, 0, 16)
                with pe.Fori(0, (RTILES - 1) // 2) as v:
                    expand(v * 2 + 1, 1, v * 16 + 16)
                    reduce(v * 2, 0)
                    expand(v * 2 + 2, 0, v * 16 + 32)
                    reduce(v * 2 + 1, 1)
                reduce(RTILES - 1, 0)

            @block.scalar
            def _(act):
                def copy_x(t, k):
                    act.wait_ge(s_tx, t + 1)
                    act.activation(xT[k][:], pX[:, 0:P], ACT.Copy).then_inc(s_xt, 1)

                def silu(t, k):
                    act.wait_ge(s_gu, t + 1)
                    act.activation(sg[k][:], pG[k][:], ACT.Silu).then_inc(s_sg, 1)

                def copy_o(t, k, stored):
                    act.wait_ge(s_o, t + 1)
                    if stored is not None:
                        act.wait_ge(s_ro[k], stored)
                    act.activation(ro[k][:], pO[:, 0:D], ACT.Copy).then_inc(s_oc, 1)

                copy_x(0, 0)
                silu(0, 0)
                with act.Fori(0, (RTILES - 1) // 2) as v:
                    copy_x(v * 2 + 1, 1)
                    silu(v * 2 + 1, 1)
                    copy_o(v * 2, 0, v * 16)
                    copy_x(v * 2 + 2, 0)
                    silu(v * 2 + 2, 0)
                    copy_o(v * 2 + 1, 1, v * 16)
                copy_o(RTILES - 1, 0, (RTILES - 1) // 2 * 16)

            @block.vector
            def _(dve):
                def mult(t, k):
                    dve.wait_ge(s_sg, t + 1)
                    dve.tensor_tensor(h[k][:].rearrange("p c n -> p (c n)"), sg[k][:], pU[k][:],
                                      ALU.mult).then_inc(s_h, 1)

                def copy_h(t, k):
                    dve.wait_ge(s_th, t + 1)
                    dve.tensor_copy(hT[k][:], pH[:]).then_inc(s_ht, 1)

                mult(0, 0)
                with dve.Fori(0, (RTILES - 1) // 2) as v:
                    copy_h(v * 2, 0)
                    mult(v * 2 + 1, 1)
                    copy_h(v * 2 + 1, 1)
                    mult(v * 2 + 2, 0)
                copy_h(RTILES - 1, 0)


def gather_and_finish(nc, X, slots, scale, RO, out):
    with ExitStack() as ctx:
        def sem(name):
            return ctx.enter_context(nc.semaphore("f_" + name))

        g = [ctx.enter_context(nc.sbuf_tensor(f"f_g{i}", [P, D], F32)) for i in range(NBATCH)]
        idx = [ctx.enter_context(nc.sbuf_tensor(f"f_idx{i}", [P, 1], I32)) for i in range(NBATCH)]
        s_i, s_a, s_pass = sem("indices_copied"), sem("added"), sem("passed")
        s_g = [sem(f"gathered{i}") for i in range(NBATCH)]
        s_out = sem("stored")
        with nc.Block() as block:
            @block.scalar
            def _(act):
                with act.Fori(0, TPB) as i:
                    for b in range(NBATCH):
                        act.wait_ge(s_g[b], i * 16)
                        act.activation(idx[b][:], slots[:, bass.ds(i * NBATCH + b, 1)], ACT.Copy).then_inc(s_i, 1)

            @block.gpsimd
            def _(gp):
                with gp.Fori(0, TPB) as i:
                    for b in range(NBATCH):
                        wait_apart(gp, s_a, i * NBATCH, s_pass)
                        wait_apart(gp, s_i, i * NBATCH + b + 1, s_pass)
                        gp.indirect_dma_start(out=g[b][:, :], out_offset=None, in_=RO,
                                              in_offset=bass.IndirectOffsetOnAxis(ap=idx[b][:, 0:1], axis=0)) \
                          .then_inc(s_g[b], 16)

            @block.vector
            def _(dve):
                with dve.Fori(0, TPB) as i:
                    for b in range(NBATCH):
                        dve.wait_ge(s_g[b], i * 16 + 16)
                        dve.scalar_tensor_tensor(out=X[:, TPB * b + i, :], in0=g[b][:],
                                                 scalar=scale[:, bass.ds(i * NBATCH + b, 1)],
                                                 in1=X[:, TPB * b + i, :],
                                                 op0=ALU.mult, op1=ALU.add).then_inc(s_a, 1)

            @block.sync
            def _(sp):
                with sp.Fori(0, TPB) as i:
                    sp.wait_ge(s_a, i * NBATCH + NBATCH)
                    sp.dma_start(out[:, bass.ts(i, P), :].rearrange("b p d -> p b d"),
                                 X[:, :, :].rearrange("p (b i) d -> p i b d", b=NBATCH)[:, bass.ds(i, 1), :, :]
                                 .rearrange("p i b d -> p (i b) d")).then_inc(s_out, 16)
                sp.wait_ge(s_out, TPB * 16)


def load_expert_weights(nc, WG, WU, WD, w):
    with nc.semaphore("w_loaded") as s_w, nc.Block() as block:
        @block.sync
        def _(sp):
            for dst, src in ((WG[:, 0:7, :], w["gate_w"].rearrange("e d h -> d e h")),
                             (WU[:, 0:7, :], w["up_w"].rearrange("e d h -> d e h")),
                             (WG[:, 7, :], w["sg"]), (WU[:, 7, :], w["su"]),
                             (WD[:, 0:7, :, :].rearrange("p e c d -> p (e c) d"),
                              w["down_w"].rearrange("e (c p) d -> p (e c) d", p=P)),
                             (WD[:, 7, :, :], w["sd"].rearrange("(c p) d -> p c d", p=P))):
                sp.dma_start(dst, src).then_inc(s_w, 16)
            sp.wait_ge(s_w, 6 * 16)


def build(nc, w, out):
    QD = nc.dram_tensor("q_stacks", [QUADS, 4, ROWS, SEQ], BF16, kind="Internal").ap()
    KD = nc.dram_tensor("k_stacks", [QUADS, 4, ROWS, SEQ], BF16, kind="Internal").ap()
    MD = nc.dram_tensor("neg_maxima", [96, P], BF16, kind="Internal").ap()
    ND = nc.dram_tensor("attended", [QUADS, 4, 2 * HD, SEQ], F32, kind="Internal").ap()
    YS = nc.dram_tensor("sorted_in", [RTILES * P, D], F32, kind="Internal").ap()
    RO = nc.dram_tensor("sorted_out", [RTILES * P, D], F32, kind="Internal").ap()
    with ExitStack() as ctx:
        def sb(name, shape, dt=F32):
            return ctx.enter_context(nc.sbuf_tensor(name, shape, dt))

        X = sb("x", [P, TILES, D])
        with nc.sbuf_tensor("v_by_quads", [P, QUADS, TPB, 32], F32) as VS:
            project_and_rotate(nc, X, VS, w["x"], w["cos"], w["sin"], w["qw"], w["qws"], w["kw"], w["kws"],
                               w["vw"], QD, KD)
            attend(nc, VS, QD, KD, MD, ND)
        WG, WU, WD = sb("WG", [P, NEXP, 512]), sb("WU", [P, NEXP, 512]), sb("WD", [P, NEXP, 4, D])
        Y4, L2 = sb("y4", [P, TILES, D]), sb("logits2", [P, TILES, NEXP])
        slots, scale = sb("slots", [P, TILES], I32), sb("scale", [P, TILES])
        experts = sb("experts", [1, RTILES], I32)
        load_expert_weights(nc, WG, WU, WD, w)
        middle_layers(nc, X, Y4, L2, ND, {**w, "sg": WG[:, 7, :], "su": WU[:, 7, :], "sd": WD[:, 7, :, :]})
        order_tokens(nc, Y4, L2, slots, scale, experts, YS, w)
        routed_experts(nc, WG, WU, WD, experts, YS, RO)
        gather_and_finish(nc, X, slots, scale, RO, out)


def host_arrays(i):
    cos, sin = tables()
    swap = np.arange(D) ^ 1
    e = np.arange(8)
    return {
        "x": i["L0_attn_x"], "cos": cos, "sin": sin,
        "qw": i["L0_attn_qw"], "qws": i["L0_attn_qw"][:, swap],
        "kw": i["L0_attn_kw"], "kws": i["L0_attn_kw"][:, swap],
        "vw": i["L0_attn_vw"], "ow": i["L0_attn_ow"],
        "gate": i["L0_ffn_gate_w"], "Wu": i["L0_ffn_Wu"], "Wv": i["L0_ffn_Wv"], "Wo": i["L0_ffn_Wo"],
        "Win": i["L1_attn_in_proj_weight"].T, "bias": i["L1_attn_in_proj_bias"].reshape(3, D).T,
        "outw": i["L1_attn_out_w"].T, "outb": i["L1_attn_out_b"], "router": i["L1_ffn_router_w"],
        "up_w": i["L1_ffn_up_w"], "gate_w": i["L1_ffn_gate_w"], "down_w": i["L1_ffn_down_w"],
        "su": i["L1_ffn_shared_up_w"], "sg": i["L1_ffn_shared_gate_w"], "sd": i["L1_ffn_shared_down_w"],
        "sums": head_sums(), "tri": (e[:, None] > e[None, :]).astype(np.float32).reshape(64),
        "down8": (8 - e).astype(np.float32), "tau": np.arange(RTILES, dtype=np.float32),
    }


def kernel(**inputs):
    import concourse.bacc as bacc
    from concourse.bass_utils import run_bass_kernel_spmd

    nc = bacc.Bacc("TRN2", target_bir_lowering=False, num_devices=1)
    arrays, args = {}, {}
    for name, a in host_arrays({k: np.asarray(v) for k, v in inputs.items()}).items():
        a = np.ascontiguousarray(a)
        arrays[f"in_{name}"] = a
        args[name] = nc.dram_tensor(f"in_{name}", a.shape, mybir.dt.from_np(a.dtype), kind="ExternalInput").ap()
    out = nc.dram_tensor("out", (NBATCH, SEQ, D), F32, kind="ExternalOutput").ap()
    build(nc, args, out)
    result = run_bass_kernel_spmd(nc, [arrays], core_ids=[0])
    return result.results[0]["out"]
```

```python
import numpy as np
import concourse.bass as bass
from concourse import mybir
from contextlib import ExitStack

F32 = mybir.dt.float32
BF16 = mybir.dt.bfloat16
I32 = mybir.dt.int32
U32 = mybir.dt.uint32
ALU = mybir.AluOpType
ACT = mybir.ActivationFunctionType
AX = mybir.AxisListType

P = 128
NBATCH, SEQ, D = 4, 1024, 128
TILES = NBATCH * SEQ // P
TPB = SEQ // P
HEADS, HD = 16, 8
QUADS = NBATCH * HEADS // 4
SLOTS = 6
ROWS = SLOTS * HD
EPS = 1e-5
Q_PART = [0, 1, 2, 0, 1, 0]
K_PART = [0, 0, 0, 1, 1, 2]
QSCALE = float(1.0 / np.sqrt(HD))
MASKED = -1.0e30

UNITS = [(h, i, c * 512, min(512, (i + 1) * P - c * 512))
         for h in range(4) for i in range(TPB) for c in range((i * P + P - 1) // 512 + 1)]
MBANKS = 3
NUNITS = len(UNITS) + MBANKS
LATE_T = 4
EARLY = 16
GROUPS = [(j, c) for j in range(TPB) for c in (0, 1) if j < 4 * (c + 1)]
NGROUPS = len(GROUPS)
SBANKS = 3
PBUFS = 4


def wait_apart(eng, sem, value, passed):
    eng.wait_ge(sem, value)
    eng.sem_inc(passed, 1)


def tables():
    inv = (np.float32(1.0) / np.power(np.float32(10000.0), np.arange(0, HD, 2, dtype=np.float32) / np.float32(HD))).astype(np.float32)
    freq = np.arange(SEQ, dtype=np.float32)[:, None] * inv[None, :]
    f = np.arange(D)
    ang = freq[:, (f % HD) // 2].T.astype(np.float64)
    sign = np.where(f % 2 == 0, -1.0, 1.0)[:, None]
    return np.cos(ang).astype(np.float32), (np.sin(ang) * sign).astype(np.float32)


class StackBuffers:

    def __init__(self, nc, ctx):
        def both(name, shape):
            return [ctx.enter_context(nc.sbuf_tensor(f"b_{name}{i}", shape, BF16)) for i in range(2)]

        self.Qz, self.Kz = both("Qz", [P, 4, SEQ]), both("Kz", [P, 4, SEQ])
        self.Qm, self.Km = both("Qm", [P, 2, SEQ]), both("Km", [P, 2, SEQ])
        self.ones = ctx.enter_context(nc.sbuf_tensor("b_ones", [3, SEQ], BF16))
        self.parts = [ctx.enter_context(nc.sbuf_tensor(f"a_parts{k}", [P, 3, NBATCH * SEQ], BF16)) for k in range(2)]
        self.s_store = ctx.enter_context(nc.semaphore("a_parts_stored"))
        self.s_ks = [ctx.enter_context(nc.semaphore(f"b_max_stacks_loaded{i}")) for i in range(2)]
        self.s_qs = [ctx.enter_context(nc.semaphore(f"b_exp_stacks_loaded{i}")) for i in range(2)]


def load_stacks(sp, zeroed, moving, src_z, src_m, u, par, s):
    for e in range(2):
        rows = slice(64 * e, 64 * e + ROWS)
        sp.dma_start(zeroed[par][rows, e::2, :], src_z[bass.ds(u, 1), e::2, :, :]
                     .rearrange("u h r t -> (u r) h t")).then_inc(s[par], 16)
        sp.dma_start(moving[par][rows, :, :], src_m[bass.ds(u, 1), e::2, :, :]
                     .rearrange("u h r t -> (u r) h t")).then_inc(s[par], 16)


def store_parts(sp, bufs, QD, KD, b, done):
    for k, (dst, order) in enumerate(((QD, Q_PART), (KD, K_PART))):
        for s, part in enumerate(order):
            sp.dma_start(dst[bass.ts(b, 4), :, s * HD:(s + 1) * HD, :].rearrange("g h d t -> (g h) d t"),
                         bufs.parts[k][:, part, bass.ts(b, SEQ)]).then_inc(done, 16)


def project_and_rotate(nc, X, VS, bufs, x, cos, sin, wq, wqs, wk, wks, wv, QD, KD):
    with ExitStack() as ctx:
        def sb(name, shape, dt=F32):
            return ctx.enter_context(nc.sbuf_tensor(name, shape, dt))

        def sem(name):
            return ctx.enter_context(nc.semaphore(name))

        def both(name, shape, dt=F32):
            return [sb(f"{name}{i}", shape, dt) for i in range(2)]

        HT = 4
        NH = 2 * NBATCH
        ident = sb("a_ident", [P, P])
        W = sb("a_w", [P, 5, D])
        tab = sb("a_tab", [P, 2, SEQ])
        half, eps = sb("a_minus_half", [P, HT]), sb("a_eps", [P, HT])
        stats, mv, rstd = both("a_stats", [P, HT, 6]), both("a_mean_var", [P, HT, 2]), both("a_rstd", [P, HT])
        Y, YT = both("a_y", [P, HT, D]), both("a_yT", [P, 512])
        rot = [both(f"a_rot_{'qk'[k]}", [P, 2, 512]) for k in range(2)]
        parts = bufs.parts
        pT = [ctx.enter_context(nc.psum_tensor(f"a_pT{i}", [P, HT, P], F32)) for i in range(2)]
        pQ = [ctx.enter_context(nc.psum_tensor(f"a_pQ{i}", [P, 512], F32)) for i in range(4)]
        pV = ctx.enter_context(nc.psum_tensor("a_pV", [P, HT, D], F32))

        s_x0, s_x, s_w, s_tab = sem("a_x0_loaded"), sem("a_x_loaded"), sem("a_w_loaded"), sem("a_tab_loaded")
        s_id, s_zero, s_ones = sem("a_const_steps"), sem("a_zeroed"), sem("a_ones_set")
        s_st, s_mv, s_rstd = sem("a_stats_done"), sem("a_mean_var_done"), sem("a_rstd_steps")
        s_y, s_t, s_yt = sem("a_y_done"), sem("a_transposed"), sem("a_yT_done")
        s_qk, s_v, s_vc = sem("a_projected"), sem("a_v_projected"), sem("a_v_copied")
        s_mul, s_sum, s_res = sem("a_terms_done"), sem("a_rotated"), sem("a_residue_done")
        s_hi, s_mid = sem("a_hi_done"), sem("a_mid_done")
        s_part, s_store0, s_store = sem("a_parts_done"), sem("a_batch0_stored"), bufs.s_store
        s_pass = sem("a_passed")

        def span(n):
            return bass.ds(n * 512, 512)

        def each_half(eng, before, step):
            if before:
                before()
            step(0, 0, 2)
            step(1, 1, 2)
            with eng.Fori(1, NBATCH - 1) as b:
                step(b * 2, 0, 2)
                step(b * 2 + 1, 1, 2)
            step(NH - 2, 0, 1)
            step(NH - 1, 1, 0)

        with nc.Block() as block:
            @block.sync
            def _(sp):
                sp.dma_start(X[:, 0:TPB, :], x[0:1].rearrange("b (t p) d -> p (b t) d", p=P)).then_inc(s_x0, 16)
                sp.dma_start(X[:, TPB:, :], x[1:].rearrange("b (t p) d -> p (b t) d", p=P)).then_inc(s_x, 16)
                sp.wait_ge(s_zero, 2)
                for par in range(2):
                    for e in range(2):
                        for h in range(2):
                            sp.dma_start(bufs.Kz[par][64 * e + ROWS:64 * e + ROWS + 3, e + 2 * h, :],
                                         bufs.ones[:, :]).then_inc(s_ones, 16)

                sp.wait_ge(s_part, 4)
                store_parts(sp, bufs, QD, KD, 0, s_store0)
                sp.wait_ge(s_store0, 2 * SLOTS * 16)
                load_stacks(sp, bufs.Qz, bufs.Km, QD, KD, 0, 0, bufs.s_ks)
                load_stacks(sp, bufs.Kz, bufs.Qm, KD, QD, 0, 0, bufs.s_qs)
                load_stacks(sp, bufs.Qz, bufs.Km, QD, KD, 1, 1, bufs.s_ks)
                with sp.Fori(1, NBATCH - 1) as b:
                    sp.wait_ge(s_part, b * 4 + 4)
                    store_parts(sp, bufs, QD, KD, b, s_store)
                sp.wait_ge(s_ones, 8 * 16)

            @block.gpsimd
            def _(gp):
                gp.memset(half[:], -0.5)
                gp.memset(eps[:], EPS).then_inc(s_id, 1)
                gp.memset(ident[:], 0.0).then_inc(s_id, 1)
                gp.wait_ge(s_id, 2)
                gp.affine_select(out=ident[:], in_=ident[:], compare_op=ALU.not_equal, fill=1.0, base=0,
                                 pattern=[[-1, P]], channel_multiplier=1).then_inc(s_id, 1)
                for t in (bufs.Kz[0], bufs.Kz[1], bufs.Qz[0], bufs.Qz[1]):
                    gp.memset(t[:].bitcast(U32), 0)
                gp.memset(bufs.ones[:], 1.0).then_inc(s_zero, 1)

                def power(n, par):
                    gp.wait_ge(s_mv, n + 1)
                    gp.tensor_tensor(rstd[par][:], mv[par][:, :, 1], eps[:], ALU.add).then_inc(s_rstd, 1)
                    gp.wait_ge(s_rstd, n * 2 + 1)
                    gp.tensor_tensor(rstd[par][:], rstd[par][:], half[:], ALU.pow).then_inc(s_rstd, 1)

                def step(n, par, ahead):
                    if ahead == 2:
                        power(n + 2, par)
                    for k in range(2):
                        gp.wait_ge(s_mid, n * 2 + k + 1)
                        gp.tensor_tensor(parts[k][:, 2, span(n)], rot[k][par][:, 1, :], parts[k][:, 1, span(n)],
                                         ALU.subtract).then_inc(s_part, 1)

                each_half(gp, lambda: (power(0, 0), power(1, 1)), step)

            @block.vector
            def _(dve):
                def moments(n, par):
                    for t in range(HT):
                        ins = dve.bn_stats(stats[par][:, t, :], X[:, n * HT + t, :])
                    ins.then_inc(s_st, 1)
                    wait_apart(dve, s_st, n + 1, s_pass)
                    for t in range(HT):
                        ins = dve.bn_aggr(mv[par][:, t, :], stats[par][:, t, :])
                    ins.then_inc(s_mv, 1)

                def normalize(n, par):
                    dve.wait_ge(s_rstd, n * 2 + 2)
                    dve.wait_ge(s_mv, n + 1)
                    if not (isinstance(n, int) and n < 2):
                        dve.wait_ge(s_t, n - 1)
                    for t in range(HT):
                        ins = dve.tensor_scalar(Y[par][:, t, :], X[:, n * HT + t, :], mv[par][:, t, 0:1],
                                                rstd[par][:, t:t + 1], ALU.subtract, ALU.mult)
                    ins.then_inc(s_y, 1)

                def before():
                    for t in (bufs.Qm[0], bufs.Qm[1], bufs.Km[0], bufs.Km[1]):
                        ins = dve.memset(t[:].bitcast(U32), 0)
                    ins.then_inc(s_zero, 1)
                    dve.wait_ge(s_x0, 16)
                    moments(0, 0)
                    moments(1, 1)
                    normalize(0, 0)
                    dve.wait_ge(s_tab, 32)
                    dve.wait_ge(s_x, 16)

                def step(n, par, ahead):
                    if ahead:
                        normalize(n + 1, 1 - par)
                    cols = slice(par * 512, par * 512 + 512)
                    for k in range(2):
                        dve.wait_ge(s_qk, n * 2 + k + 1)
                        if not (isinstance(n, int) and n < 2):
                            dve.wait_ge(s_part, n * 2 + k - 3)
                        dve.tensor_tensor(rot[k][par][:, 0, :], pQ[2 * k][:], tab[:, 0, cols], ALU.mult)
                        dve.tensor_tensor(rot[k][par][:, 1, :], pQ[2 * k + 1][:], tab[:, 1, cols],
                                          ALU.mult).then_inc(s_mul, 1)
                    if ahead == 2:
                        moments(n + 2, par)
                    for k in range(2):
                        dve.wait_ge(s_mul, n * 2 + k + 1)
                        dve.tensor_tensor(rot[k][par][:, 0, :], rot[k][par][:, 0, :], rot[k][par][:, 1, :],
                                          ALU.add).then_inc(s_sum, 1)
                    for k in range(2):
                        dve.wait_ge(s_sum, n * 2 + k + 1)
                        dve.wait_ge(s_hi, n * 2 + k + 1)
                        dve.tensor_tensor(rot[k][par][:, 1, :], rot[k][par][:, 0, :], parts[k][:, 0, span(n)],
                                          ALU.subtract).then_inc(s_res, 1)

                each_half(dve, before, step)

            @block.scalar
            def _(act):
                for k, w in enumerate((wq, wqs, wk, wks, wv)):
                    act.dma_start(W[:, k, :], w).then_inc(s_w, 16)
                act.dma_start(tab[:, 0, :], cos).then_inc(s_tab, 16)
                act.dma_start(tab[:, 1, :], sin).then_inc(s_tab, 16)

                def copy_y(n, par):
                    act.wait_ge(s_t, n + 1)
                    if not (isinstance(n, int) and n < 2):
                        act.wait_ge(s_v, n - 1)
                    act.activation(YT[par][:], pT[par][:].rearrange("p a b -> p (a b)"),
                                   ACT.Copy).then_inc(s_yt, 1)

                def step(n, par, ahead):
                    if ahead:
                        copy_y(n + 1, 1 - par)
                    for k in range(2):
                        act.wait_ge(s_sum, n * 2 + k + 1)
                        act.activation(parts[k][:, 0, span(n)], rot[k][par][:, 0, :], ACT.Copy).then_inc(s_hi, 1)
                    act.wait_ge(s_v, n + 1)
                    quads = slice(2 * (n - par), 2 * (n - par) + 4) if isinstance(n, int) else bass.ds(n * 2 - 2 * par, 4)
                    act.activation(VS[:, quads, HT * par:HT * par + HT, :],
                                   pV[:].rearrange("p j (g f) -> p g j f", g=4), ACT.Copy).then_inc(s_vc, 1)
                    for k in range(2):
                        act.wait_ge(s_res, n * 2 + k + 1)
                        act.activation(parts[k][:, 1, span(n)], rot[k][par][:, 1, :], ACT.Copy).then_inc(s_mid, 1)

                each_half(act, lambda: copy_y(0, 0), step)

            @block.tensor
            def _(pe):
                def transpose(n, par):
                    pe.wait_ge(s_y, n + 1)
                    if not (isinstance(n, int) and n < 2):
                        pe.wait_ge(s_yt, n - 1)
                    for t in range(HT):
                        ins = pe.transpose(pT[par][:, t, :], Y[par][:, t, :], ident[:])
                    ins.then_inc(s_t, 1)

                def before():
                    pe.wait_ge(s_id, 3)
                    transpose(0, 0)
                    pe.wait_ge(s_w, 16 * 5)

                def step(n, par, ahead):
                    for k in range(2):
                        if k == 0:
                            pe.wait_ge(s_yt, n + 1)
                        if not (isinstance(n, int) and n < 1):
                            pe.wait_ge(s_mul, n * 2 + k - 1)
                        pe.matmul(pQ[2 * k][:], W[:, 2 * k, :], YT[par][:], start=True, stop=True)
                        pe.matmul(pQ[2 * k + 1][:], W[:, 2 * k + 1, :], YT[par][:], start=True,
                                  stop=True).then_inc(s_qk, 1)
                        if k == 0 and ahead:
                            transpose(n + 1, 1 - par)
                    if not (isinstance(n, int) and n < 1):
                        pe.wait_ge(s_vc, n)
                    for t in range(HT):
                        ins = pe.matmul(pV[:, t, :], YT[par][:, t * P:t * P + P], W[:, 4, :], start=True, stop=True)
                    ins.then_inc(s_v, 1)

                each_half(pe, before, step)


def attend(nc, VS, bufs, QD, KD, MD, ND):
    with ExitStack() as ctx:
        def sb(name, shape, dt=F32):
            return ctx.enter_context(nc.sbuf_tensor(name, shape, dt))

        def sem(name):
            return ctx.enter_context(nc.semaphore(name))

        def both(name, shape, dt=F32):
            return [sb(f"{name}{i}", shape, dt) for i in range(2)]

        Qz, Kz, Qm, Km = bufs.Qz, bufs.Kz, bufs.Qm, bufs.Km
        Vq = both("b_Vq", [P, TPB, 4, 32])
        probs = [sb(f"b_probs{i}", [P, 4, 512]) for i in range(PBUFS)]
        raw = both("b_raw", [P, SEQ])
        identb = sb("b_ident", [P, P], BF16)
        maskb = sb("b_mask", [P, P], BF16)
        mx = both("b_mx", [P, 4, TPB, 2])
        res = sb("b_res", [P, 4, TPB])
        nm = both("b_negmax", [P, 2, 3, 2, TPB], BF16)
        MT = sb("b_negmaxT", [96, P], BF16)
        st = [ctx.enter_context(nc.psum_tensor(f"b_st{i}", [P, 512], F32)) for i in range(SBANKS)]
        acc = ctx.enter_context(nc.psum_tensor("b_acc", [P, SEQ], F32))
        mb = [ctx.enter_context(nc.psum_tensor(f"b_mb{i}", [P, 512], F32)) for i in range(MBANKS)]

        s_cst, s_ks, s_qs = sem("b_const_steps"), bufs.s_ks, bufs.s_qs
        s_mm, s_red, s_fin = sem("b_unit_made"), sem("b_unit_reduced"), sem("b_negmax_steps")
        s_mt, s_md, s_mrow = sem("b_negmaxT_copied"), sem("b_negmax_stored"), sem("b_negmax_loaded")
        s_st, s_exp, s_mask = sem("b_scores"), sem("b_exp_done"), sem("b_masked")
        s_pv, s_raw, s_nd = sem("b_pv_done"), sem("b_raw_done"), [sem(f"b_raw_stored{i}") for i in range(2)]
        s_vq, s_vone = sem("b_v_ready"), sem("b_v_ones")
        s_pass = sem("b_passed")
        LOAD = 4 * 16
        NT = QUADS

        STEPS = 4 * NGROUPS

        def width(j, c):
            return 512 * (c + 1) - max(P * j, 512 * c)

        def number(n):
            return n if n < LATE_T else n + MBANKS

        def stream(first, second):
            out = [(first, n) for n in range(EARLY, len(UNITS))]
            if second:
                out += [(first + 1, n) for n in range(LATE_T)]
            out.append((first, "T"))
            if second:
                out += [(first + 1, n) for n in range(LATE_T, EARLY)]
            return out

        def spread(units):
            cost = [(UNITS[n][3] if n != "T" else P) + 70 for _, n in units]
            lens = [2 * width(*GROUPS[k // 4]) + 120 for k in range(STEPS)]
            plan, spent, passed, at = [], 0, 0, 0
            for k in range(STEPS):
                passed += lens[k]
                now = []
                while at < len(units) and (spent + cost[at] / 2) * sum(lens) <= passed * sum(cost):
                    spent += cost[at]
                    now.append(units[at])
                    at += 1
                plan.append(now)
            plan[-1] += units[at:]
            return plan

        VALUES_AT = 9
        EVACUATE_AT = 1
        EVACUATE0_AT = 10
        PROLOGUE = [(0, n) for n in range(EARLY)] + stream(0, True)
        FULL = spread(stream(1, True))
        LAST = spread(stream(1, False))

        def unit_number(u, ahead, n, last):
            if n == "T":
                return (u + ahead + 1) * NUNITS + (0 if last else LATE_T)
            return (u + ahead) * NUNITS + number(n)

        def unit_bank(n, last):
            return mb[unit_number(0, 0, n, last) % MBANKS]

        def counts(u, ahead, n):
            if n == "T":
                return MBANKS
            return 1 + MBANKS if isinstance(u, int) and u + ahead == 0 and n == LATE_T - 1 else 1

        def each_quad(eng, prologue, body, epilogue):
            if prologue:
                prologue()
            body(0, 0, -1, FULL, False)
            body(1, 1, 0, FULL, False)
            body(2, 0, 0, FULL, False)
            with eng.Fori(1, 6) as v:
                body(v * 2 + 1, 1, v, FULL, False)
                body(v * 2 + 2, 0, v, FULL, False)
            body(13, 1, 6, FULL, False)
            body(14, 0, 6, LAST, True)
            body(15, 1, 7, [[]] * STEPS, True)
            if epilogue:
                epilogue()

        with nc.Block() as block:
            @block.sync
            def _(sp):
                def maxima(u, ahead, par, last):
                    sp.wait_ge(s_red, unit_number(u, ahead, "T", last) + 1)
                    sp.dma_start(MD[:, :], MT[:, :]).then_inc(s_md, 16)
                    sp.wait_ge(s_md, (u + ahead) * 16 + 16)
                    for e in range(2):
                        sp.dma_start(Qm[par][64 * e + ROWS:64 * e + ROWS + 3, :, :],
                                     MD[48 * e:48 * e + 48, :].rearrange("(c p i) q -> c p (i q)", c=3, p=2)) \
                          .then_inc(s_mrow, 16)

                def store_raw(u, par, ):
                    sp.wait_ge(s_raw, 2 * u + 2)
                    for h in range(4):
                        sp.dma_start(ND[bass.ds(u, 1), h, :, :].rearrange("u r t -> (u r) t"),
                                     raw[par][32 * h:32 * h + HD + 1, :]).then_inc(s_nd[par], 16)

                def prologue():
                    store_parts(sp, bufs, QD, KD, NBATCH - 1, bufs.s_store)
                    maxima(0, 0, 0, False)
                    sp.wait_ge(bufs.s_store, (NBATCH - 1) * 2 * SLOTS * 16)

                def body(u, par, v, plan, last):
                    static = isinstance(u, int)
                    if not (static and u + 1 >= NT):
                        if not (static and u == 0):
                            sp.wait_ge(s_exp, u * STEPS)
                        load_stacks(sp, Kz, Qm, KD, QD, u + 1, 1 - par, s_qs)
                    if not (static and u + 2 >= NT):
                        sp.wait_ge(s_red, (u + 1) * NUNITS)
                        load_stacks(sp, Qz, Km, QD, KD, u + 2, par, s_ks)
                    if not (static and u == 0):
                        store_raw(u - 1, 1 - par)
                    if not (static and u + 1 >= NT):
                        maxima(u, 1, 1 - par, last)

                def epilogue():
                    store_raw(NT - 1, (NT - 1) % 2)
                    for par in range(2):
                        sp.wait_ge(s_nd[par], NT // 2 * 64)

                each_quad(sp, prologue, body, epilogue)

            @block.vector
            def _(dve):
                def unit(u, ahead, n, par, last):
                    num = unit_number(u, ahead, n, last)
                    bank = unit_bank(n, last)
                    dve.wait_ge(s_mm, num + 1)
                    if n == "T":
                        q = u + ahead
                        if not (isinstance(q, int) and q == 0):
                            dve.wait_ge(s_md, q * 16)
                        dve.tensor_copy(MT[:, :], bank[0:96, 0:P // 2].bitcast(BF16)) \
                           .then_inc(s_red, counts(u, ahead, n))
                        return
                    h, i, k0, w = UNITS[n]
                    dve.tensor_reduce(mx[par][:, h, i, k0 // 512:k0 // 512 + 1], bank[:, 0:w], AX.X, ALU.max) \
                       .then_inc(s_red, counts(u, ahead, n))
                    if n == len(UNITS) - 1:
                        q = u + ahead
                        dve.wait_ge(s_red, num + 1)
                        dve.tensor_tensor(mx[par][:, :, 4:8, 0], mx[par][:, :, 4:8, 0], mx[par][:, :, 4:8, 1],
                                          ALU.max).then_inc(s_fin, 1)
                        dve.wait_ge(s_fin, q * 5 + 1)
                        if not (isinstance(q, int) and q < 2):
                            dve.wait_ge(s_mm, (q - 1) * NUNITS + LATE_T + 1)
                        m = mx[par][:, :, :, 0].rearrange("q (p e) i -> q e p i", e=2)
                        neg = nm[par]
                        r = res[:, :, :].rearrange("q (e p) i -> q e p i", e=2)
                        dve.tensor_scalar(neg[:, :, 0, :, :], m, -1.0, None, ALU.mult).then_inc(s_fin, 1)
                        dve.wait_ge(s_fin, q * 5 + 2)
                        for e in range(2):
                            ins = dve.scalar_tensor_tensor(out=r[:, e], in0=m[:, e], scalar=-1.0, in1=neg[:, e, 0],
                                                           op0=ALU.mult, op1=ALU.subtract)
                        ins.then_inc(s_fin, 1)
                        dve.wait_ge(s_fin, q * 5 + 3)
                        dve.tensor_copy(neg[:, :, 1, :, :], r).then_inc(s_fin, 1)
                        dve.wait_ge(s_fin, q * 5 + 4)
                        dve.tensor_tensor(neg[:, :, 2, :, :], r, neg[:, :, 1, :, :], ALU.subtract).then_inc(s_fin, 1)
                        dve.wait_ge(s_fin, q * 5 + 5)

                def prologue():
                    for ahead, n in PROLOGUE:
                        unit(0, ahead, n, ahead, False)

                def body(u, par, v, plan, last):
                    for units in plan:
                        for ahead, n in units:
                            unit(u, ahead, n, (par + ahead) % 2, last)

                each_quad(dve, prologue, body, None)

            @block.gpsimd
            def _(gp):
                gp.memset(identb[:], 0.0)
                gp.memset(maskb[:], 0.0).then_inc(s_cst, 1)
                gp.wait_ge(s_cst, 1)
                gp.affine_select(out=identb[:], in_=identb[:], compare_op=ALU.not_equal, fill=1.0, base=0,
                                 pattern=[[-1, P]], channel_multiplier=1)
                gp.affine_select(out=maskb[:], in_=maskb[:], compare_op=ALU.is_ge, fill=MASKED, base=0,
                                 pattern=[[-1, P]], channel_multiplier=1).then_inc(s_cst, 1)
                for t in Vq:
                    gp.memset(t[:], 0.0).then_inc(s_vone, 1)
                gp.wait_ge(s_vone, 2)
                for t in Vq:
                    gp.memset(t[:, :, :, HD:2 * HD], 1.0).then_inc(s_vone, 1)

                def take_v(u, par):
                    gp.tensor_copy(Vq[par][:, :, :, 0:HD],
                                   VS[:, bass.ds(u, 1), :, :].rearrange("p u j (h f) -> p (u j) h f", h=4)) \
                      .then_inc(s_vq, 1)

                def prologue():
                    gp.wait_ge(s_vone, 4)
                    take_v(0, 0)

                def body(u, par, v, plan, last):
                    static = isinstance(u, int)
                    for g, (j, c) in enumerate(GROUPS):
                        if c != j // 4:
                            continue
                        wait_apart(gp, s_exp, u * STEPS + 4 * g + 4, s_pass)
                        diag = probs[g % PBUFS][:, :, P * j - 512 * c:P * j - 512 * c + P]
                        gp.affine_select(out=diag, in_=diag, compare_op=ALU.is_ge, fill=0.0, base=0,
                                         pattern=[[0, 4], [1, P]], channel_multiplier=-1).then_inc(s_mask, 1)
                        if j == 1 and not (static and u + 1 >= NT):
                            if not (static and u == 0):
                                gp.wait_ge(s_pv, u * NGROUPS)
                            take_v(u + 1, 1 - par)

                each_quad(gp, prologue, body, None)

            @block.scalar
            def _(act):
                def evacuate(u, par, v, c):
                    act.wait_ge(s_pv, u * NGROUPS + (NGROUPS if c else GROUPS.index((3, 0)) + 1))
                    if c == 0 and not (isinstance(u, int) and u < 2):
                        act.wait_ge(s_nd[par], v * 64)
                    act.activation(raw[par][:, 512 * c:512 * c + 512], acc[:, 512 * c:512 * c + 512],
                                   ACT.Copy).then_inc(s_raw, 1)

                def body(u, par, v, plan, last):
                    static = isinstance(u, int)
                    for g, (j, c) in enumerate(GROUPS):
                        for h in range(4):
                            k = 4 * g + h
                            a = 512 - width(j, c)
                            act.wait_ge(s_st, u * STEPS + k + 1)
                            if h == 0 and not (static and u == 0 and g < PBUFS):
                                act.wait_ge(s_pv, u * NGROUPS + g - PBUFS + 1)
                            act.activation(probs[g % PBUFS][:, h, a:512], st[k % SBANKS][:, a:512], ACT.Exp,
                                           scale=QSCALE).then_inc(s_exp, 1)
                        if g == EVACUATE_AT and not (static and u == 0):
                            evacuate(u - 1, 1 - par, None, 1)
                        if g == EVACUATE0_AT:
                            evacuate(u, par, u // 2 if static else v + 1 - par, 0)

                each_quad(act, None, body, lambda: evacuate(NT - 1, 1, None, 1))

            @block.tensor
            def _(pe):
                def unit(u, ahead, n, par, last):
                    num = unit_number(u, ahead, n, last)
                    bank = unit_bank(n, last)
                    if not (isinstance(num, int) and num < MBANKS):
                        pe.wait_ge(s_red, num - MBANKS + 1)
                    if n == "T":
                        pe.wait_ge(s_fin, (u + ahead) * 5 + 5)
                        pe.transpose(bank[0:96, 0:P // 2].bitcast(BF16),
                                     nm[par][:, :, :, :, :].rearrange("q e c p i -> q (e c p i)"),
                                     identb[:]).then_inc(s_mm, counts(u, ahead, n))
                        return
                    h, i, k0, w = UNITS[n]
                    if n == 0:
                        pe.wait_ge(s_ks[par], half_index[0](u, ahead) * LOAD + LOAD)
                    diagonal = k0 + w == (i + 1) * P
                    ins = pe.matmul(bank[:, 0:w], Qz[par][:, h, P * i:P * i + P], Km[par][:, h // 2, k0:k0 + w],
                                    start=True, stop=not diagonal)
                    if diagonal:
                        ins = pe.matmul(bank[:, w - P:w], identb[:], maskb[:], start=False, stop=True)
                    ins.then_inc(s_mm, counts(u, ahead, n))

                half_index = [None]

                def scores(u, par, k):
                    g, h = k // 4, k % 4
                    j, c = GROUPS[g]
                    if k == 0:
                        pe.wait_ge(s_qs[par], half_index[0](u, 0) * LOAD + LOAD)
                        pe.wait_ge(s_mrow, u * 32 + 32)
                    if not (isinstance(u, int) and u == 0 and k < SBANKS):
                        pe.wait_ge(s_exp, u * STEPS + k - SBANKS + 1)
                    a = 512 - width(j, c)
                    pe.matmul(st[k % SBANKS][:, a:512], Kz[par][:, h, P * j:P * j + P],
                              Qm[par][:, h // 2, 512 * c + a:512 * c + 512], start=True, stop=True).then_inc(s_st, 1)

                def values(u, par, g):
                    j, c = GROUPS[g]
                    if c == j // 4:
                        pe.wait_ge(s_mask, u * TPB + j + 1)
                    else:
                        pe.wait_ge(s_exp, u * STEPS + 4 * g + 4)
                    if g == 0:
                        pe.wait_ge(s_vq, u + 1)
                    if j == 0 and not (isinstance(u, int) and u == 0):
                        pe.wait_ge(s_raw, 2 * u - 1 + c)
                    a = 512 - width(j, c)
                    for h in range(4):
                        ins = pe.matmul(acc[32 * h:32 * h + 32, 512 * c + a:512 * c + 512], Vq[par][:, j, h, :],
                                        probs[g % PBUFS][:, h, a:512], start=(j == 0), stop=(j == 4 * c + 3))
                    ins.then_inc(s_pv, 1)

                def prologue():
                    pe.wait_ge(s_cst, 2)
                    half_index[0] = lambda u, ahead: (u + ahead) // 2
                    for ahead, n in PROLOGUE:
                        unit(0, ahead, n, ahead, False)

                def body(u, par, v, plan, last):
                    static = isinstance(u, int)
                    half_index[0] = (lambda u_, ahead: (u_ + ahead) // 2) if static else \
                        (lambda u_, ahead: v + ((1 if par else 2) + ahead) // 2)
                    for k in range(STEPS):
                        scores(u, par, k)
                        for ahead, n in plan[k]:
                            unit(u, ahead, n, (par + ahead) % 2, last)
                        if k >= VALUES_AT and (k - VALUES_AT) % 4 == 0:
                            values(u, par, (k - VALUES_AT) // 4)
                        elif k < VALUES_AT and (k - VALUES_AT) % 4 == 0 and not (static and u == 0):
                            values(u - 1, 1 - par, NGROUPS + (k - VALUES_AT) // 4)

                def epilogue():
                    for g in range((STEPS - 1 - VALUES_AT) // 4 + 1, NGROUPS):
                        values(NT - 1, 1, g)

                each_quad(pe, prologue, body, epilogue)


def head_sums():
    f = np.arange(D) // HD
    cosines = np.cos(np.pi / 2 * np.arange(NBATCH) / NBATCH)[:, None, None]
    same = (f[:, None] == f[None, :])[None] * cosines
    heads = (f[:, None] == (np.arange(32) % HEADS)[None, :])[None] * cosines
    spread = np.zeros((NBATCH, P, D))
    for n in range(NBATCH):
        spread[n, 32 * n + f, np.arange(D)] = 1.0
    return same.astype(np.float32), heads.astype(np.float32), spread.astype(np.float32)


def reached(eng, sem, value, total=None):
    if isinstance(value, int):
        value = value if total is None else min(value, total)
        if value <= 0:
            return
    eng.wait_ge(sem, value)


def middle_layers(nc, X, Y4, YT4, L2, ND, RD, w, shared_loaded):
    with ExitStack() as ctx:
        def sb(name, shape, dt=F32):
            return ctx.enter_context(nc.sbuf_tensor("c_" + name, shape, dt))

        def sem(name):
            return ctx.enter_context(nc.semaphore("c_" + name))

        def bank(name):
            return ctx.enter_context(nc.psum_tensor("c_" + name, [P, 4, P], F32))

        B = NBATCH
        EXP, R = 8, 32
        CH = TPB
        ident, half, eps = sb("ident", [P, P]), sb("half", [P, B]), sb("eps", [P, B])
        ow, gate, Wuv = sb("ow", [P, D]), sb("gate", [P, EXP]), sb("Wuv", [P, 2, EXP, R])
        Wo, Win, outw = sb("Wo", [P, 2, D]), sb("Win", [P, 3, D]), sb("outw", [P, D])
        bias, outb, router = sb("bias", [P, 3]), sb("outb", [P, D]), sb("router", [P, 8])
        sums, heads, spread = sb("sums", [P, B, D]), sb("heads", [P, B, 32]), sb("spread", [P, B, D])
        tri = sb("tri", [P, EXP, EXP])
        dens = sb("dens", [P, 512])
        num, den, attT = sb("num", [P, B, P]), sb("den", [P, B, P]), sb("attT", [P, B, P])
        LN = [(sb(f"stats{k}", [P, B, 6]), sb(f"mv{k}", [P, B, 2]), sb(f"rs{k}", [P, B])) for k in range(3)]
        y, yT = sb("y", [P, B, D]), sb("yT", [P, B, P])
        lg, rank = sb("lg", [P, B, EXP]), sb("rank", [P, B, EXP])
        cmp, eq = sb("cmp", [P, B, EXP, EXP]), sb("eq", [P, B, EXP, EXP])
        hs, th, wt = sb("hs", [P, B]), sb("th", [P, B, EXP]), sb("wt", [P, B, EXP])
        su = [sb(f"su{i}", [P, EXP, R]) for i in range(2)]
        sv = [sb(f"sv{i}", [P, EXP, R]) for i in range(2)]
        sw = [sb(f"sw{i}", [P, 2, P]) for i in range(2)]
        swT = sb("swT", [P, B, 2, P])
        z, zT, xb = sb("z", [P, B, D]), sb("zT", [P, B, P]), sb("xb", [P, B, D])
        qkv = sb("qkv", [P, 3, B, P])
        prod = [sb(f"prod{i}", [P, B, P]) for i in range(2)]
        av = [sb(f"av{i}", [P, B, P]) for i in range(2)]
        nsum, dn, at = sb("nsum", [P, B, P]), sb("dn", [P, P]), sb("at", [P, B, P])
        z4, yT4 = sb("z4", [P, B, D]), sb("yT4", [P, B, P])
        O, S, Ta, Tb = bank("O"), bank("S"), bank("Ta"), bank("Tb")
        UV, A = [bank("UV0"), bank("UV1")], [bank("A0"), bank("A1")]
        S_LG1, S_LG2, S_DN = S[:, 0, 0:B * EXP], S[:, 1, 0:B * 8], S[:, 2, :]

        s_w, s_cst, s_dn0, s_dr = sem("weights_loaded"), sem("const_steps"), sem("dens_loaded"), sem("dens_inverted")
        s_rd, s_nd, s_att = sem("dens_stored"), sem("attended_loaded"), sem("attT_done")
        s_p1, s_p3, s_wo, s_ex = sem("att1_projected"), sem("att2_projected"), sem("mixture_out_made"), sem("den_spread")
        s_r1, s_r2, s_r3 = sem("residual1_done"), sem("residual2_done"), sem("residual3_done")
        s_st, s_mv, s_pw, s_nm = [[sem(f"{n}{k}") for k in range(3)] for n in ("stats_done", "meanvar_done",
                                                                             "pow_steps", "normalized")]
        s_t1, s_t2, s_t3, s_tw = sem("y_transposed"), sem("z_transposed"), sem("z4_transposed"), sem("sw_transposed")
        s_yt, s_zt, s_y4t, s_swt = sem("yT_copied"), sem("zT_copied"), sem("yT4_copied"), sem("swT_copied")
        s_kept = sem("y4_kept")
        s_l1, s_l2, s_lg, s_lg2 = sem("logits1_made"), sem("logits2_made"), sem("logits1_copied"), sem("logits2_copied")
        s_uv, s_rt, s_th, s_tt, s_wt = sem("uv_made"), sem("route_steps"), sem("halves_done"), sem("tanh_done"), sem("weights_done")
        s_su, s_sv, s_sw = sem("silu_u"), sem("gated"), sem("weighted")
        s_xb, s_pj, s_qk = sem("xb_done"), sem("qkv_made"), sem("qkv_copied")
        s_pr, s_a, s_dp, s_av, s_ns = sem("prod_done"), sem("A_made"), sem("den_added"), sem("Av_done"), sem("num_steps")
        s_mx, s_rc, s_at = sem("den_clipped"), sem("den_inverted"), sem("at_done")
        s_pass = sem("passed")
        NW = 14

        def xs(c):
            return X[:, :, :].rearrange("p (b i) d -> p i b d", b=B)[:, bass.ds(c, 1), :, :] \
                .rearrange("p i b d -> p (i b) d")

        def flat(t):
            return t[:].rearrange("p a b -> p (a b)")

        def each_turn(eng, turn):
            def at_turn(i):
                chunks = [n if 0 <= n < CH else None for n in (i + 2, i + 1, i, i - 1)]
                turn(*chunks)

            for i in range(-2, 1):
                at_turn(i)
            with eng.Fori(1, CH - 2) as i:
                turn(i + 2, i + 1, i, i - 1)
            for i in range(CH - 2, CH + 1):
                at_turn(i)

        with nc.Block() as block:
            @block.sync
            def _(sp):
                for e in range(2):
                    sp.dma_start(dens[64 * e:64 * e + 64, :],
                                 ND[:, :, HD, 512 * e:512 * e + 512].rearrange("u h t -> (u h) t")).then_inc(s_dn0, 16)
                sp.wait_ge(s_dr, 1)
                for e in range(2):
                    sp.dma_start(RD[:, 512 * e:512 * e + 512], dens[64 * e:64 * e + 64, :]).then_inc(s_rd, 16)
                sp.wait_ge(s_rd, 32)

                def load(c):
                    for b in range(B):
                        sp.dma_start(num[:, b, :], ND[4 * b:4 * b + 4, :, 0:HD, bass.ts(c, P)]
                                     .rearrange("g h r q -> (g h) r q")).then_inc(s_nd, 16)
                        sp.dma_start(den[:, b, :], RD[HEADS * b:HEADS * b + HEADS, bass.ts(c, P)]
                                     .unsqueeze(1).broadcast_to([HEADS, HD, P])).then_inc(s_nd, 16)

                load(0)
                with sp.Fori(1, CH) as c:
                    sp.wait_ge(s_att, c)
                    load(c)

            @block.gpsimd
            def _(gp):
                gp.memset(half[:], -0.5)
                gp.memset(eps[:], EPS).then_inc(s_cst, 1)
                gp.memset(ident[:], 0.0).then_inc(s_cst, 1)
                gp.wait_ge(s_cst, 2)
                gp.affine_select(out=ident[:], in_=ident[:], compare_op=ALU.not_equal, fill=1.0, base=0,
                                 pattern=[[-1, P]], channel_multiplier=1).then_inc(s_cst, 1)
                gp.wait_ge(s_w, NW * 16)

                def power(k, c):
                    _, mv, rs = LN[k]
                    gp.wait_ge(s_mv[k], c + 1)
                    gp.tensor_tensor(rs[:], mv[:, :, 1], eps[:], ALU.add).then_inc(s_pw[k], 1)
                    gp.wait_ge(s_pw[k], c * 2 + 1)
                    gp.tensor_tensor(rs[:], rs[:], half[:], ALU.pow).then_inc(s_pw[k], 1)

                def weigh(c, b):
                    gp.wait_ge(s_sv, c * 4 + b + 1)
                    if b == 0:
                        gp.wait_ge(s_wt, c + 1)
                    reached(gp, s_tw, c * 2 + b // 2)
                    gp.tensor_tensor(sw[b % 2][:].rearrange("p c (e r) -> p (c e) r", r=R), sv[b % 2][:],
                                     wt[:, b, :].unsqueeze(2).broadcast_to([P, EXP, R]),
                                     ALU.mult).then_inc(s_sw, 1)

                def add_bias(c):
                    gp.wait_ge(s_r2, c + 1)
                    reached(gp, s_r3, c)
                    gp.tensor_tensor(xb[:], xs(c), outb[:].unsqueeze(1).broadcast_to([P, B, D]),
                                     ALU.add).then_inc(s_xb, 1)

                def sum_up(c, l):
                    gp.wait_ge(s_av, c * 4 + l + 1)
                    if l == 0:
                        reached(gp, s_at, c)
                    t = av[l % 2]
                    gp.tensor_tensor(t[:, 0:2, :], t[:, 0:2, :], t[:, 2:4, :], ALU.add).then_inc(s_ns, 1)
                    gp.wait_ge(s_ns, c * 8 + 2 * l + 1)
                    gp.tensor_tensor(nsum[:, l, :], t[:, 0, :], t[:, 1, :], ALU.add).then_inc(s_ns, 1)

                def turn(a, b, c, d):
                    if c is not None:
                        power(1, c)
                    if d is not None:
                        power(2, d)
                    if c is not None:
                        add_bias(c)
                    if a is not None:
                        power(0, a)
                    if b is not None:
                        weigh(b, 0)
                        weigh(b, 1)
                    if c is not None:
                        sum_up(c, 0)
                        sum_up(c, 1)
                    if b is not None:
                        weigh(b, 2)
                        weigh(b, 3)
                    if c is not None:
                        sum_up(c, 2)
                        sum_up(c, 3)

                each_turn(gp, turn)

            @block.vector
            def _(dve):
                def xtile(c):
                    return lambda b: X[:, TPB * b + c, :]

                def moments(k, c, updated):
                    stats, mv, _ = LN[k]
                    src = xtile(c)
                    wait_apart(dve, updated, c + 1, s_pass)
                    for b in range(B):
                        ins = dve.bn_stats(stats[:, b, :], src(b))
                    ins.then_inc(s_st[k], 1)
                    wait_apart(dve, s_st[k], c + 1, s_pass)
                    for b in range(B):
                        ins = dve.bn_aggr(mv[:, b, :], stats[:, b, :])
                    ins.then_inc(s_mv[k], 1)

                def normalize(k, c, dst, transposed, kept=None):
                    _, mv, rs = LN[k]
                    src = xtile(c)
                    dve.wait_ge(s_mv[k], c + 1)
                    dve.wait_ge(s_pw[k], c * 2 + 2)
                    reached(dve, transposed, c)
                    if kept:
                        reached(dve, kept, c)
                    for b in range(B):
                        ins = dve.tensor_scalar(dst[:, b, :], src(b), mv[:, b, 0:1], rs[:, b:b + 1],
                                                ALU.subtract, ALU.mult)
                    ins.then_inc(s_nm[k], 1)

                def divide1(c):
                    dve.wait_ge(s_nd, c * 128 + 128)
                    reached(dve, s_p1, c)
                    dve.tensor_tensor(attT[:], num[:], den[:], ALU.mult).then_inc(s_att, 1)

                def residual1(c):
                    dve.wait_ge(s_p1, c + 1)
                    dve.tensor_tensor(xs(c), xs(c), O[:], ALU.add).then_inc(s_r1, 1)

                mine = lg[:].unsqueeze(3).broadcast_to([P, B, EXP, EXP])
                other = lg[:].unsqueeze(2).broadcast_to([P, B, EXP, EXP])

                def compare(c):
                    dve.wait_ge(s_l1, c + 1)
                    dve.tensor_copy(lg[:], S_LG1.rearrange("p (b e) -> p b e", b=B)).then_inc(s_lg, 1)
                    dve.wait_ge(s_lg, c + 1)
                    n = c * 7
                    dve.tensor_tensor(cmp[:], other, mine, ALU.is_gt)
                    dve.tensor_tensor(eq[:], other, mine, ALU.is_equal).then_inc(s_rt, 1)
                    dve.wait_ge(s_rt, n + 1)
                    dve.tensor_tensor(eq[:], eq[:], tri[:].unsqueeze(1).broadcast_to([P, B, EXP, EXP]),
                                      ALU.mult).then_inc(s_rt, 1)
                    dve.wait_ge(s_rt, n + 2)
                    dve.tensor_tensor(cmp[:], cmp[:], eq[:], ALU.add).then_inc(s_rt, 1)

                def choose(c):
                    n = c * 7
                    dve.wait_ge(s_rt, n + 3)
                    dve.tensor_reduce(rank[:], cmp[:], AX.X, ALU.add).then_inc(s_rt, 1)
                    dve.wait_ge(s_rt, n + 4)
                    dve.tensor_scalar(rank[:], rank[:], 2.0, 0.5, ALU.is_lt, ALU.mult).then_inc(s_rt, 1)
                    dve.wait_ge(s_rt, n + 5)
                    dve.tensor_tensor(th[:], rank[:], lg[:], ALU.mult).then_inc(s_rt, 1)
                    dve.wait_ge(s_rt, n + 6)
                    dve.tensor_reduce(hs[:], th[:], AX.X, ALU.add).then_inc(s_rt, 1)
                    dve.wait_ge(s_rt, n + 7)
                    dve.tensor_tensor(th[:], lg[:], hs[:].unsqueeze(2).broadcast_to([P, B, EXP]),
                                      ALU.subtract).then_inc(s_th, 1)

                def weights(c):
                    dve.wait_ge(s_tt, c + 1)
                    reached(dve, s_sw, c * 4)
                    dve.scalar_tensor_tensor(out=wt[:].rearrange("p b e -> p (b e)"),
                                             in0=th[:].rearrange("p b e -> p (b e)"), scalar=1.0,
                                             in1=rank[:].rearrange("p b e -> p (b e)"),
                                             op0=ALU.add, op1=ALU.mult).then_inc(s_wt, 1)

                def gated(c, b):
                    dve.wait_ge(s_su, c * 4 + b + 1)
                    reached(dve, s_sw, c * 4 + b - 1)
                    dve.tensor_tensor(sv[b % 2][:].rearrange("p e r -> p (e r)"),
                                      su[b % 2][:].rearrange("p e r -> p (e r)"),
                                      flat(UV[b % 2])[:, EXP * R:], ALU.mult).then_inc(s_sv, 1)

                def residual2(c):
                    dve.wait_ge(s_wo, c + 1)
                    dve.tensor_tensor(xs(c), xs(c), O[:], ALU.add).then_inc(s_r2, 1)

                def product(c, l):
                    if l == 0:
                        dve.wait_ge(s_qk, c * 3 + 2)
                    reached(dve, s_dp, c * 4 + l - 1)
                    dve.tensor_tensor(prod[l % 2][:], qkv[:, 1, :, :],
                                      qkv[:, 0, l, :].unsqueeze(1).broadcast_to([P, B, P]),
                                      ALU.mult).then_inc(s_pr, 1)

                def weigh_values(c, l):
                    dve.wait_ge(s_a, c * 4 + l + 1)
                    if l == 0:
                        dve.wait_ge(s_qk, c * 3 + 3)
                    reached(dve, s_ns, c * 8 + 2 * l - 2)
                    dve.tensor_tensor(av[l % 2][:], A[(l + 1) % 2][:], qkv[:, 2, :, :], ALU.mult).then_inc(s_av, 1)

                def invert(c):
                    dve.wait_ge(s_dp, c * 4 + 4)
                    reached(dve, s_ex, c)
                    dve.tensor_scalar(dn[:], S_DN, 1e-3, None, ALU.max).then_inc(s_mx, 1)
                    dve.wait_ge(s_mx, c + 1)
                    dve.reciprocal(dn[:], dn[:]).then_inc(s_rc, 1)

                def divide2(c):
                    dve.wait_ge(s_ex, c + 1)
                    dve.wait_ge(s_ns, c * 8 + 8)
                    reached(dve, s_p3, c)
                    dve.tensor_tensor(at[:], nsum[:], Tb[:], ALU.mult).then_inc(s_at, 1)

                def residual3(c):
                    dve.wait_ge(s_p3, c + 1)
                    dve.wait_ge(s_xb, c + 1)
                    dve.tensor_tensor(xs(c), xb[:], O[:], ALU.add).then_inc(s_r3, 1)

                def keep_logits(c):
                    dve.wait_ge(s_l2, c + 1)
                    dve.tensor_copy(L2[:, bass.ts(c, B), :], S_LG2.rearrange("p (b e) -> p b e", b=B)) \
                       .then_inc(s_lg2, 1)

                dve.wait_ge(s_dn0, 32)
                dve.reciprocal(dens[:], dens[:]).then_inc(s_dr, 1)
                dve.wait_ge(s_w, NW * 16)

                def turn(a, b, c, d):
                    if c is not None:
                        moments(1, c, s_r2)
                    if d is not None:
                        residual3(d)
                    if a is not None:
                        divide1(a)
                    if d is not None:
                        moments(2, d, s_r3)
                    if c is not None:
                        normalize(1, c, z, s_t2)
                    if b is not None:
                        compare(b)
                    if d is not None:
                        normalize(2, d, z4, s_t3, s_kept)
                    if b is not None:
                        choose(b)
                    if c is not None:
                        product(c, 0)
                        product(c, 1)
                    if a is not None:
                        residual1(a)
                        moments(0, a, s_r1)
                    if d is not None:
                        keep_logits(d)
                    if b is not None:
                        weights(b)
                        gated(b, 0)
                        gated(b, 1)
                    if c is not None:
                        weigh_values(c, 0)
                        product(c, 2)
                        weigh_values(c, 1)
                        product(c, 3)
                    if a is not None:
                        normalize(0, a, y, s_t1)
                    if b is not None:
                        gated(b, 2)
                        gated(b, 3)
                    if c is not None:
                        weigh_values(c, 2)
                        weigh_values(c, 3)
                        invert(c)
                    if b is not None:
                        residual2(b)
                    if c is not None:
                        divide2(c)

                each_turn(dve, turn)

            @block.scalar
            def _(act):
                for dst, src in ((ow[:], w["ow"]), (gate[:], w["gate"]),
                                 (Wuv[:, 0], w["Wu"].rearrange("e d r -> d e r")),
                                 (Wuv[:, 1], w["Wv"].rearrange("e d r -> d e r")),
                                 (Wo[:], w["Wo"].rearrange("(c e) r d -> (e r) c d", c=2)),
                                 (Win[:], w["Win"].rearrange("d (c n) -> d c n", c=3)), (outw[:], w["outw"]),
                                 (bias[:], w["bias"]), (outb[:], w["outb"].partition_broadcast(P)),
                                 (router[:], w["router"]), (sums[:], w["sums"].rearrange("n f g -> f n g")),
                                 (heads[:], w["heads"].rearrange("n f g -> f n g")),
                                 (spread[:], w["spread"].rearrange("n f g -> f n g")),
                                 (tri[:].rearrange("p e f -> p (e f)"), w["tri"].partition_broadcast(P))):
                    act.dma_start(dst, src).then_inc(s_w, 16)
                act.wait_ge(s_w, NW * 16)

                def copy_y(c):
                    act.wait_ge(s_t1, c + 1)
                    reached(act, s_uv, c * 4)
                    act.activation(yT[:], Ta[:], ACT.Copy).then_inc(s_yt, 1)

                def silu_u(c, b):
                    act.wait_ge(s_uv, c * 4 + b + 1)
                    reached(act, s_sv, c * 4 + b - 1)
                    act.activation(su[b % 2][:].rearrange("p e r -> p (e r)"), flat(UV[b % 2])[:, 0:EXP * R],
                                   ACT.Silu).then_inc(s_su, 1)

                def tanh(c):
                    act.wait_ge(s_th, c + 1)
                    act.activation(th[:], th[:], ACT.Tanh).then_inc(s_tt, 1)

                def copy_hidden(c, n):
                    act.wait_ge(s_tw, c * 2 + n + 1)
                    if n == 0:
                        reached(act, s_wo, c)
                    act.activation(swT[:, 2 * n:2 * n + 2, :, :].rearrange("p a b q -> p (a b) q"),
                                   (Tb if n == 0 else Ta)[:], ACT.Copy).then_inc(s_swt, 1)

                def copy_z(c):
                    act.wait_ge(s_t2, c + 1)
                    reached(act, s_pj, c * 3)
                    act.activation(zT[:], Tb[:], ACT.Copy).then_inc(s_zt, 1)

                def copy_qkv(c, n):
                    act.wait_ge(s_pj, c * 3 + n + 1)
                    if n == 0:
                        reached(act, s_pr, c * 4)
                    if n == 2:
                        reached(act, s_av, c * 4)
                    act.activation(qkv[:, n, :, :], A[n % 2][:], ACT.Relu if n < 2 else ACT.Identity,
                                   bias=bias[:, n:n + 1]).then_inc(s_qk, 1)

                def copy_y4(c):
                    act.wait_ge(s_t3, c + 1)
                    reached(act, s_l2, c)
                    act.activation(yT4[:], Ta[:], ACT.Copy).then_inc(s_y4t, 1)
                    act.activation(YT4[:, bass.ts(c, B), :], Ta[:], ACT.Copy).then_inc(s_y4t, 1)
                    act.activation(Y4[:, bass.ts(c, B), :], z4[:], ACT.Copy).then_inc(s_kept, 1)

                def turn(a, b, c, d):
                    if isinstance(a, int) and a == 1:
                        for dst, src in ((w["WG"][:, 7, :], w["sg"]), (w["WU"][:, 7, :], w["su"]),
                                         (w["WD"][:, 7, :, :], w["sd"].rearrange("(c p) d -> p c d", p=P))):
                            act.dma_start(dst, src).then_inc(shared_loaded, 16)
                    if b is not None:
                        copy_y(b)
                        silu_u(b, 0)
                        silu_u(b, 1)
                    if c is not None:
                        copy_z(c)
                        copy_qkv(c, 0)
                        copy_qkv(c, 1)
                        copy_qkv(c, 2)
                    if d is not None:
                        copy_y4(d)
                    if b is not None:
                        tanh(b)
                        silu_u(b, 2)
                        silu_u(b, 3)
                        copy_hidden(b, 0)
                        copy_hidden(b, 1)

                each_turn(act, turn)

            @block.tensor
            def _(pe):
                pe.wait_ge(s_w, NW * 16)
                pe.wait_ge(s_cst, 3)

                def project1(c):
                    pe.wait_ge(s_att, c + 1)
                    reached(pe, s_r3, c - 2)
                    for b in range(B):
                        ins = pe.matmul(O[:, b, :], attT[:, b, :], ow[:], start=True, stop=True)
                    ins.then_inc(s_p1, 1)

                def transpose1(c):
                    pe.wait_ge(s_nm[0], c + 1)
                    reached(pe, s_swt, c * 2)
                    for b in range(B):
                        ins = pe.transpose(Ta[:, b, :], y[:, b, :], ident[:])
                    ins.then_inc(s_t1, 1)

                def logits1(c):
                    pe.wait_ge(s_yt, c + 1)
                    reached(pe, s_mx, c - 1)
                    for b in range(B):
                        ins = pe.matmul(S_LG1[:, b * EXP:b * EXP + EXP], yT[:, b, :], gate[:], start=True, stop=True)
                    ins.then_inc(s_l1, 1)

                def up(c, b):
                    reached(pe, s_sv, c * 4 + b - 1)
                    pe.matmul(flat(UV[b % 2]), yT[:, b, :], Wuv[:].rearrange("p a e r -> p (a e r)"),
                              start=True, stop=True).then_inc(s_uv, 1)

                def transpose_hidden(c, n):
                    T = Tb if n == 0 else Ta
                    if n == 0:
                        reached(pe, s_zt, c, CH)
                    else:
                        reached(pe, s_y4t, 2 * c - 2)
                    for b in range(2):
                        pe.wait_ge(s_sw, c * 4 + 2 * n + b + 1)
                        for k in range(2):
                            ins = pe.transpose(T[:, 2 * b + k, :], sw[b][:, k, :], ident[:])
                    ins.then_inc(s_tw, 1)

                def down(c):
                    pe.wait_ge(s_swt, c * 2 + 2)
                    reached(pe, s_r1, c + 2, CH)
                    for b in range(B):
                        for k in range(2):
                            ins = pe.matmul(O[:, b, :], swT[:, b, k, :], Wo[:, k, :], start=(k == 0), stop=(k == 1))
                    ins.then_inc(s_wo, 1)

                def transpose2(c):
                    pe.wait_ge(s_nm[1], c + 1)
                    reached(pe, s_at, c)
                    reached(pe, s_swt, c * 2 + 1, 2 * CH)
                    for b in range(B):
                        ins = pe.transpose(Tb[:, b, :], z[:, b, :], ident[:])
                    ins.then_inc(s_t2, 1)

                def project_qkv(c, n):
                    if n == 0:
                        pe.wait_ge(s_zt, c + 1)
                        reached(pe, s_av, c * 4)
                    if n == 2:
                        pe.wait_ge(s_qk, c * 3 + 1)
                    pe.matmul(flat(A[n % 2]), Win[:, n, :], flat(zT), start=True, stop=True).then_inc(s_pj, 1)

                def scores(c, l):
                    pe.wait_ge(s_pr, c * 4 + l + 1)
                    if l < 2:
                        pe.wait_ge(s_qk, c * 3 + 2 + l)
                    else:
                        pe.wait_ge(s_av, c * 4 + l - 1)
                    for s in range(B):
                        ins = pe.matmul(A[(l + 1) % 2][:, s, :], sums[:, abs(l - s), :], prod[l % 2][:, s, :],
                                        start=True, stop=True)
                    ins.then_inc(s_a, 1)
                    if l == 0:
                        reached(pe, s_lg, c + 2, CH)
                        reached(pe, s_lg2, c)
                    for s in range(B):
                        ins = pe.matmul(S_DN[32 * l:32 * l + 32, :], heads[:, abs(l - s), :], prod[l % 2][:, s, :],
                                        start=(s == 0), stop=(s == B - 1))
                    ins.then_inc(s_dp, 1)

                def spread_inverse(c):
                    pe.wait_ge(s_rc, c + 1)
                    reached(pe, s_swt, c * 2 + 3, 2 * CH)
                    for l in range(B):
                        ins = pe.matmul(Tb[:, l, :], spread[:, l, :], dn[:], start=True, stop=True)
                    ins.then_inc(s_ex, 1)

                def project3(c):
                    pe.wait_ge(s_at, c + 1)
                    reached(pe, s_r2, c + 2, CH)
                    for b in range(B):
                        ins = pe.matmul(O[:, b, :], at[:, b, :], outw[:], start=True, stop=True)
                    ins.then_inc(s_p3, 1)

                def transpose3(c):
                    pe.wait_ge(s_nm[2], c + 1)
                    reached(pe, s_yt, c + 3, CH)
                    for b in range(B):
                        ins = pe.transpose(Ta[:, b, :], z4[:, b, :], ident[:])
                    ins.then_inc(s_t3, 1)

                def logits2(c):
                    pe.wait_ge(s_y4t, c * 2 + 1)
                    reached(pe, s_lg, c + 3, CH)
                    for b in range(B):
                        ins = pe.matmul(S_LG2[:, b * 8:b * 8 + 8], yT4[:, b, :], router[:], start=True, stop=True)
                    ins.then_inc(s_l2, 1)

                def turn(a, b, c, d):
                    if d is not None:
                        project3(d)
                    if b is not None:
                        transpose1(b)
                        logits1(b)
                        up(b, 0)
                        up(b, 1)
                    if c is not None:
                        transpose2(c)
                        project_qkv(c, 0)
                        project_qkv(c, 1)
                    if a is not None:
                        project1(a)
                    if c is not None:
                        project_qkv(c, 2)
                    if d is not None:
                        transpose3(d)
                        logits2(d)
                    if c is not None:
                        scores(c, 0)
                        scores(c, 1)
                    if b is not None:
                        up(b, 2)
                        up(b, 3)
                        transpose_hidden(b, 0)
                    if c is not None:
                        scores(c, 2)
                        scores(c, 3)
                    if b is not None:
                        transpose_hidden(b, 1)
                        down(b)
                    if c is not None:
                        spread_inverse(c)

                each_turn(pe, turn)


RTILES = TILES + 7
NEXP = 8


def order_tokens(nc, X, Y4, YT4, L2, slots, scale, experts, YS, w, shared_loaded, experts_loaded):
    with ExitStack() as ctx:
        def sb(name, shape, dt=F32):
            return ctx.enter_context(nc.sbuf_tensor("d_" + name, shape, dt))

        def sem(name):
            return ctx.enter_context(nc.semaphore("d_" + name))

        SH = [P, TILES, NEXP]
        zero = sb("zero", [P, D])
        before, ones = sb("before", [P, P]), sb("ones", [P, P])
        rows = sb("rows", [P, NEXP])
        tau = sb("tau", [1, RTILES])
        top, sm = sb("top", [P, TILES]), sb("sm", [P, TILES])
        dl, oh, sc = sb("dl", SH), sb("oh", SH), sb("sc", SH)
        run = [sb(f"run{i}", SH) for i in range(2)]
        ti = sb("ti", [P, NEXP], I32)
        tl = sb("tl", [P, NEXP])
        ends = [sb(f"ends{i}", [P, NEXP]) for i in range(2)]
        ct = sb("ct", [1, RTILES, 6])
        sf = sb("sf", [P, TILES])
        HC = 4
        CH = TPB
        sg = [sb(f"sg{i}", [P, NBATCH * P]) for i in range(2)]
        hid = [sb(f"hid{i}", [P, HC, NBATCH * P]) for i in range(2)]
        WG, WU, WD = w["WG"], w["WU"], w["WD"]
        pR = ctx.enter_context(nc.psum_tensor("d_pR", SH, F32))
        pC = ctx.enter_context(nc.psum_tensor("d_pC", SH, F32))
        s_c, s_k, s_z0, s_z = sem("const_loaded"), sem("const_steps"), sem("zero_made"), sem("YS_zeroed")
        s_dl, s_ex, s_d, s_oh, s_cnt = sem("shifted"), sem("exp_done"), sem("dve_steps"), sem("onehot"), sem("counted")
        pG, pU = [[ctx.enter_context(nc.psum_tensor(f"d_p{n}{i}", [P, 512], F32)) for i in range(2)] for n in "GU"]
        pO = ctx.enter_context(nc.psum_tensor("d_pO", [P, NBATCH, D], F32))
        s_slots, s_sc = sem("slots_done"), sem("scattered")
        s_g, s_u, s_sg, s_hid = sem("gate_made"), sem("up_made"), sem("silu_done"), sem("hidden_done")
        s_do, s_res = sem("down_made"), sem("residual_done")

        def each_chunk(eng, chunk):
            chunk(0, 0)
            chunk(1, 1)
            with eng.Fori(1, CH // 2) as v:
                chunk(v * 2, 0)
                chunk(v * 2 + 1, 1)

        with nc.Block() as block:
            @block.sync
            def _(sp):
                sp.dma_start(rows[:], w["down8"].partition_broadcast(P)).then_inc(s_c, 16)
                sp.dma_start(tau[:], w["tau"].rearrange("(a n) -> a n", a=1)).then_inc(s_c, 16)
                sp.wait_ge(s_z0, 1)
                sp.dma_start(YS.rearrange("(n p) d -> p n d", p=P),
                             zero[:].unsqueeze(1).broadcast_to([P, RTILES, D])).then_inc(s_z, 16)
                for dst, src in ((w["WG"][:, 0:7, :], w["gate_w"].rearrange("e d h -> d e h")),
                                 (w["WU"][:, 0:7, :], w["up_w"].rearrange("e d h -> d e h")),
                                 (w["WD"][:, 0:7, :, :].rearrange("p e c d -> p (e c) d"),
                                  w["down_w"].rearrange("e (c p) d -> p (e c) d", p=P))):
                    sp.dma_start(dst, src).then_inc(experts_loaded, 16)
                sp.wait_ge(experts_loaded, 3 * 16)

            @block.gpsimd
            def _(gp):
                gp.memset(zero[:], 0.0).then_inc(s_z0, 1)
                gp.memset(before[:], 1.0).then_inc(s_k, 1)
                gp.wait_ge(s_k, 1)
                gp.affine_select(out=before[:], in_=before[:], compare_op=ALU.is_gt, fill=0.0, base=0,
                                 pattern=[[1, P]], channel_multiplier=-1).then_inc(s_k, 1)
                gp.memset(ones[:], 1.0).then_inc(s_k, 1)
                gp.wait_ge(s_z, 16)

                gp.wait_ge(s_slots, 1)
                for n in range(TILES):
                    gp.indirect_dma_start(out=YS, out_offset=bass.IndirectOffsetOnAxis(ap=slots[:, n:n + 1], axis=0),
                                          in_=Y4[:, n, :], in_offset=None).then_inc(s_sc, 16)
                gp.wait_ge(s_sc, TILES * 16)

            @block.scalar
            def _(act):
                act.wait_ge(s_dl, 1)
                act.activation(dl[:], dl[:], ACT.Exp).then_inc(s_ex, 1)

                def chunk(i, par):
                    for c in range(HC):
                        m = i * HC + c
                        act.wait_ge(s_g, m + 1)
                        reached(act, s_hid, m - 1)
                        act.activation(sg[c % 2][:], pG[c % 2][:], ACT.Silu).then_inc(s_sg, 1)

                each_chunk(act, chunk)

            @block.tensor
            def _(pe):
                pe.wait_ge(shared_loaded, 3 * 16)

                def up(i, c):
                    m = i * HC + c
                    reached(pe, s_hid, m - 1)
                    tokens = YT4[:, bass.ts(i, NBATCH), :].rearrange("p t q -> p (t q)")
                    pe.matmul(pG[c % 2][:], WG[:, 7, c * P:c * P + P], tokens, start=True, stop=True).then_inc(s_g, 1)
                    pe.matmul(pU[c % 2][:], WU[:, 7, c * P:c * P + P], tokens, start=True,
                              stop=True).then_inc(s_u, 1)

                def down(i, par):
                    pe.wait_ge(s_hid, i * HC + HC)
                    reached(pe, s_res, i)
                    for b in range(NBATCH):
                        for c in range(HC):
                            ins = pe.matmul(pO[:, b, :], hid[par][:, c, b * P:b * P + P], WD[:, 7, c, :],
                                            start=(c == 0), stop=(c == HC - 1))
                    ins.then_inc(s_do, 1)

                def chunk(i, par):
                    up(i, 0)
                    up(i, 1)
                    if isinstance(i, int) and i == 0:
                        pe.wait_ge(s_k, 3)
                        pe.wait_ge(s_oh, 1)
                        flat_oh = oh[:].rearrange("p t e -> p (t e)")
                        pe.matmul(pR[:].rearrange("p t e -> p (t e)"), before[:], flat_oh, start=True, stop=True)
                        pe.matmul(pC[:].rearrange("p t e -> p (t e)"), ones[:], flat_oh, start=True,
                                  stop=True).then_inc(s_cnt, 1)
                    else:
                        down(i - 1, 1 - par)
                    up(i, 2)
                    up(i, 3)

                each_chunk(pe, chunk)
                down(CH - 1, 1)

            @block.vector
            def _(dve):
                steps = [0]
                SHARED_FROM, SHARED_EVERY = 6, 4

                def gate(i, par, c):
                    dve.wait_ge(s_sg, i * HC + c + 1)
                    dve.wait_ge(s_u, i * HC + c + 1)
                    if c == 0:
                        reached(dve, s_do, i - 1)
                    dve.tensor_tensor(hid[par][:, c, :], sg[c % 2][:], pU[c % 2][:], ALU.mult).then_inc(s_hid, 1)

                def add(i):
                    dve.wait_ge(s_do, i + 1)
                    x = X[:, :, :].rearrange("p (b i) d -> p i b d", b=NBATCH)[:, bass.ds(i, 1), :, :] \
                        .rearrange("p i b d -> p (i b) d")
                    dve.tensor_tensor(x, x, pO[:], ALU.add).then_inc(s_res, 1)

                def chunk(i, par):
                    if isinstance(i, int) and i == 0:
                        return
                    gate(i, par, 0)
                    gate(i, par, 1)
                    add(i - 1)
                    gate(i, par, 2)
                    gate(i, par, 3)

                def step(ins):
                    steps[0] += 1
                    ins.then_inc(s_d, 1)
                    c, rest = divmod(steps[0] - SHARED_FROM, SHARED_EVERY)
                    if rest == 0 and 0 <= c < HC:
                        gate(0, 0, c)
                    dve.wait_ge(s_d, steps[0])

                def wide(t):
                    return t[:].unsqueeze(2).broadcast_to(SH)

                dve.wait_ge(s_c, 32)
                step(dve.tensor_reduce(top[:], L2[:], AX.X, ALU.max))
                dve.tensor_tensor(dl[:], L2[:], wide(top), ALU.subtract).then_inc(s_dl, 1)
                step(dve.tensor_tensor(sc[:], L2[:], wide(top), ALU.is_equal))
                step(dve.tensor_tensor(sc[:], sc[:], rows[:].unsqueeze(1).broadcast_to(SH), ALU.mult))
                step(dve.tensor_reduce(top[:], sc[:], AX.X, ALU.max))
                dve.tensor_tensor(oh[:], sc[:], wide(top), ALU.is_equal).then_inc(s_oh, 1)
                dve.wait_ge(s_oh, 1)
                dve.wait_ge(s_ex, 1)
                step(dve.tensor_reduce(sm[:], dl[:], AX.X, ALU.add))
                step(dve.reciprocal(sm[:], sm[:]))
                step(dve.tensor_scalar(top[:], oh[:, :, 7], -2.0, 2.0, ALU.mult, ALU.add))
                step(dve.tensor_tensor(scale[:], sm[:], top[:], ALU.mult))
                dve.wait_ge(s_cnt, 1)
                step(dve.tensor_copy(run[0][:], pC[:]))
                k = 0
                for s in (1, 2, 4, 8, 16):
                    a, b = run[k], run[1 - k]
                    dve.tensor_copy(b[:, 0:s, :], a[:, 0:s, :])
                    step(dve.tensor_tensor(b[:, s:, :], a[:, s:, :], a[:, 0:TILES - s, :], ALU.add))
                    k = 1 - k
                step(dve.tensor_scalar(ti[:], run[k][:, TILES - 1, :], float(P - 1), None, ALU.add))
                step(dve.tensor_scalar(ti[:], ti[:], 7, None, ALU.arith_shift_right))
                step(dve.tensor_copy(tl[:], ti[:]))
                step(dve.tensor_copy(ends[0][:], tl[:]))
                j = 0
                for s in (1, 2, 4):
                    a, b = ends[j], ends[1 - j]
                    dve.tensor_copy(b[:, 0:s], a[:, 0:s])
                    step(dve.tensor_tensor(b[:, s:], a[:, s:], a[:, 0:NEXP - s], ALU.add))
                    j = 1 - j
                step(dve.tensor_tensor(ct[:], tau[:].unsqueeze(2).broadcast_to([1, RTILES, 6]),
                                       ends[j][0:1, 0:6].unsqueeze(1).broadcast_to([1, RTILES, 6]), ALU.is_ge))
                step(dve.tensor_reduce(tau[:], ct[:], AX.X, ALU.add))
                step(dve.tensor_copy(experts[:], tau[:]))
                step(dve.tensor_tensor(tl[:], ends[j][:], tl[:], ALU.subtract))
                step(dve.tensor_scalar(tl[:], tl[:], float(P), None, ALU.mult))
                step(dve.tensor_tensor(run[k][:], run[k][:], pC[:], ALU.subtract))
                step(dve.tensor_tensor(run[k][:], run[k][:], pR[:], ALU.add))
                step(dve.tensor_tensor(run[k][:], run[k][:], tl[:].unsqueeze(1).broadcast_to(SH), ALU.add))
                step(dve.tensor_tensor(run[k][:], run[k][:], oh[:], ALU.mult))
                step(dve.tensor_reduce(sf[:], run[k][:], AX.X, ALU.add))
                dve.tensor_copy(slots[:], sf[:]).then_inc(s_slots, 1)
                each_chunk(dve, chunk)
                add(CH - 1)


def routed_experts(nc, WG, WU, WD, experts, YS, RO):
    with ExitStack() as ctx:
        def sb(name, shape, dt=F32):
            return ctx.enter_context(nc.sbuf_tensor("e_" + name, shape, dt))

        def sem(name):
            return ctx.enter_context(nc.semaphore("e_" + name))

        def two(name, shape):
            return [sb(f"{name}{i}", shape) for i in range(2)]

        HC = 4
        ident = sb("ident", [P, P])
        xin, xT, sg, h, hT, ro = (two(n, s) for n, s in (
            ("xin", [P, D]), ("xT", [P, P]), ("sg", [P, 512]), ("h", [P, HC, P]), ("hT", [P, HC, P]), ("ro", [P, D])))
        pX = ctx.enter_context(nc.psum_tensor("e_pX", [P, 512], F32))
        pG = [ctx.enter_context(nc.psum_tensor(f"e_pG{i}", [P, 512], F32)) for i in range(2)]
        pU = [ctx.enter_context(nc.psum_tensor(f"e_pU{i}", [P, 512], F32)) for i in range(2)]
        pH = ctx.enter_context(nc.psum_tensor("e_pH", [P, HC, P], F32))
        pO = ctx.enter_context(nc.psum_tensor("e_pO", [P, 512], F32))
        s_k = sem("const_steps")
        s_in, s_ro = [[sem(f"{n}{i}") for i in range(2)] for n in ("tile_loaded", "tile_stored")]
        s_tx, s_xt, s_g, s_u, s_sg, s_h = (sem("pX_made"), sem("xT_copied"), sem("gate_made"), sem("up_made"),
                                           sem("silu_done"), sem("h_done"))
        s_th, s_ht, s_o, s_oc = sem("pH_made"), sem("hT_copied"), sem("pO_made"), sem("ro_copied")

        def each_turn(eng, turn):
            full = ("next", "this", "last", "before")
            turn(0, 0, 0, full[:2])
            turn(1, 1, 0, full[:3])
            turn(2, 0, 1, full)
            with eng.Fori(1, (RTILES - 4) // 2) as v:
                turn(v * 2 + 1, 1, v, full)
                turn(v * 2 + 2, 0, v + 1, full)
            for t in range((RTILES - 4) // 2 * 2 + 1, RTILES + 2):
                turn(t, t % 2, t // 2, [n for n, tile in zip(full, (t + 1, t, t - 1, t - 2)) if tile < RTILES])

        def uses(par, half, ahead):
            return half + (par + ahead) // 2 + 1

        with nc.Block() as block:
            @block.sync
            def _(sp):
                def load(t, k):
                    sp.dma_start(xin[k][:], YS[bass.ts(t, P), :]).then_inc(s_in[k], 16)

                load(0, 0)
                load(1, 1)

                def turn(t, par, half, which):
                    if isinstance(t, int) and t == 0:
                        sp.wait_ge(s_tx, 1)
                        load(2, 0)
                    if not (isinstance(t, int) and t + 3 >= RTILES):
                        sp.wait_ge(s_tx, t + 2)
                        load(t + 3, 1 - par)
                    if "before" in which:
                        sp.wait_ge(s_oc, t - 1)
                        sp.dma_start(RO[bass.ts(t - 2, P), :], ro[par][:]).then_inc(s_ro[par], 16)

                each_turn(sp, turn)
                sp.wait_ge(s_ro[0], (RTILES + 1) // 2 * 16)
                sp.wait_ge(s_ro[1], RTILES // 2 * 16)

            @block.gpsimd
            def _(gp):
                gp.memset(ident[:], 0.0).then_inc(s_k, 1)
                gp.wait_ge(s_k, 1)
                gp.affine_select(out=ident[:], in_=ident[:], compare_op=ALU.not_equal, fill=1.0, base=0,
                                 pattern=[[-1, P]], channel_multiplier=1).then_inc(s_k, 1)

            @block.tensor
            def _(pe):
                pe.wait_ge(s_k, 2)

                def transpose_in(t, k, loads):
                    pe.wait_ge(s_in[k], loads * 16)
                    reached(pe, s_xt, t)
                    pe.transpose(pX[:, 0:P], xin[k][:], ident[:]).then_inc(s_tx, 1)

                def turn(t, par, half, which):
                    if isinstance(t, int) and t == 0:
                        transpose_in(0, 0, 1)
                    if "next" in which:
                        transpose_in(t + 1, 1 - par, uses(par, half, 1))
                    if "before" in which:
                        e = pe.value_load(experts[0:1, bass.ds(t - 2, 1)], min_val=0, max_val=6)
                        pe.wait_ge(s_ht, t - 1)
                        reached(pe, s_oc, t - 2)
                        for c in range(HC):
                            ins = pe.matmul(pO[:, 0:D], hT[par][:, c, :],
                                            WD[:, bass.ds(e, 1), c, :].rearrange("p e n -> p (e n)"),
                                            start=(c == 0), stop=(c == HC - 1))
                        ins.then_inc(s_o, 1)
                    if "last" in which:
                        pe.wait_ge(s_h, t)
                        reached(pe, s_ht, t - 1)
                        for c in range(HC):
                            ins = pe.transpose(pH[:, c, :], h[1 - par][:, c, :], ident[:])
                        ins.then_inc(s_th, 1)
                    if "this" in which:
                        e = pe.value_load(experts[0:1, bass.ds(t, 1)], min_val=0, max_val=6)
                        pe.wait_ge(s_xt, t + 1)
                        reached(pe, s_h, t - 1)
                        pe.matmul(pG[par][:], xT[par][:], WG[:, bass.ds(e, 1), :].rearrange("p e n -> p (e n)"),
                                  start=True, stop=True).then_inc(s_g, 1)
                        pe.matmul(pU[par][:], xT[par][:], WU[:, bass.ds(e, 1), :].rearrange("p e n -> p (e n)"),
                                  start=True, stop=True).then_inc(s_u, 1)

                each_turn(pe, turn)

            @block.scalar
            def _(act):
                def copy_in(t, k):
                    act.wait_ge(s_tx, t + 1)
                    reached(act, s_u, t - 1)
                    act.activation(xT[k][:], pX[:, 0:P], ACT.Copy).then_inc(s_xt, 1)

                def turn(t, par, half, which):
                    if isinstance(t, int) and t == 0:
                        copy_in(0, 0)
                    if "next" in which:
                        copy_in(t + 1, 1 - par)
                    if "before" in which:
                        act.wait_ge(s_o, t - 1)
                        reached(act, s_ro[par], (uses(par, half, -2) - 1) * 16)
                        act.activation(ro[par][:], pO[:, 0:D], ACT.Copy).then_inc(s_oc, 1)
                    if "this" in which:
                        act.wait_ge(s_g, t + 1)
                        reached(act, s_h, t - 1)
                        act.activation(sg[par][:], pG[par][:], ACT.Silu).then_inc(s_sg, 1)

                each_turn(act, turn)

            @block.vector
            def _(dve):
                def turn(t, par, half, which):
                    if "last" in which:
                        dve.wait_ge(s_th, t)
                        reached(dve, s_o, t - 2)
                        dve.tensor_copy(hT[1 - par][:], pH[:]).then_inc(s_ht, 1)
                    if "this" in which:
                        dve.wait_ge(s_sg, t + 1)
                        dve.wait_ge(s_u, t + 1)
                        reached(dve, s_th, t - 1)
                        dve.tensor_tensor(h[par][:].rearrange("p c n -> p (c n)"), sg[par][:], pU[par][:],
                                          ALU.mult).then_inc(s_h, 1)

                each_turn(dve, turn)


def gather_and_finish(nc, X, slots, scale, RO, out):
    with ExitStack() as ctx:
        def sem(name):
            return ctx.enter_context(nc.semaphore("f_" + name))

        G = ctx.enter_context(nc.sbuf_tensor("f_gathered", [P, TILES, D], F32))
        s_a, s_out = sem("added"), sem("stored")
        s_g = [sem(f"gathered{i}") for i in range(TPB)]
        with nc.Block() as block:
            @block.gpsimd
            def _(gp):
                for i in range(TPB):
                    for n in range(i * NBATCH, i * NBATCH + NBATCH):
                        gp.indirect_dma_start(out=G[:, n, :], out_offset=None, in_=RO,
                                              in_offset=bass.IndirectOffsetOnAxis(ap=slots[:, n:n + 1], axis=0)) \
                          .then_inc(s_g[i], 16)

            @block.vector
            def _(dve):
                for i in range(TPB):
                    dve.wait_ge(s_g[i], NBATCH * 16)
                    for b in range(NBATCH):
                        n = i * NBATCH + b
                        ins = dve.scalar_tensor_tensor(out=X[:, TPB * b + i, :], in0=G[:, n, :],
                                                       scalar=scale[:, n:n + 1], in1=X[:, TPB * b + i, :],
                                                       op0=ALU.mult, op1=ALU.add)
                    ins.then_inc(s_a, 1)

            @block.sync
            def _(sp):
                with sp.Fori(0, TPB) as i:
                    sp.wait_ge(s_a, i + 1)
                    sp.dma_start(out[:, bass.ts(i, P), :].rearrange("b p d -> p b d"),
                                 X[:, :, :].rearrange("p (b i) d -> p i b d", b=NBATCH)[:, bass.ds(i, 1), :, :]
                                 .rearrange("p i b d -> p (i b) d")).then_inc(s_out, 16)
                sp.wait_ge(s_out, TPB * 16)


def build(nc, w, out):
    QD = nc.dram_tensor("q_stacks", [QUADS, 4, ROWS, SEQ], BF16, kind="Internal").ap()
    KD = nc.dram_tensor("k_stacks", [QUADS, 4, ROWS, SEQ], BF16, kind="Internal").ap()
    MD = nc.dram_tensor("neg_maxima", [96, P], BF16, kind="Internal").ap()
    ND = nc.dram_tensor("attended", [QUADS, 4, HD + 1, SEQ], F32, kind="Internal").ap()
    RD = nc.dram_tensor("inverse_dens", [NBATCH * HEADS, SEQ], F32, kind="Internal").ap()
    YS = nc.dram_tensor("sorted_in", [RTILES * P, D], F32, kind="Internal").ap()
    RO = nc.dram_tensor("sorted_out", [RTILES * P, D], F32, kind="Internal").ap()
    with ExitStack() as ctx:
        def sb(name, shape, dt=F32):
            return ctx.enter_context(nc.sbuf_tensor(name, shape, dt))

        X = sb("x", [P, TILES, D])
        with nc.sbuf_tensor("v_by_quads", [P, QUADS, TPB, 32], F32) as VS, ExitStack() as stacks:
            bufs = StackBuffers(nc, stacks)
            project_and_rotate(nc, X, VS, bufs, w["x"], w["cos"], w["sin"], w["qw"], w["qws"], w["kw"], w["kws"],
                               w["vw"], QD, KD)
            attend(nc, VS, bufs, QD, KD, MD, ND)
        WG, WU, WD = sb("WG", [P, NEXP, 512]), sb("WU", [P, NEXP, 512]), sb("WD", [P, NEXP, 4, D])
        Y4, L2 = sb("y4", [P, TILES, D]), sb("logits2", [P, TILES, NEXP])
        slots, scale = sb("slots", [P, TILES], I32), sb("scale", [P, TILES])
        experts = sb("experts", [1, RTILES], I32)
        shared_loaded = ctx.enter_context(nc.semaphore("shared_weights_loaded"))
        experts_loaded = ctx.enter_context(nc.semaphore("expert_weights_loaded"))
        w = {**w, "WG": WG, "WU": WU, "WD": WD}
        with nc.sbuf_tensor("y4T", [P, TILES, P], F32) as YT4:
            middle_layers(nc, X, Y4, YT4, L2, ND, RD, w, shared_loaded)
            order_tokens(nc, X, Y4, YT4, L2, slots, scale, experts, YS, w, shared_loaded, experts_loaded)
        routed_experts(nc, WG, WU, WD, experts, YS, RO)
        gather_and_finish(nc, X, slots, scale, RO, out)


def host_arrays(i):
    cos, sin = tables()
    swap = np.arange(D) ^ 1
    e = np.arange(8)
    sums, heads, spread = head_sums()
    return {
        "x": i["L0_attn_x"], "cos": cos, "sin": sin,
        "qw": i["L0_attn_qw"], "qws": i["L0_attn_qw"][:, swap],
        "kw": i["L0_attn_kw"], "kws": i["L0_attn_kw"][:, swap],
        "vw": i["L0_attn_vw"], "ow": i["L0_attn_ow"],
        "gate": i["L0_ffn_gate_w"], "Wu": i["L0_ffn_Wu"], "Wv": i["L0_ffn_Wv"], "Wo": i["L0_ffn_Wo"],
        "Win": i["L1_attn_in_proj_weight"].T, "bias": i["L1_attn_in_proj_bias"].reshape(3, D).T,
        "outw": i["L1_attn_out_w"].T, "outb": i["L1_attn_out_b"], "router": i["L1_ffn_router_w"],
        "up_w": i["L1_ffn_up_w"], "gate_w": i["L1_ffn_gate_w"], "down_w": i["L1_ffn_down_w"],
        "su": i["L1_ffn_shared_up_w"], "sg": i["L1_ffn_shared_gate_w"], "sd": i["L1_ffn_shared_down_w"],
        "sums": sums, "heads": heads, "spread": spread, "tri": (e[:, None] > e[None, :]).astype(np.float32).reshape(64),
        "down8": (8 - e).astype(np.float32), "tau": np.arange(RTILES, dtype=np.float32),
    }


def kernel(**inputs):
    import concourse.bacc as bacc
    from concourse.bass_utils import run_bass_kernel_spmd

    nc = bacc.Bacc("TRN2", target_bir_lowering=False, num_devices=1)
    arrays, args = {}, {}
    for name, a in host_arrays({k: np.asarray(v) for k, v in inputs.items()}).items():
        a = np.ascontiguousarray(a)
        arrays[f"in_{name}"] = a
        args[name] = nc.dram_tensor(f"in_{name}", a.shape, mybir.dt.from_np(a.dtype), kind="ExternalInput").ap()
    out = nc.dram_tensor("out", (NBATCH, SEQ, D), F32, kind="ExternalOutput").ap()
    build(nc, args, out)
    result = run_bass_kernel_spmd(nc, [arrays], core_ids=[0])
    return result.results[0]["out"]
```

```python
import numpy as np
import concourse.bass as bass
from concourse import mybir
from contextlib import ExitStack

F32 = mybir.dt.float32
BF16 = mybir.dt.bfloat16
I32 = mybir.dt.int32
U32 = mybir.dt.uint32
ALU = mybir.AluOpType
ACT = mybir.ActivationFunctionType
AX = mybir.AxisListType

P = 128
NBATCH, SEQ, D = 4, 1024, 128
TILES = NBATCH * SEQ // P
TPB = SEQ // P
HEADS, HD = 16, 8
QUADS = NBATCH * HEADS // 4
SLOTS = 6
ROWS = SLOTS * HD
EPS = 1e-5
Q_PART = [0, 1, 2, 0, 1, 0]
K_PART = [0, 0, 0, 1, 1, 2]
QSCALE = float(1.0 / np.sqrt(HD))
MASKED = -1.0e30

UNITS = [(h, i, c * 512, min(512, (i + 1) * P - c * 512))
         for h in range(4) for i in range(TPB) for c in range((i * P + P - 1) // 512 + 1)]
MBANKS = 3
NUNITS = len(UNITS) + MBANKS
LATE_T = 6
EARLY = 16
GROUPS = [(j, c) for j in range(TPB) for c in (0, 1) if j < 4 * (c + 1)]
NGROUPS = len(GROUPS)
SBANKS = 3
PBUFS = 4


def wait_apart(eng, sem, value, passed):
    eng.wait_ge(sem, value)
    eng.sem_inc(passed, 1)


def tables():
    inv = (np.float32(1.0) / np.power(np.float32(10000.0), np.arange(0, HD, 2, dtype=np.float32) / np.float32(HD))).astype(np.float32)
    freq = np.arange(SEQ, dtype=np.float32)[:, None] * inv[None, :]
    f = np.arange(D)
    ang = freq[:, (f % HD) // 2].T.astype(np.float64)
    sign = np.where(f % 2 == 0, -1.0, 1.0)[:, None]
    return np.cos(ang).astype(np.float32), (np.sin(ang) * sign).astype(np.float32)


class StackBuffers:

    def __init__(self, nc, ctx):
        def both(name, shape):
            return [ctx.enter_context(nc.sbuf_tensor(f"b_{name}{i}", shape, BF16)) for i in range(2)]

        self.Qz, self.Kz = both("Qz", [P, 4, SEQ]), both("Kz", [P, 4, SEQ])
        self.Qm, self.Km = both("Qm", [P, 2, SEQ]), both("Km", [P, 2, SEQ])
        self.ones = ctx.enter_context(nc.sbuf_tensor("b_ones", [3, SEQ], BF16))
        self.parts = [ctx.enter_context(nc.sbuf_tensor(f"a_parts{k}", [P, 3, NBATCH * SEQ], BF16)) for k in range(2)]
        self.s_store = ctx.enter_context(nc.semaphore("a_parts_stored"))
        self.s_ks = [ctx.enter_context(nc.semaphore(f"b_max_stacks_loaded{i}")) for i in range(2)]
        self.s_qs = [ctx.enter_context(nc.semaphore(f"b_exp_stacks_loaded{i}")) for i in range(2)]


def load_stacks(sp, zeroed, moving, src_z, src_m, u, par, s):
    for e in range(2):
        rows = slice(64 * e, 64 * e + ROWS)
        sp.dma_start(zeroed[par][rows, e::2, :], src_z[bass.ds(u, 1), e::2, :, :]
                     .rearrange("u h r t -> (u r) h t")).then_inc(s[par], 16)
        sp.dma_start(moving[par][rows, :, :], src_m[bass.ds(u, 1), e::2, :, :]
                     .rearrange("u h r t -> (u r) h t")).then_inc(s[par], 16)


def store_parts(sp, bufs, QD, KD, b, done):
    for k, (dst, order) in enumerate(((QD, Q_PART), (KD, K_PART))):
        for s, part in enumerate(order):
            sp.dma_start(dst[bass.ts(b, 4), :, s * HD:(s + 1) * HD, :].rearrange("g h d t -> (g h) d t"),
                         bufs.parts[k][:, part, bass.ts(b, SEQ)]).then_inc(done, 16)


def project_and_rotate(nc, X, VS, bufs, x, cos, sin, wq, wqs, wk, wks, wv, QD, KD):
    with ExitStack() as ctx:
        def sb(name, shape, dt=F32):
            return ctx.enter_context(nc.sbuf_tensor(name, shape, dt))

        def sem(name):
            return ctx.enter_context(nc.semaphore(name))

        def both(name, shape, dt=F32):
            return [sb(f"{name}{i}", shape, dt) for i in range(2)]

        HT = 4
        NH = 2 * NBATCH
        ident = sb("a_ident", [P, P])
        W = sb("a_w", [P, 5, D])
        tab = sb("a_tab", [P, 2, SEQ])
        half, eps = sb("a_minus_half", [P, HT]), sb("a_eps", [P, HT])
        stats, mv, rstd = both("a_stats", [P, HT, 6]), both("a_mean_var", [P, HT, 2]), both("a_rstd", [P, HT])
        Y, YT = both("a_y", [P, HT, D]), both("a_yT", [P, 512])
        rot = [both(f"a_rot_{'qk'[k]}", [P, 2, 512]) for k in range(2)]
        parts = bufs.parts
        pT = [ctx.enter_context(nc.psum_tensor(f"a_pT{i}", [P, HT, P], F32)) for i in range(2)]
        pQ = [ctx.enter_context(nc.psum_tensor(f"a_pQ{i}", [P, 512], F32)) for i in range(4)]
        pV = ctx.enter_context(nc.psum_tensor("a_pV", [P, HT, D], F32))

        s_x0, s_x, s_w, s_tab = sem("a_x0_loaded"), sem("a_x_loaded"), sem("a_w_loaded"), sem("a_tab_loaded")
        s_id, s_zero, s_ones = sem("a_const_steps"), sem("a_zeroed"), sem("a_ones_set")
        s_st, s_mv, s_rstd = sem("a_stats_done"), sem("a_mean_var_done"), sem("a_rstd_steps")
        s_y, s_t, s_yt = sem("a_y_done"), sem("a_transposed"), sem("a_yT_done")
        s_qk, s_v, s_vc = sem("a_projected"), sem("a_v_projected"), sem("a_v_copied")
        s_mul, s_sum, s_res = sem("a_terms_done"), sem("a_rotated"), [sem(f"a_residue_{n}_done") for n in "qk"]
        s_hi, s_mid = sem("a_hi_done"), sem("a_mid_done")
        s_part, s_store0, s_store = sem("a_parts_done"), sem("a_batch0_stored"), bufs.s_store
        s_pass = sem("a_passed")

        def span(n):
            return bass.ds(n * 512, 512)

        def each_half(eng, before, step):
            if before:
                before()
            step(0, 0, 2)
            step(1, 1, 2)
            with eng.Fori(1, NBATCH - 1) as b:
                step(b * 2, 0, 2)
                step(b * 2 + 1, 1, 2)
            step(NH - 2, 0, 1)
            step(NH - 1, 1, 0)

        with nc.Block() as block:
            @block.sync
            def _(sp):
                sp.dma_start(X[:, 0:TPB, :], x[0:1].rearrange("b (t p) d -> p (b t) d", p=P)).then_inc(s_x0, 16)
                sp.wait_ge(s_zero, 2)
                for par in range(2):
                    for e in range(2):
                        for h in range(2):
                            sp.dma_start(bufs.Kz[par][64 * e + ROWS:64 * e + ROWS + 3, e + 2 * h, :],
                                         bufs.ones[:, :]).then_inc(s_ones, 16)

                sp.wait_ge(s_part, 4)
                store_parts(sp, bufs, QD, KD, 0, s_store0)
                sp.wait_ge(s_store0, 2 * SLOTS * 16)
                load_stacks(sp, bufs.Qz, bufs.Km, QD, KD, 0, 0, bufs.s_ks)
                load_stacks(sp, bufs.Kz, bufs.Qm, KD, QD, 0, 0, bufs.s_qs)
                load_stacks(sp, bufs.Qz, bufs.Km, QD, KD, 1, 1, bufs.s_ks)
                with sp.Fori(1, NBATCH - 1) as b:
                    sp.wait_ge(s_part, b * 4 + 4)
                    store_parts(sp, bufs, QD, KD, b, s_store)
                sp.wait_ge(s_ones, 8 * 16)

            @block.gpsimd
            def _(gp):
                gp.memset(half[:], -0.5)
                gp.memset(eps[:], EPS).then_inc(s_id, 1)
                gp.memset(ident[:], 0.0).then_inc(s_id, 1)
                gp.wait_ge(s_id, 2)
                gp.affine_select(out=ident[:], in_=ident[:], compare_op=ALU.not_equal, fill=1.0, base=0,
                                 pattern=[[-1, P]], channel_multiplier=1).then_inc(s_id, 1)

                def power(n, par):
                    gp.wait_ge(s_mv, n + 1)
                    gp.tensor_tensor(rstd[par][:], mv[par][:, :, 1], eps[:], ALU.add).then_inc(s_rstd, 1)
                    gp.wait_ge(s_rstd, n * 2 + 1)
                    gp.tensor_tensor(rstd[par][:], rstd[par][:], half[:], ALU.pow).then_inc(s_rstd, 1)

                def step(n, par, ahead):
                    if ahead == 2:
                        power(n + 2, par)
                    gp.wait_ge(s_hi, n * 2 + 2)
                    gp.tensor_tensor(rot[1][par][:, 1, :], rot[1][par][:, 0, :], parts[1][:, 0, span(n)],
                                     ALU.subtract).then_inc(s_res[1], 1)
                    for k in range(2):
                        gp.wait_ge(s_mid, n * 2 + k + 1)
                        gp.tensor_tensor(parts[k][:, 2, span(n)], rot[k][par][:, 1, :], parts[k][:, 1, span(n)],
                                         ALU.subtract).then_inc(s_part, 1)

                def before():
                    gp.memset(bufs.Kz[0][:].bitcast(U32), 0)
                    gp.memset(bufs.Kz[1][:].bitcast(U32), 0)
                    power(0, 0)
                    power(1, 1)
                    gp.memset(bufs.Qz[0][:].bitcast(U32), 0)
                    gp.memset(bufs.Qz[1][:].bitcast(U32), 0)
                    gp.memset(bufs.ones[:], 1.0).then_inc(s_zero, 1)

                each_half(gp, before, step)

            @block.vector
            def _(dve):
                def moments(n, par):
                    for t in range(HT):
                        ins = dve.bn_stats(stats[par][:, t, :], X[:, n * HT + t, :])
                    ins.then_inc(s_st, 1)
                    wait_apart(dve, s_st, n + 1, s_pass)
                    for t in range(HT):
                        ins = dve.bn_aggr(mv[par][:, t, :], stats[par][:, t, :])
                    ins.then_inc(s_mv, 1)

                def normalize(n, par):
                    dve.wait_ge(s_rstd, n * 2 + 2)
                    dve.wait_ge(s_mv, n + 1)
                    if not (isinstance(n, int) and n < 2):
                        dve.wait_ge(s_t, n - 1)
                    for t in range(HT):
                        ins = dve.tensor_scalar(Y[par][:, t, :], X[:, n * HT + t, :], mv[par][:, t, 0:1],
                                                rstd[par][:, t:t + 1], ALU.subtract, ALU.mult)
                    ins.then_inc(s_y, 1)

                def before():
                    for t in (bufs.Qm[0], bufs.Qm[1], bufs.Km[0], bufs.Km[1]):
                        ins = dve.memset(t[:].bitcast(U32), 0)
                    ins.then_inc(s_zero, 1)
                    dve.wait_ge(s_x0, 16)
                    moments(0, 0)
                    moments(1, 1)
                    normalize(0, 0)
                    normalize(1, 1)
                    dve.wait_ge(s_tab, 32)

                def step(n, par, ahead):
                    cols = slice(par * 512, par * 512 + 512)
                    for k in range(2):
                        dve.wait_ge(s_qk, n * 2 + k + 1)
                        if not (isinstance(n, int) and n < 2):
                            dve.wait_ge(s_part, n * 2 + k - 3)
                        dve.tensor_tensor(rot[k][par][:, 0, :], pQ[2 * k][:], tab[:, 0, cols], ALU.mult)
                        dve.tensor_tensor(rot[k][par][:, 1, :], pQ[2 * k + 1][:], tab[:, 1, cols],
                                          ALU.mult).then_inc(s_mul, 1)
                    if ahead == 2:
                        if isinstance(n, int) and n == 0:
                            dve.wait_ge(s_x, 16)
                        moments(n + 2, par)
                    for k in range(2):
                        dve.wait_ge(s_mul, n * 2 + k + 1)
                        dve.tensor_tensor(rot[k][par][:, 0, :], rot[k][par][:, 0, :], rot[k][par][:, 1, :],
                                          ALU.add).then_inc(s_sum, 1)
                    dve.wait_ge(s_sum, n * 2 + 1)
                    dve.wait_ge(s_hi, n * 2 + 1)
                    dve.tensor_tensor(rot[0][par][:, 1, :], rot[0][par][:, 0, :], parts[0][:, 0, span(n)],
                                      ALU.subtract).then_inc(s_res[0], 1)
                    if ahead == 2:
                        normalize(n + 2, par)

                each_half(dve, before, step)

            @block.scalar
            def _(act):
                for k, w in enumerate((wq, wqs, wk, wks, wv)):
                    act.dma_start(W[:, k, :], w).then_inc(s_w, 16)
                act.dma_start(X[:, TPB:, :], x[1:].rearrange("b (t p) d -> p (b t) d", p=P)).then_inc(s_x, 16)
                act.dma_start(tab[:, 0, :], cos).then_inc(s_tab, 16)
                act.dma_start(tab[:, 1, :], sin).then_inc(s_tab, 16)

                def copy_y(n, par):
                    act.wait_ge(s_t, n + 1)
                    if not (isinstance(n, int) and n < 2):
                        act.wait_ge(s_v, n - 1)
                    act.activation(YT[par][:], pT[par][:].rearrange("p a b -> p (a b)"),
                                   ACT.Copy).then_inc(s_yt, 1)

                def step(n, par, ahead):
                    if ahead:
                        copy_y(n + 1, 1 - par)
                    for k in range(2):
                        act.wait_ge(s_sum, n * 2 + k + 1)
                        act.activation(parts[k][:, 0, span(n)], rot[k][par][:, 0, :], ACT.Copy).then_inc(s_hi, 1)
                    act.wait_ge(s_v, n + 1)
                    quads = slice(2 * (n - par), 2 * (n - par) + 4) if isinstance(n, int) else bass.ds(n * 2 - 2 * par, 4)
                    act.activation(VS[:, quads, HT * par:HT * par + HT, :],
                                   pV[:].rearrange("p j (g f) -> p g j f", g=4), ACT.Copy).then_inc(s_vc, 1)
                    for k in range(2):
                        act.wait_ge(s_res[k], n + 1)
                        act.activation(parts[k][:, 1, span(n)], rot[k][par][:, 1, :], ACT.Copy).then_inc(s_mid, 1)

                each_half(act, lambda: copy_y(0, 0), step)

            @block.tensor
            def _(pe):
                def transpose(n, par):
                    pe.wait_ge(s_y, n + 1)
                    if not (isinstance(n, int) and n < 2):
                        pe.wait_ge(s_yt, n - 1)
                    for t in range(HT):
                        ins = pe.transpose(pT[par][:, t, :], Y[par][:, t, :], ident[:])
                    ins.then_inc(s_t, 1)

                def before():
                    pe.wait_ge(s_id, 3)
                    transpose(0, 0)
                    pe.wait_ge(s_w, 16 * 5)

                def step(n, par, ahead):
                    for k in range(2):
                        if k == 0:
                            pe.wait_ge(s_yt, n + 1)
                        if not (isinstance(n, int) and n < 1):
                            pe.wait_ge(s_mul, n * 2 + k - 1)
                        pe.matmul(pQ[2 * k][:], W[:, 2 * k, :], YT[par][:], start=True, stop=True)
                        pe.matmul(pQ[2 * k + 1][:], W[:, 2 * k + 1, :], YT[par][:], start=True,
                                  stop=True).then_inc(s_qk, 1)
                    if ahead:
                        transpose(n + 1, 1 - par)
                    if not (isinstance(n, int) and n < 1):
                        pe.wait_ge(s_vc, n)
                    for t in range(HT):
                        ins = pe.matmul(pV[:, t, :], YT[par][:, t * P:t * P + P], W[:, 4, :], start=True, stop=True)
                    ins.then_inc(s_v, 1)

                each_half(pe, before, step)


def attend(nc, VS, bufs, load_next, QD, KD, MD, ND):
    with ExitStack() as ctx:
        def sb(name, shape, dt=F32):
            return ctx.enter_context(nc.sbuf_tensor(name, shape, dt))

        def sem(name):
            return ctx.enter_context(nc.semaphore(name))

        def both(name, shape, dt=F32):
            return [sb(f"{name}{i}", shape, dt) for i in range(2)]

        Qz, Kz, Qm, Km = bufs.Qz, bufs.Kz, bufs.Qm, bufs.Km
        Vq = both("b_Vq", [P, TPB, 4, 32])
        probs = [sb(f"b_probs{i}", [P, 4, 512]) for i in range(PBUFS)]
        raw = both("b_raw", [P, SEQ])
        identb = sb("b_ident", [P, P], BF16)
        maskb = sb("b_mask", [P, P], BF16)
        mx = both("b_mx", [P, 4, TPB, 2])
        res, left = sb("b_res", [P, 4, TPB]), sb("b_left", [P, 4, TPB])
        rest = left[:, :, :].rearrange("q (e p) i -> q e p i", e=2)
        zeros = sb("b_zeros", [P, 4, TPB])
        nm = both("b_negmax", [P, 2, 3, 2, TPB], BF16)
        MT = sb("b_negmaxT", [96, P], BF16)
        st = [ctx.enter_context(nc.psum_tensor(f"b_st{i}", [P, 512], F32)) for i in range(SBANKS)]
        acc = ctx.enter_context(nc.psum_tensor("b_acc", [P, SEQ], F32))
        mb = [ctx.enter_context(nc.psum_tensor(f"b_mb{i}", [P, 512], F32)) for i in range(MBANKS)]

        s_cst, s_ks, s_qs = sem("b_const_steps"), bufs.s_ks, bufs.s_qs
        s_mm, s_red, s_fin = sem("b_unit_made"), sem("b_unit_reduced"), sem("b_negmax_steps")
        s_mt, s_md, s_mrow = sem("b_negmaxT_copied"), sem("b_negmax_stored"), sem("b_negmax_loaded")
        s_st, s_exp, s_mask = sem("b_scores"), sem("b_exp_done"), sem("b_masked")
        s_pv, s_raw, s_nd = sem("b_pv_done"), sem("b_raw_done"), [sem(f"b_raw_stored{i}") for i in range(2)]
        s_mid = sem("b_mid_done")
        s_vq, s_vone = sem("b_v_ready"), sem("b_v_ones")
        s_pass = sem("b_passed")
        LOAD = 4 * 16
        NT = QUADS

        STEPS = 4 * NGROUPS

        def width(j, c):
            return 512 * (c + 1) - max(P * j, 512 * c)

        def number(n):
            return n if n < LATE_T else n + MBANKS

        def stream(first, second):
            out = [(first, n) for n in range(EARLY, len(UNITS))]
            if second:
                out += [(first + 1, n) for n in range(LATE_T)]
            out.append((first, "T"))
            if second:
                out += [(first + 1, n) for n in range(LATE_T, EARLY)]
            return out

        def spread(units, steps):
            cost = [(UNITS[n][3] if n != "T" else P) + 300 for _, n in units]
            lens = [2 * width(*GROUPS[k // 4]) for k in range(steps)]
            plan, spent, passed, at = [], 0, 0, 0
            for k in range(steps):
                passed += lens[k]
                now = []
                while at < len(units) and (spent + cost[at] / 2) * sum(lens) <= passed * sum(cost):
                    spent += cost[at]
                    now.append(units[at])
                    at += 1
                plan.append(now)
            plan[-1] += units[at:]
            return plan + [[] for _ in range(STEPS - steps)]

        VALUES_AT = 9
        EVACUATE_AT = 1
        EVACUATE0_AT = 9
        PROLOGUE = [(0, n) for n in range(EARLY)] + stream(0, True)
        FULL = spread(stream(1, True), STEPS)
        LAST = spread(stream(1, False)[:-1], 24)
        LAST[32].append((1, "T"))

        def unit_number(u, ahead, n, last):
            if n == "T":
                return (u + ahead + 1) * NUNITS + (0 if last else LATE_T)
            return (u + ahead) * NUNITS + number(n)

        def unit_bank(n, last):
            return mb[unit_number(0, 0, n, last) % MBANKS]

        def counts(u, ahead, n):
            if n == "T":
                return MBANKS
            return 1 + MBANKS if isinstance(u, int) and u + ahead == 0 and n == LATE_T - 1 else 1

        def each_quad(eng, prologue, body, epilogue):
            if prologue:
                prologue()
            body(0, 0, -1, FULL, False)
            body(1, 1, 0, FULL, False)
            body(2, 0, 0, FULL, False)
            with eng.Fori(1, 6) as v:
                body(v * 2 + 1, 1, v, FULL, False)
                body(v * 2 + 2, 0, v, FULL, False)
            body(13, 1, 6, FULL, False)
            body(14, 0, 6, LAST, True)
            body(15, 1, 7, [[]] * STEPS, True)
            if epilogue:
                epilogue()

        with nc.Block() as block:
            @block.sync
            def _(sp):
                def maxima(u, ahead, par, last):
                    sp.wait_ge(s_red, unit_number(u, ahead, "T", last) + 1)
                    sp.dma_start(MD[:, :], MT[:, :]).then_inc(s_md, 16)
                    sp.wait_ge(s_md, (u + ahead) * 16 + 16)
                    for e in range(2):
                        sp.dma_start(Qm[par][64 * e + ROWS:64 * e + ROWS + 3, :, :],
                                     MD[48 * e:48 * e + 48, :].rearrange("(c p i) q -> c p (i q)", c=3, p=2)) \
                          .then_inc(s_mrow, 16)

                def store_raw(u, par, ):
                    sp.wait_ge(s_raw, 2 * u + 2)
                    for h in range(4):
                        sp.dma_start(ND[bass.ds(u, 1), h, :, :].rearrange("u r t -> (u r) t"),
                                     raw[par][32 * h:32 * h + HD + 1, :]).then_inc(s_nd[par], 16)

                def prologue():
                    store_parts(sp, bufs, QD, KD, NBATCH - 1, bufs.s_store)
                    maxima(0, 0, 0, False)
                    load_next(sp)
                    sp.wait_ge(bufs.s_store, (NBATCH - 1) * 2 * SLOTS * 16)

                def body(u, par, v, plan, last):
                    static = isinstance(u, int)
                    if not (static and u + 1 >= NT):
                        if not (static and u == 0):
                            sp.wait_ge(s_exp, u * STEPS)
                        load_stacks(sp, Kz, Qm, KD, QD, u + 1, 1 - par, s_qs)
                    if not (static and u + 2 >= NT):
                        sp.wait_ge(s_red, (u + 1) * NUNITS)
                        load_stacks(sp, Qz, Km, QD, KD, u + 2, par, s_ks)
                    if not (static and u == 0):
                        store_raw(u - 1, 1 - par)
                    if not (static and u + 1 >= NT):
                        maxima(u, 1, 1 - par, last)

                def epilogue():
                    store_raw(NT - 1, (NT - 1) % 2)
                    for par in range(2):
                        sp.wait_ge(s_nd[par], NT // 2 * 64)

                each_quad(sp, prologue, body, epilogue)

            @block.vector
            def _(dve):
                def unit(u, ahead, n, par, last):
                    num = unit_number(u, ahead, n, last)
                    bank = unit_bank(n, last)
                    dve.wait_ge(s_mm, num + 1)
                    if n == "T":
                        q = u + ahead
                        if not (isinstance(q, int) and q == 0):
                            dve.wait_ge(s_md, q * 16)
                        dve.tensor_copy(MT[:, :], bank[0:96, 0:P // 2].bitcast(BF16)) \
                           .then_inc(s_red, counts(u, ahead, n))
                        return
                    h, i, k0, w = UNITS[n]
                    if n == 0 and not (isinstance(u, int) and u + ahead < 2):
                        dve.wait_ge(s_fin, (u + ahead - 1) * 5)
                    dve.tensor_reduce(mx[par][:, h, i, k0 // 512:k0 // 512 + 1], bank[:, 0:w], AX.X, ALU.max) \
                       .then_inc(s_red, counts(u, ahead, n))
                    if n == len(UNITS) - 1:
                        dve.wait_ge(s_red, num + 1)
                        dve.tensor_tensor(mx[par][:, :, 4:8, 0], mx[par][:, :, 4:8, 0], mx[par][:, :, 4:8, 1],
                                          ALU.max).then_inc(s_fin, 1)

                def prologue():
                    for ahead, n in PROLOGUE:
                        unit(0, ahead, n, ahead, False)

                def body(u, par, v, plan, last):
                    for units in plan:
                        for ahead, n in units:
                            unit(u, ahead, n, (par + ahead) % 2, last)

                each_quad(dve, prologue, body, None)

            @block.gpsimd
            def _(gp):
                gp.memset(zeros[:], 0.0)
                gp.memset(identb[:], 0.0)
                gp.memset(maskb[:], 0.0).then_inc(s_cst, 1)
                gp.wait_ge(s_cst, 1)
                gp.affine_select(out=identb[:], in_=identb[:], compare_op=ALU.not_equal, fill=1.0, base=0,
                                 pattern=[[-1, P]], channel_multiplier=1)
                gp.affine_select(out=maskb[:], in_=maskb[:], compare_op=ALU.is_ge, fill=MASKED, base=0,
                                 pattern=[[-1, P]], channel_multiplier=1).then_inc(s_cst, 1)
                for t in Vq:
                    gp.memset(t[:], 0.0).then_inc(s_vone, 1)
                gp.wait_ge(s_vone, 2)
                for t in Vq:
                    gp.memset(t[:, :, :, HD:2 * HD], 1.0).then_inc(s_vone, 1)

                def take_v(u, par):
                    gp.tensor_copy(Vq[par][:, :, :, 0:HD],
                                   VS[:, bass.ds(u, 1), :, :].rearrange("p u j (h f) -> p (u j) h f", h=4)) \
                      .then_inc(s_vq, 1)

                def split_maxima(u, ahead, par):
                    q = u + ahead
                    gp.wait_ge(s_fin, q * 5 + 1)
                    m = mx[par][:, :, :, 0].rearrange("q (p e) i -> q e p i", e=2)
                    r = res[:, :, :].rearrange("q (e p) i -> q e p i", e=2)
                    neg = nm[par]
                    for e in range(2):
                        ins = gp.tensor_tensor(r[:, e], zeros[:, 0:2, :], m[:, e], ALU.subtract)
                    ins.then_inc(s_fin, 1)
                    wait_apart(gp, s_fin, q * 5 + 2, s_pass)
                    if not (isinstance(q, int) and q < 2):
                        wait_apart(gp, s_mm, (q - 1) * NUNITS + LATE_T + 1, s_pass)
                    gp.tensor_copy(neg[:, :, 0, :, :], r).then_inc(s_fin, 1)
                    gp.wait_ge(s_fin, q * 5 + 3)
                    for e in range(2):
                        ins = gp.tensor_tensor(rest[:, e], r[:, e], neg[:, e, 0], ALU.subtract)
                    ins.then_inc(s_fin, 1)
                    wait_apart(gp, s_fin, q * 5 + 4, s_pass)
                    gp.tensor_copy(neg[:, :, 1, :, :], rest).then_inc(s_mid, 1)
                    gp.wait_ge(s_mid, q + 1)
                    for e in range(2):
                        ins = gp.tensor_tensor(neg[:, e, 2], rest[:, e], neg[:, e, 1], ALU.subtract)
                    ins.then_inc(s_fin, 1)

                def prologue():
                    gp.wait_ge(s_vone, 4)
                    take_v(0, 0)
                    split_maxima(0, 0, 0)

                def body(u, par, v, plan, last):
                    static = isinstance(u, int)
                    for g, (j, c) in enumerate(GROUPS):
                        for ahead, n in sum(plan[4 * g:4 * g + 4], []):
                            if n == len(UNITS) - 1:
                                split_maxima(u, ahead, (par + ahead) % 2)
                        if c != j // 4:
                            continue
                        wait_apart(gp, s_exp, u * STEPS + 4 * g + 4, s_pass)
                        diag = probs[g % PBUFS][:, :, P * j - 512 * c:P * j - 512 * c + P]
                        gp.affine_select(out=diag, in_=diag, compare_op=ALU.is_ge, fill=0.0, base=0,
                                         pattern=[[0, 4], [1, P]], channel_multiplier=-1).then_inc(s_mask, 1)
                        if j == 1 and not (static and u + 1 >= NT):
                            if not (static and u == 0):
                                wait_apart(gp, s_pv, u * NGROUPS, s_pass)
                            take_v(u + 1, 1 - par)

                each_quad(gp, prologue, body, None)

            @block.scalar
            def _(act):
                def evacuate(u, par, v, c):
                    act.wait_ge(s_pv, u * NGROUPS + (NGROUPS if c else GROUPS.index((3, 0)) + 1))
                    if c == 0 and not (isinstance(u, int) and u < 2):
                        act.wait_ge(s_nd[par], v * 64)
                    act.activation(raw[par][:, 512 * c:512 * c + 512], acc[:, 512 * c:512 * c + 512],
                                   ACT.Copy).then_inc(s_raw, 1)

                def body(u, par, v, plan, last):
                    static = isinstance(u, int)
                    for g, (j, c) in enumerate(GROUPS):
                        for h in range(4):
                            k = 4 * g + h
                            a = 512 - width(j, c)
                            act.wait_ge(s_st, u * STEPS + k + 1)
                            if h == 0 and not (static and u == 0 and g < PBUFS):
                                act.wait_ge(s_pv, u * NGROUPS + g - PBUFS + 1)
                            act.activation(probs[g % PBUFS][:, h, a:512], st[k % SBANKS][:, a:512], ACT.Exp,
                                           scale=QSCALE).then_inc(s_exp, 1)
                        if g == EVACUATE_AT and not (static and u == 0):
                            evacuate(u - 1, 1 - par, None, 1)
                        if g == EVACUATE0_AT:
                            evacuate(u, par, u // 2 if static else v + 1 - par, 0)

                each_quad(act, None, body, lambda: evacuate(NT - 1, 1, None, 1))

            @block.tensor
            def _(pe):
                def unit(u, ahead, n, par, last):
                    num = unit_number(u, ahead, n, last)
                    bank = unit_bank(n, last)
                    if not (isinstance(num, int) and num < MBANKS):
                        pe.wait_ge(s_red, num - MBANKS + 1)
                    if n == "T":
                        pe.wait_ge(s_fin, (u + ahead) * 5 + 5)
                        pe.transpose(bank[0:96, 0:P // 2].bitcast(BF16),
                                     nm[par][:, :, :, :, :].rearrange("q e c p i -> q (e c p i)"),
                                     identb[:]).then_inc(s_mm, counts(u, ahead, n))
                        return
                    h, i, k0, w = UNITS[n]
                    if n == 0:
                        pe.wait_ge(s_ks[par], half_index[0](u, ahead) * LOAD + LOAD)
                    diagonal = k0 + w == (i + 1) * P
                    ins = pe.matmul(bank[:, 0:w], Qz[par][:, h, P * i:P * i + P], Km[par][:, h // 2, k0:k0 + w],
                                    start=True, stop=not diagonal)
                    if diagonal:
                        ins = pe.matmul(bank[:, w - P:w], identb[:], maskb[:], start=False, stop=True)
                    ins.then_inc(s_mm, counts(u, ahead, n))

                half_index = [None]

                def scores(u, par, k):
                    g, h = k // 4, k % 4
                    j, c = GROUPS[g]
                    if k == 0:
                        pe.wait_ge(s_qs[par], half_index[0](u, 0) * LOAD + LOAD)
                        pe.wait_ge(s_mrow, u * 32 + 32)
                    if not (isinstance(u, int) and u == 0 and k < SBANKS):
                        pe.wait_ge(s_exp, u * STEPS + k - SBANKS + 1)
                    a = 512 - width(j, c)
                    pe.matmul(st[k % SBANKS][:, a:512], Kz[par][:, h, P * j:P * j + P],
                              Qm[par][:, h // 2, 512 * c + a:512 * c + 512], start=True, stop=True).then_inc(s_st, 1)

                def values(u, par, g):
                    j, c = GROUPS[g]
                    if c == j // 4:
                        pe.wait_ge(s_mask, u * TPB + j + 1)
                    else:
                        pe.wait_ge(s_exp, u * STEPS + 4 * g + 4)
                    if g == 0:
                        pe.wait_ge(s_vq, u + 1)
                    if j == 0 and not (isinstance(u, int) and u == 0):
                        pe.wait_ge(s_raw, 2 * u - 1 + c)
                    a = 512 - width(j, c)
                    for h in range(4):
                        ins = pe.matmul(acc[32 * h:32 * h + 32, 512 * c + a:512 * c + 512], Vq[par][:, j, h, :],
                                        probs[g % PBUFS][:, h, a:512], start=(j == 0), stop=(j == 4 * c + 3))
                    ins.then_inc(s_pv, 1)

                def prologue():
                    pe.wait_ge(s_cst, 2)
                    half_index[0] = lambda u, ahead: (u + ahead) // 2
                    for ahead, n in PROLOGUE:
                        unit(0, ahead, n, ahead, False)

                def body(u, par, v, plan, last):
                    static = isinstance(u, int)
                    half_index[0] = (lambda u_, ahead: (u_ + ahead) // 2) if static else \
                        (lambda u_, ahead: v + ((1 if par else 2) + ahead) // 2)
                    for k in range(STEPS):
                        scores(u, par, k)
                        for ahead, n in plan[k]:
                            unit(u, ahead, n, (par + ahead) % 2, last)
                        if k >= VALUES_AT and (k - VALUES_AT) % 4 == 0:
                            values(u, par, (k - VALUES_AT) // 4)
                        elif k < VALUES_AT and (k - VALUES_AT) % 4 == 0 and not (static and u == 0):
                            values(u - 1, 1 - par, NGROUPS + (k - VALUES_AT) // 4)

                def epilogue():
                    for g in range((STEPS - 1 - VALUES_AT) // 4 + 1, NGROUPS):
                        values(NT - 1, 1, g)

                each_quad(pe, prologue, body, epilogue)


def head_sums():
    f = np.arange(D) // HD
    cosines = np.cos(np.pi / 2 * np.arange(NBATCH) / NBATCH)[:, None, None]
    same = (f[:, None] == f[None, :])[None] * cosines
    heads = (f[:, None] == (np.arange(32) % HEADS)[None, :])[None] * cosines
    spread = np.zeros((NBATCH, P, D))
    for n in range(NBATCH):
        spread[n, 32 * n + f, np.arange(D)] = 1.0
    return same.astype(np.float32), heads.astype(np.float32), spread.astype(np.float32)


class MiddleWeights:
    EXP, R = 8, 32

    def __init__(self, nc, ctx):
        def sb(name, shape):
            return ctx.enter_context(nc.sbuf_tensor("c_" + name, shape, F32))

        self.ow, self.gate, self.Wuv = sb("ow", [P, D]), sb("gate", [P, self.EXP]), sb("Wuv", [P, 2, self.EXP, self.R])
        self.Wo, self.Win, self.outw = sb("Wo", [P, 2, D]), sb("Win", [P, 3, D]), sb("outw", [P, D])
        self.bias, self.outb, self.router = sb("bias", [P, 3]), sb("outb", [P, D]), sb("router", [P, 8])
        self.sums, self.heads = sb("sums", [P, NBATCH, D]), sb("heads", [P, NBATCH, 32])
        self.spread, self.tri = sb("spread", [P, NBATCH, D]), sb("tri", [P, self.EXP, self.EXP])
        self.loaded = ctx.enter_context(nc.semaphore("c_weights_loaded"))
        self.count = 14 * 16

    def load(self, queue, w):
        for dst, src in ((self.ow[:], w["ow"]), (self.gate[:], w["gate"]),
                         (self.Wuv[:, 0], w["Wu"].rearrange("e d r -> d e r")),
                         (self.Wuv[:, 1], w["Wv"].rearrange("e d r -> d e r")),
                         (self.Wo[:], w["Wo"].rearrange("(c e) r d -> (e r) c d", c=2)),
                         (self.Win[:], w["Win"].rearrange("d (c n) -> d c n", c=3)), (self.outw[:], w["outw"]),
                         (self.bias[:], w["bias"]), (self.outb[:], w["outb"].partition_broadcast(P)),
                         (self.router[:], w["router"]), (self.sums[:], w["sums"].rearrange("n f g -> f n g")),
                         (self.heads[:], w["heads"].rearrange("n f g -> f n g")),
                         (self.spread[:], w["spread"].rearrange("n f g -> f n g")),
                         (self.tri[:].rearrange("p e f -> p (e f)"), w["tri"].partition_broadcast(P))):
            queue.dma_start(dst, src).then_inc(self.loaded, 16)


def reached(eng, sem, value, total=None):
    if isinstance(value, int):
        value = value if total is None else min(value, total)
        if value <= 0:
            return
    eng.wait_ge(sem, value)


def middle_layers(nc, X, Y4, YT4, L2, ND, RD, mw, w, shared_loaded):
    with ExitStack() as ctx:
        def sb(name, shape, dt=F32):
            return ctx.enter_context(nc.sbuf_tensor("c_" + name, shape, dt))

        def sem(name):
            return ctx.enter_context(nc.semaphore("c_" + name))

        def bank(name):
            return ctx.enter_context(nc.psum_tensor("c_" + name, [P, 4, P], F32))

        B = NBATCH
        EXP, R = mw.EXP, mw.R
        CH = TPB
        ow, gate, Wuv, Wo, Win, outw = mw.ow, mw.gate, mw.Wuv, mw.Wo, mw.Win, mw.outw
        bias, outb, router, sums, heads, spread, tri = (mw.bias, mw.outb, mw.router, mw.sums, mw.heads,
                                                        mw.spread, mw.tri)
        ident, half, eps = sb("ident", [P, P]), sb("half", [P, B]), sb("eps", [P, B])
        dens = sb("dens", [P, 512])
        num, den, attT = sb("num", [P, B, P]), sb("den", [P, B, P]), sb("attT", [P, B, P])
        LN = [(sb(f"stats{k}", [P, B, 6]), sb(f"mv{k}", [P, B, 2]), sb(f"rs{k}", [P, B])) for k in range(3)]
        y, yT = sb("y", [P, B, D]), sb("yT", [P, B, P])
        lg, rank = sb("lg", [P, B, EXP]), sb("rank", [P, B, EXP])
        cmp, eq = sb("cmp", [P, B, EXP, EXP]), sb("eq", [P, B, EXP, EXP])
        hs, th, wt = sb("hs", [P, B]), sb("th", [P, B, EXP]), sb("wt", [P, B, EXP])
        su = [sb(f"su{i}", [P, EXP, R]) for i in range(2)]
        sv = [sb(f"sv{i}", [P, EXP, R]) for i in range(2)]
        sw = [sb(f"sw{i}", [P, 2, P]) for i in range(2)]
        swT = sb("swT", [P, B, 2, P])
        z, zT, xb = sb("z", [P, B, D]), sb("zT", [P, B, P]), sb("xb", [P, B, D])
        qkv = sb("qkv", [P, 3, B, P])
        prod = [sb(f"prod{i}", [P, B, P]) for i in range(2)]
        av = [sb(f"av{i}", [P, B, P]) for i in range(2)]
        nsum, dn, at = sb("nsum", [P, B, P]), sb("dn", [P, P]), sb("at", [P, B, P])
        z4, yT4 = sb("z4", [P, B, D]), sb("yT4", [P, B, P])
        O, S, Ta, Tb = bank("O"), bank("S"), bank("Ta"), bank("Tb")
        UV, A = [bank("UV0"), bank("UV1")], [bank("A0"), bank("A1")]
        S_LG1, S_LG2, S_DN = S[:, 0, 0:B * EXP], S[:, 1, 0:B * 8], S[:, 2, :]

        s_w, s_cst, s_dn0, s_dr = mw.loaded, sem("const_steps"), sem("dens_loaded"), sem("dens_inverted")
        s_den0 = sem("den0_loaded")
        s_rd, s_nd, s_att = sem("dens_stored"), sem("attended_loaded"), sem("attT_done")
        s_p1, s_p3, s_wo, s_ex = sem("att1_projected"), sem("att2_projected"), sem("mixture_out_made"), sem("den_spread")
        s_r1, s_r2, s_r3 = sem("residual1_done"), sem("residual2_done"), sem("residual3_done")
        s_st, s_mv, s_pw, s_nm = [[sem(f"{n}{k}") for k in range(3)] for n in ("stats_done", "meanvar_done",
                                                                             "pow_steps", "normalized")]
        s_t1, s_t2, s_t3, s_tw = sem("y_transposed"), sem("z_transposed"), sem("z4_transposed"), sem("sw_transposed")
        s_yt, s_zt, s_y4t, s_swt = sem("yT_copied"), sem("zT_copied"), sem("yT4_copied"), sem("swT_copied")
        s_kept = sem("y4_kept")
        s_l1, s_l2, s_lg, s_lg2 = sem("logits1_made"), sem("logits2_made"), sem("logits1_copied"), sem("logits2_copied")
        s_uv, s_rt, s_th, s_tt, s_wt = sem("uv_made"), sem("route_steps"), sem("halves_done"), sem("tanh_done"), sem("weights_done")
        s_su, s_sv, s_sw = sem("silu_u"), sem("gated"), sem("weighted")
        s_xb, s_pj, s_qk = sem("xb_done"), sem("qkv_made"), sem("qkv_copied")
        s_pr = [sem(f"prod{i}_done") for i in range(2)]
        s_a, s_dp, s_av, s_ns = sem("A_made"), sem("den_added"), sem("Av_done"), sem("num_steps")
        s_mx, s_rc, s_at = sem("den_clipped"), sem("den_inverted"), sem("at_done")
        s_pass = sem("passed")

        def xs(c):
            return X[:, :, :].rearrange("p (b i) d -> p i b d", b=B)[:, bass.ds(c, 1), :, :] \
                .rearrange("p i b d -> p (i b) d")

        def flat(t):
            return t[:].rearrange("p a b -> p (a b)")

        def each_turn(eng, turn):
            def at_turn(i):
                chunks = [n if 0 <= n < CH else None for n in (i + 2, i + 1, i, i - 1)]
                turn(*chunks)

            for i in range(-2, 2):
                at_turn(i)
            with eng.Fori(2, CH - 2) as i:
                turn(i + 2, i + 1, i, i - 1)
            for i in range(CH - 2, CH + 1):
                at_turn(i)

        def load_num(queue, c):
            for b in range(B):
                queue.dma_start(num[:, b, :], ND[4 * b:4 * b + 4, :, 0:HD, bass.ts(c, P)]
                                .rearrange("g h r q -> (g h) r q")).then_inc(s_nd, 16)

        with nc.Block() as block:
            @block.sync
            def _(sp):
                def load_den(c, src, loaded):
                    for b in range(B):
                        sp.dma_start(den[:, b, :], src[HEADS * b:HEADS * b + HEADS, bass.ts(c, P)]
                                     .unsqueeze(1).broadcast_to([HEADS, HD, P])).then_inc(loaded, 16)

                sums_of_exp = ND.rearrange("u h r t -> (u h) r t")[:, HD, :]
                load_den(0, sums_of_exp, s_den0)
                for e in range(2):
                    sp.dma_start(dens[64 * e:64 * e + 64, :],
                                 sums_of_exp[:, 512 * e:512 * e + 512]).then_inc(s_dn0, 16)
                sp.wait_ge(s_dr, 2)
                for e in range(2):
                    sp.dma_start(RD[:, 512 * e:512 * e + 512], dens[64 * e:64 * e + 64, :]).then_inc(s_rd, 16)
                sp.wait_ge(s_rd, 32)
                with sp.Fori(1, CH) as c:
                    sp.wait_ge(s_att, c)
                    load_num(sp, c)
                    load_den(c, RD, s_nd)

            @block.gpsimd
            def _(gp):
                gp.memset(half[:], -0.5)
                gp.memset(eps[:], EPS).then_inc(s_cst, 1)
                gp.memset(ident[:], 0.0).then_inc(s_cst, 1)
                gp.wait_ge(s_cst, 2)
                gp.affine_select(out=ident[:], in_=ident[:], compare_op=ALU.not_equal, fill=1.0, base=0,
                                 pattern=[[-1, P]], channel_multiplier=1).then_inc(s_cst, 1)
                gp.wait_ge(s_w, mw.count)

                def power(c, k):
                    _, mv, rs = LN[k]
                    gp.wait_ge(s_mv[k], c + 1)
                    gp.tensor_tensor(rs[:], mv[:, :, 1], eps[:], ALU.add).then_inc(s_pw[k], 1)
                    gp.wait_ge(s_pw[k], c * 2 + 1)
                    gp.tensor_tensor(rs[:], rs[:], half[:], ALU.pow).then_inc(s_pw[k], 1)

                def divide1(c):
                    gp.wait_ge(s_nd, c * 128 + 64)
                    if isinstance(c, int) and c == 0:
                        gp.wait_ge(s_dr, 1)
                    reached(gp, s_p1, c)
                    gp.tensor_tensor(attT[:], num[:], den[:], ALU.mult).then_inc(s_att, 1)

                def product(c, l):
                    if l == 1:
                        gp.wait_ge(s_qk, c * 3 + 2)
                    reached(gp, s_dp, c * 4 + l - 1)
                    gp.tensor_tensor(prod[1][:], qkv[:, 1, :, :], qkv[:, 0, l, :].unsqueeze(1).broadcast_to([P, B, P]),
                                     ALU.mult).then_inc(s_pr[1], 1)

                def weigh(c, b):
                    gp.wait_ge(s_sv, c * 4 + b + 1)
                    if b == 0:
                        gp.wait_ge(s_wt, c + 1)
                    reached(gp, s_tw, c * 2 + b // 2)
                    gp.tensor_tensor(sw[b % 2][:].rearrange("p c (e r) -> p (c e) r", r=R), sv[b % 2][:],
                                     wt[:, b, :].unsqueeze(2).broadcast_to([P, EXP, R]),
                                     ALU.mult).then_inc(s_sw, 1)

                def add_bias(c):
                    gp.wait_ge(s_r2, c + 1)
                    reached(gp, s_r3, c)
                    gp.tensor_tensor(xb[:], xs(c), outb[:].unsqueeze(1).broadcast_to([P, B, D]),
                                     ALU.add).then_inc(s_xb, 1)

                def sum_up(c, l):
                    gp.wait_ge(s_av, c * 4 + l + 1)
                    if l == 0:
                        reached(gp, s_at, c)
                    t = av[l % 2]
                    gp.tensor_tensor(t[:, 0:2, :], t[:, 0:2, :], t[:, 2:4, :], ALU.add).then_inc(s_ns, 1)
                    gp.wait_ge(s_ns, c * 8 + 2 * l + 1)
                    gp.tensor_tensor(nsum[:, l, :], t[:, 0, :], t[:, 1, :], ALU.add).then_inc(s_ns, 1)

                def turn(a, b, c, d):
                    if a is not None:
                        divide1(a)
                    if c is not None:
                        power(c, 1)
                        add_bias(c)
                    if d is not None:
                        power(d, 2)
                    if b is not None:
                        weigh(b, 0)
                    if c is not None:
                        product(c, 1)
                    if b is not None:
                        weigh(b, 1)
                    if c is not None:
                        sum_up(c, 0)
                        product(c, 3)
                    if b is not None:
                        weigh(b, 2)
                        weigh(b, 3)
                    if c is not None:
                        sum_up(c, 1)
                    if a is not None:
                        power(a, 0)
                    if c is not None:
                        sum_up(c, 2)
                        sum_up(c, 3)

                each_turn(gp, turn)

            @block.vector
            def _(dve):
                def xtile(c):
                    return lambda b: X[:, TPB * b + c, :]

                def moments(c, k):
                    stats, mv, _ = LN[k]
                    src = xtile(c)
                    wait_apart(dve, (s_r1, s_r2, s_r3)[k], c + 1, s_pass)
                    for b in range(B):
                        ins = dve.bn_stats(stats[:, b, :], src(b))
                    ins.then_inc(s_st[k], 1)
                    wait_apart(dve, s_st[k], c + 1, s_pass)
                    for b in range(B):
                        ins = dve.bn_aggr(mv[:, b, :], stats[:, b, :])
                    ins.then_inc(s_mv[k], 1)

                def normalize(c, k):
                    _, mv, rs = LN[k]
                    src, dst = xtile(c), (y, z, z4)[k]
                    dve.wait_ge(s_mv[k], c + 1)
                    dve.wait_ge(s_pw[k], c * 2 + 2)
                    reached(dve, (s_t1, s_t2, s_t3)[k], c)
                    if k == 2:
                        reached(dve, s_kept, c)
                    for b in range(B):
                        ins = dve.tensor_scalar(dst[:, b, :], src(b), mv[:, b, 0:1], rs[:, b:b + 1],
                                                ALU.subtract, ALU.mult)
                    ins.then_inc(s_nm[k], 1)

                def residual1(c):
                    dve.wait_ge(s_p1, c + 1)
                    dve.tensor_tensor(xs(c), xs(c), O[:], ALU.add).then_inc(s_r1, 1)

                mine = lg[:].unsqueeze(3).broadcast_to([P, B, EXP, EXP])
                other = lg[:].unsqueeze(2).broadcast_to([P, B, EXP, EXP])

                def compare(c):
                    dve.wait_ge(s_l1, c + 1)
                    dve.tensor_copy(lg[:], S_LG1.rearrange("p (b e) -> p b e", b=B)).then_inc(s_lg, 1)
                    dve.wait_ge(s_lg, c + 1)
                    n = c * 7
                    dve.tensor_tensor(cmp[:], other, mine, ALU.is_gt)
                    dve.tensor_tensor(eq[:], other, mine, ALU.is_equal).then_inc(s_rt, 1)
                    dve.wait_ge(s_rt, n + 1)
                    dve.tensor_tensor(eq[:], eq[:], tri[:].unsqueeze(1).broadcast_to([P, B, EXP, EXP]),
                                      ALU.mult).then_inc(s_rt, 1)
                    dve.wait_ge(s_rt, n + 2)
                    dve.tensor_tensor(cmp[:], cmp[:], eq[:], ALU.add).then_inc(s_rt, 1)

                def choose(c):
                    n = c * 7
                    dve.wait_ge(s_rt, n + 3)
                    dve.tensor_reduce(rank[:], cmp[:], AX.X, ALU.add).then_inc(s_rt, 1)
                    dve.wait_ge(s_rt, n + 4)
                    dve.tensor_scalar(rank[:], rank[:], 2.0, 0.5, ALU.is_lt, ALU.mult).then_inc(s_rt, 1)
                    dve.wait_ge(s_rt, n + 5)
                    dve.tensor_tensor(th[:], rank[:], lg[:], ALU.mult).then_inc(s_rt, 1)
                    dve.wait_ge(s_rt, n + 6)
                    dve.tensor_reduce(hs[:], th[:], AX.X, ALU.add).then_inc(s_rt, 1)
                    dve.wait_ge(s_rt, n + 7)
                    dve.tensor_tensor(th[:], lg[:], hs[:].unsqueeze(2).broadcast_to([P, B, EXP]),
                                      ALU.subtract).then_inc(s_th, 1)

                def weights(c):
                    dve.wait_ge(s_tt, c + 1)
                    reached(dve, s_sw, c * 4)
                    dve.scalar_tensor_tensor(out=wt[:].rearrange("p b e -> p (b e)"),
                                             in0=th[:].rearrange("p b e -> p (b e)"), scalar=1.0,
                                             in1=rank[:].rearrange("p b e -> p (b e)"),
                                             op0=ALU.add, op1=ALU.mult).then_inc(s_wt, 1)

                def gated(c, b):
                    dve.wait_ge(s_su, c * 4 + b + 1)
                    reached(dve, s_sw, c * 4 + b - 1)
                    dve.tensor_tensor(sv[b % 2][:].rearrange("p e r -> p (e r)"),
                                      su[b % 2][:].rearrange("p e r -> p (e r)"),
                                      flat(UV[b % 2])[:, EXP * R:], ALU.mult).then_inc(s_sv, 1)

                def residual2(c):
                    dve.wait_ge(s_wo, c + 1)
                    dve.tensor_tensor(xs(c), xs(c), O[:], ALU.add).then_inc(s_r2, 1)

                def product(c, l):
                    if l == 0:
                        dve.wait_ge(s_qk, c * 3 + 2)
                    reached(dve, s_dp, c * 4 + l - 1)
                    dve.tensor_tensor(prod[0][:], qkv[:, 1, :, :],
                                      qkv[:, 0, l, :].unsqueeze(1).broadcast_to([P, B, P]),
                                      ALU.mult).then_inc(s_pr[0], 1)

                def weigh_values(c, l):
                    dve.wait_ge(s_a, c * 4 + l + 1)
                    if l == 0:
                        dve.wait_ge(s_qk, c * 3 + 3)
                    reached(dve, s_ns, c * 8 + 2 * l - 2)
                    dve.tensor_tensor(av[l % 2][:], A[(l + 1) % 2][:], qkv[:, 2, :, :], ALU.mult).then_inc(s_av, 1)

                def invert(c):
                    dve.wait_ge(s_dp, c * 4 + 4)
                    reached(dve, s_ex, c)
                    dve.tensor_scalar(dn[:], S_DN, 1e-3, None, ALU.max).then_inc(s_mx, 1)
                    dve.wait_ge(s_mx, c + 1)
                    dve.reciprocal(dn[:], dn[:]).then_inc(s_rc, 1)

                def divide2(c):
                    dve.wait_ge(s_ex, c + 1)
                    dve.wait_ge(s_ns, c * 8 + 8)
                    reached(dve, s_p3, c)
                    dve.tensor_tensor(at[:], nsum[:], Tb[:], ALU.mult).then_inc(s_at, 1)

                def residual3(c):
                    dve.wait_ge(s_p3, c + 1)
                    dve.wait_ge(s_xb, c + 1)
                    dve.tensor_tensor(xs(c), xb[:], O[:], ALU.add).then_inc(s_r3, 1)

                def keep_logits(c):
                    dve.wait_ge(s_l2, c + 1)
                    dve.tensor_copy(L2[:, bass.ts(c, B), :], S_LG2.rearrange("p (b e) -> p b e", b=B)) \
                       .then_inc(s_lg2, 1)

                dve.wait_ge(s_den0, B * 16)
                dve.reciprocal(den[:], den[:]).then_inc(s_dr, 1)
                dve.wait_ge(s_dn0, 32)
                dve.reciprocal(dens[:], dens[:]).then_inc(s_dr, 1)
                dve.wait_ge(s_w, mw.count)

                def turn(a, b, c, d):
                    if c is not None:
                        moments(c, 1)
                    if b is not None:
                        compare(b)
                    if c is not None:
                        normalize(c, 1)
                    if d is not None:
                        residual3(d)
                        moments(d, 2)
                    if b is not None:
                        choose(b)
                    if d is not None:
                        normalize(d, 2)
                    if b is not None:
                        weights(b)
                        gated(b, 0)
                    if c is not None:
                        product(c, 0)
                    if b is not None:
                        gated(b, 1)
                    if a is not None:
                        residual1(a)
                    if b is not None:
                        gated(b, 2)
                    if c is not None:
                        weigh_values(c, 0)
                    if d is not None:
                        keep_logits(d)
                    if c is not None:
                        weigh_values(c, 1)
                        product(c, 2)
                    if b is not None:
                        gated(b, 3)
                    if a is not None:
                        moments(a, 0)
                    if c is not None:
                        weigh_values(c, 2)
                        weigh_values(c, 3)
                        invert(c)
                    if a is not None:
                        normalize(a, 0)
                    if b is not None:
                        residual2(b)
                    if c is not None:
                        divide2(c)

                each_turn(dve, turn)

            @block.scalar
            def _(act):
                load_num(act, 0)
                act.wait_ge(s_w, mw.count)

                def copy_y(c):
                    act.wait_ge(s_t1, c + 1)
                    reached(act, s_uv, c * 4)
                    act.activation(yT[:], Ta[:], ACT.Copy).then_inc(s_yt, 1)

                def silu_u(c, b):
                    act.wait_ge(s_uv, c * 4 + b + 1)
                    reached(act, s_sv, c * 4 + b - 1)
                    act.activation(su[b % 2][:].rearrange("p e r -> p (e r)"), flat(UV[b % 2])[:, 0:EXP * R],
                                   ACT.Silu).then_inc(s_su, 1)

                def tanh(c):
                    act.wait_ge(s_th, c + 1)
                    act.activation(th[:], th[:], ACT.Tanh).then_inc(s_tt, 1)

                def copy_hidden(c, n):
                    act.wait_ge(s_tw, c * 2 + n + 1)
                    if n == 0:
                        reached(act, s_wo, c)
                    act.activation(swT[:, 2 * n:2 * n + 2, :, :].rearrange("p a b q -> p (a b) q"),
                                   (Tb if n == 0 else Ta)[:], ACT.Copy).then_inc(s_swt, 1)

                def copy_z(c):
                    act.wait_ge(s_t2, c + 1)
                    reached(act, s_pj, c * 3)
                    act.activation(zT[:], Tb[:], ACT.Copy).then_inc(s_zt, 1)

                def copy_qkv(c, n):
                    act.wait_ge(s_pj, c * 3 + n + 1)
                    if n == 0:
                        for s_prod in s_pr:
                            reached(act, s_prod, c * 2)
                    if n == 2:
                        reached(act, s_av, c * 4)
                    act.activation(qkv[:, n, :, :], A[n % 2][:], ACT.Relu if n < 2 else ACT.Identity,
                                   bias=bias[:, n:n + 1]).then_inc(s_qk, 1)

                def copy_y4(c):
                    act.wait_ge(s_t3, c + 1)
                    reached(act, s_l2, c)
                    act.activation(yT4[:], Ta[:], ACT.Copy).then_inc(s_y4t, 1)

                def keep_y4(c):
                    act.activation(YT4[:, bass.ts(c, B), :], Ta[:], ACT.Copy).then_inc(s_y4t, 1)
                    act.activation(Y4[:, bass.ts(c, B), 0:D], z4[:], ACT.Copy).then_inc(s_kept, 1)

                for dst, src in ((w["WG"][:, 7, :], w["sg"]), (w["WU"][:, 7, :], w["su"]),
                                 (w["WD"][:, 7, :, :], w["sd"].rearrange("(c p) d -> p c d", p=P))):
                    act.dma_start(dst, src).then_inc(shared_loaded, 16)

                def turn(a, b, c, d):
                    if b is not None:
                        copy_y(b)
                    if c is not None:
                        copy_z(c)
                    if b is not None:
                        silu_u(b, 0)
                    if c is not None:
                        copy_qkv(c, 0)
                    if b is not None:
                        tanh(b)
                        silu_u(b, 1)
                    if c is not None:
                        copy_qkv(c, 1)
                        copy_qkv(c, 2)
                    if d is not None:
                        copy_y4(d)
                        keep_y4(d)
                    if b is not None:
                        silu_u(b, 2)
                        silu_u(b, 3)
                        copy_hidden(b, 0)
                        copy_hidden(b, 1)

                each_turn(act, turn)

            @block.tensor
            def _(pe):
                pe.wait_ge(s_w, mw.count)
                pe.wait_ge(s_cst, 3)

                def project1(c):
                    pe.wait_ge(s_att, c + 1)
                    reached(pe, s_r3, c - 2)
                    if isinstance(c, int) and c in (1, 2):
                        pe.wait_ge(s_r1 if c == 1 else s_r2, 1)
                    for b in range(B):
                        ins = pe.matmul(O[:, b, :], attT[:, b, :], ow[:], start=True, stop=True)
                    ins.then_inc(s_p1, 1)

                def transpose1(c):
                    pe.wait_ge(s_nm[0], c + 1)
                    reached(pe, s_swt, c * 2)
                    for b in range(B):
                        ins = pe.transpose(Ta[:, b, :], y[:, b, :], ident[:])
                    ins.then_inc(s_t1, 1)

                def logits1(c):
                    pe.wait_ge(s_yt, c + 1)
                    reached(pe, s_mx, c - 1)
                    for b in range(B):
                        ins = pe.matmul(S_LG1[:, b * EXP:b * EXP + EXP], yT[:, b, :], gate[:], start=True, stop=True)
                    ins.then_inc(s_l1, 1)

                def up(c, b):
                    reached(pe, s_sv, c * 4 + b - 1)
                    pe.matmul(flat(UV[b % 2]), yT[:, b, :], Wuv[:].rearrange("p a e r -> p (a e r)"),
                              start=True, stop=True).then_inc(s_uv, 1)

                def transpose_hidden(c, n):
                    T = Tb if n == 0 else Ta
                    if n == 0:
                        reached(pe, s_zt, c, CH)
                    else:
                        reached(pe, s_y4t, 2 * c - 2)
                    for b in range(2):
                        pe.wait_ge(s_sw, c * 4 + 2 * n + b + 1)
                        for k in range(2):
                            ins = pe.transpose(T[:, 2 * b + k, :], sw[b][:, k, :], ident[:])
                    ins.then_inc(s_tw, 1)

                def down(c):
                    pe.wait_ge(s_swt, c * 2 + 2)
                    reached(pe, s_r1, c + 2, CH)
                    if isinstance(c, int) and c == CH - 1:
                        pe.wait_ge(s_r3, c - 1)
                    for b in range(B):
                        for k in range(2):
                            ins = pe.matmul(O[:, b, :], swT[:, b, k, :], Wo[:, k, :], start=(k == 0), stop=(k == 1))
                    ins.then_inc(s_wo, 1)

                def transpose2(c):
                    pe.wait_ge(s_nm[1], c + 1)
                    reached(pe, s_at, c)
                    reached(pe, s_swt, c * 2 + 1, 2 * CH)
                    for b in range(B):
                        ins = pe.transpose(Tb[:, b, :], z[:, b, :], ident[:])
                    ins.then_inc(s_t2, 1)

                def project_qkv(c, n):
                    if n == 0:
                        pe.wait_ge(s_zt, c + 1)
                        reached(pe, s_av, c * 4)
                    if n == 2:
                        pe.wait_ge(s_qk, c * 3 + 1)
                    pe.matmul(flat(A[n % 2]), Win[:, n, :], flat(zT), start=True, stop=True).then_inc(s_pj, 1)

                def scores(c, l):
                    pe.wait_ge(s_pr[l % 2], c * 2 + l // 2 + 1)
                    if l < 2:
                        pe.wait_ge(s_qk, c * 3 + 2 + l)
                    else:
                        pe.wait_ge(s_av, c * 4 + l - 1)
                    for s in range(B):
                        ins = pe.matmul(A[(l + 1) % 2][:, s, :], sums[:, abs(l - s), :], prod[l % 2][:, s, :],
                                        start=True, stop=True)
                    ins.then_inc(s_a, 1)

                def denominators(c, l):
                    if l == 0:
                        reached(pe, s_lg, c + 2, CH)
                        reached(pe, s_lg2, c)
                    for s in range(B):
                        ins = pe.matmul(S_DN[32 * l:32 * l + 32, :], heads[:, abs(l - s), :], prod[l % 2][:, s, :],
                                        start=(s == 0), stop=(s == B - 1))
                    ins.then_inc(s_dp, 1)

                def spread_inverse(c):
                    pe.wait_ge(s_rc, c + 1)
                    reached(pe, s_swt, c * 2 + 3, 2 * CH)
                    for l in range(B):
                        ins = pe.matmul(Tb[:, l, :], spread[:, l, :], dn[:], start=True, stop=True)
                    ins.then_inc(s_ex, 1)

                def project3(c):
                    pe.wait_ge(s_at, c + 1)
                    reached(pe, s_r2, c + 2, CH)
                    if isinstance(c, int) and c == CH - 1:
                        pe.wait_ge(s_r3, c)
                    for b in range(B):
                        ins = pe.matmul(O[:, b, :], at[:, b, :], outw[:], start=True, stop=True)
                    ins.then_inc(s_p3, 1)

                def transpose3(c):
                    pe.wait_ge(s_nm[2], c + 1)
                    reached(pe, s_yt, c + 3, CH)
                    if isinstance(c, int) and c == CH - 1:
                        pe.wait_ge(s_y4t, 2 * c)
                    for b in range(B):
                        ins = pe.transpose(Ta[:, b, :], z4[:, b, :], ident[:])
                    ins.then_inc(s_t3, 1)

                def logits2(c):
                    pe.wait_ge(s_y4t, c * 2 + 1)
                    reached(pe, s_lg, c + 3, CH)
                    for b in range(B):
                        ins = pe.matmul(S_LG2[:, b * 8:b * 8 + 8], yT4[:, b, :], router[:], start=True, stop=True)
                    ins.then_inc(s_l2, 1)

                def turn(a, b, c, d):
                    if b is not None:
                        transpose1(b)
                        logits1(b)
                        up(b, 0)
                    if d is not None:
                        project3(d)
                    if b is not None:
                        up(b, 1)
                    if c is not None:
                        transpose2(c)
                    if a is not None:
                        project1(a)
                    if c is not None:
                        project_qkv(c, 0)
                        project_qkv(c, 1)
                        project_qkv(c, 2)
                    if d is not None:
                        transpose3(d)
                    if b is not None:
                        up(b, 2)
                    if c is not None:
                        scores(c, 0)
                    if d is not None:
                        logits2(d)
                    if c is not None:
                        scores(c, 1)
                        denominators(c, 0)
                        denominators(c, 1)
                    if b is not None:
                        up(b, 3)
                        transpose_hidden(b, 0)
                    if c is not None:
                        scores(c, 2)
                        denominators(c, 2)
                    if b is not None:
                        transpose_hidden(b, 1)
                    if c is not None:
                        scores(c, 3)
                        denominators(c, 3)
                    if b is not None:
                        down(b)
                    if c is not None:
                        spread_inverse(c)

                each_turn(pe, turn)


RTILES = TILES + 7
TOKENS = NBATCH * SEQ
ROW = D + 1
NEXP = 8


def order_tokens(nc, X, Y4, YT4, L2, slots, scale, experts, YS, w, shared_loaded, experts_loaded):
    with ExitStack() as ctx:
        def sb(name, shape, dt=F32):
            return ctx.enter_context(nc.sbuf_tensor("d_" + name, shape, dt))

        def sem(name):
            return ctx.enter_context(nc.semaphore("d_" + name))

        SH = [P, TILES, NEXP]
        numbers = sb("numbers", [P, TILES])
        before, ones = sb("before", [P, P]), sb("ones", [P, P])
        rows = sb("rows", [P, NEXP])
        tau = sb("tau", [1, RTILES])
        top, sm = sb("top", [P, TILES]), sb("sm", [P, TILES])
        dl, oh, sc = sb("dl", SH), sb("oh", SH), sb("sc", SH)
        run = [sb(f"run{i}", SH) for i in range(2)]
        ti = sb("ti", [P, NEXP], I32)
        tl = sb("tl", [P, NEXP])
        ends = [sb(f"ends{i}", [P, NEXP]) for i in range(2)]
        ct, both = sb("ct", [1, RTILES, 6]), sb("both", [1, RTILES + 2])
        sf = sb("sf", [P, TILES])
        HC = 4
        CH = TPB
        sg = [sb(f"sg{i}", [P, NBATCH * P]) for i in range(2)]
        hid = [sb(f"hid{i}", [P, HC, NBATCH * P]) for i in range(2)]
        WG, WU, WD = w["WG"], w["WU"], w["WD"]
        pR = ctx.enter_context(nc.psum_tensor("d_pR", SH, F32))
        pC = ctx.enter_context(nc.psum_tensor("d_pC", SH, F32))
        s_c, s_k, s_z = sem("const_loaded"), sem("const_steps"), sem("YS_padded")
        s_num = sem("numbers_set")
        s_dl, s_ex, s_d, s_oh, s_cnt = sem("shifted"), sem("exp_done"), sem("dve_steps"), sem("onehot"), sem("counted")
        pG, pU = [[ctx.enter_context(nc.psum_tensor(f"d_p{n}{i}", [P, 512], F32)) for i in range(2)] for n in "GU"]
        pO = ctx.enter_context(nc.psum_tensor("d_pO", [P, NBATCH, D], F32))
        s_slots, s_sc = sem("slots_done"), sem("scattered")
        s_g, s_u, s_sg, s_hid = sem("gate_made"), sem("up_made"), sem("silu_done"), sem("hidden_done")
        s_do, s_res = sem("down_made"), sem("residual_done")

        def each_chunk(eng, chunk):
            chunk(0, 0)
            chunk(1, 1)
            with eng.Fori(1, CH // 2) as v:
                chunk(v * 2, 0)
                chunk(v * 2 + 1, 1)

        with nc.Block() as block:
            @block.sync
            def _(sp):
                sp.dma_start(rows[:], w["down8"].partition_broadcast(P)).then_inc(s_c, 16)
                sp.dma_start(tau[:], w["tau"].rearrange("(a n) -> a n", a=1)).then_inc(s_c, 16)
                sp.dma_start(numbers[:], w["numbers"]).then_inc(s_c, 16)
                sp.dma_start(YS, w["pads"]).then_inc(s_z, 16)
                for dst, src in ((w["WG"][:, 0:7, :], w["gate_w"].rearrange("e d h -> d e h")),
                                 (w["WU"][:, 0:7, :], w["up_w"].rearrange("e d h -> d e h")),
                                 (w["WD"][:, 0:7, :, :].rearrange("p e c d -> p (e c) d"),
                                  w["down_w"].rearrange("e (c p) d -> p (e c) d", p=P))):
                    sp.dma_start(dst, src).then_inc(experts_loaded, 16)
                sp.wait_ge(experts_loaded, 3 * 16)

            @block.gpsimd
            def _(gp):
                gp.memset(before[:], 1.0).then_inc(s_k, 1)
                gp.wait_ge(s_k, 1)
                gp.affine_select(out=before[:], in_=before[:], compare_op=ALU.is_gt, fill=0.0, base=0,
                                 pattern=[[1, P]], channel_multiplier=-1).then_inc(s_k, 1)
                gp.memset(ones[:], 1.0).then_inc(s_k, 1)
                gp.wait_ge(s_c, 48)
                gp.tensor_copy(Y4[:, :, D:D + 1], numbers[:].unsqueeze(2)).then_inc(s_num, 1)
                gp.wait_ge(s_num, 1)
                gp.wait_ge(s_z, 16)

                gp.wait_ge(s_slots, 1)
                for n in range(TILES):
                    gp.indirect_dma_start(out=YS, out_offset=bass.IndirectOffsetOnAxis(ap=slots[:, n:n + 1], axis=0),
                                          in_=Y4[:, n, :], in_offset=None).then_inc(s_sc, 16)
                gp.wait_ge(s_sc, TILES * 16)

            @block.scalar
            def _(act):
                act.wait_ge(s_dl, 1)
                act.activation(dl[:], dl[:], ACT.Exp).then_inc(s_ex, 1)

                def chunk(i, par):
                    for c in range(HC):
                        m = i * HC + c
                        act.wait_ge(s_g, m + 1)
                        reached(act, s_hid, m - 1)
                        act.activation(sg[c % 2][:], pG[c % 2][:], ACT.Silu).then_inc(s_sg, 1)

                each_chunk(act, chunk)

            @block.tensor
            def _(pe):
                pe.wait_ge(shared_loaded, 3 * 16)

                def up(i, c):
                    m = i * HC + c
                    reached(pe, s_hid, m - 1)
                    tokens = YT4[:, bass.ts(i, NBATCH), :].rearrange("p t q -> p (t q)")
                    pe.matmul(pG[c % 2][:], WG[:, 7, c * P:c * P + P], tokens, start=True, stop=True).then_inc(s_g, 1)
                    pe.matmul(pU[c % 2][:], WU[:, 7, c * P:c * P + P], tokens, start=True,
                              stop=True).then_inc(s_u, 1)

                def down(i, par):
                    pe.wait_ge(s_hid, i * HC + HC)
                    reached(pe, s_res, i)
                    for b in range(NBATCH):
                        for c in range(HC):
                            ins = pe.matmul(pO[:, b, :], hid[par][:, c, b * P:b * P + P], WD[:, 7, c, :],
                                            start=(c == 0), stop=(c == HC - 1))
                    ins.then_inc(s_do, 1)

                def chunk(i, par):
                    up(i, 0)
                    up(i, 1)
                    if isinstance(i, int) and i == 0:
                        pe.wait_ge(s_k, 3)
                        pe.wait_ge(s_oh, 1)
                        flat_oh = oh[:].rearrange("p t e -> p (t e)")
                        pe.matmul(pR[:].rearrange("p t e -> p (t e)"), before[:], flat_oh, start=True, stop=True)
                        pe.matmul(pC[:].rearrange("p t e -> p (t e)"), ones[:], flat_oh, start=True,
                                  stop=True).then_inc(s_cnt, 1)
                    else:
                        down(i - 1, 1 - par)
                    up(i, 2)
                    up(i, 3)

                each_chunk(pe, chunk)
                down(CH - 1, 1)

            @block.vector
            def _(dve):
                steps = [0]
                SHARED_FROM, SHARED_EVERY = 6, 4

                def gate(i, par, c):
                    dve.wait_ge(s_sg, i * HC + c + 1)
                    dve.wait_ge(s_u, i * HC + c + 1)
                    if c == 0:
                        reached(dve, s_do, i - 1)
                    dve.tensor_tensor(hid[par][:, c, :], sg[c % 2][:], pU[c % 2][:], ALU.mult).then_inc(s_hid, 1)

                def add(i):
                    dve.wait_ge(s_do, i + 1)
                    x = X[:, :, :].rearrange("p (b i) d -> p i b d", b=NBATCH)[:, bass.ds(i, 1), :, :] \
                        .rearrange("p i b d -> p (i b) d")
                    dve.tensor_tensor(x, x, pO[:], ALU.add).then_inc(s_res, 1)

                def chunk(i, par):
                    if isinstance(i, int) and i == 0:
                        return
                    gate(i, par, 0)
                    gate(i, par, 1)
                    add(i - 1)
                    gate(i, par, 2)
                    gate(i, par, 3)

                def step(ins):
                    steps[0] += 1
                    ins.then_inc(s_d, 1)
                    c, rest = divmod(steps[0] - SHARED_FROM, SHARED_EVERY)
                    if rest == 0 and 0 <= c < HC:
                        gate(0, 0, c)
                    dve.wait_ge(s_d, steps[0])

                def wide(t):
                    return t[:].unsqueeze(2).broadcast_to(SH)

                dve.wait_ge(s_c, 48)
                step(dve.tensor_reduce(top[:], L2[:], AX.X, ALU.max))
                dve.tensor_tensor(dl[:], L2[:], wide(top), ALU.subtract).then_inc(s_dl, 1)
                step(dve.tensor_tensor(sc[:], L2[:], wide(top), ALU.is_equal))
                step(dve.tensor_tensor(sc[:], sc[:], rows[:].unsqueeze(1).broadcast_to(SH), ALU.mult))
                step(dve.tensor_reduce(top[:], sc[:], AX.X, ALU.max))
                dve.tensor_tensor(oh[:], sc[:], wide(top), ALU.is_equal).then_inc(s_oh, 1)
                dve.wait_ge(s_oh, 1)
                dve.wait_ge(s_ex, 1)
                step(dve.tensor_reduce(sm[:], dl[:], AX.X, ALU.add))
                step(dve.reciprocal(sm[:], sm[:]))
                step(dve.tensor_scalar(top[:], oh[:, :, 7], -2.0, 2.0, ALU.mult, ALU.add))
                step(dve.tensor_tensor(scale[:], sm[:], top[:], ALU.mult))
                dve.wait_ge(s_cnt, 1)
                step(dve.tensor_copy(run[0][:], pC[:]))
                k = 0
                for s in (1, 2, 4, 8, 16):
                    a, b = run[k], run[1 - k]
                    dve.tensor_copy(b[:, 0:s, :], a[:, 0:s, :])
                    step(dve.tensor_tensor(b[:, s:, :], a[:, s:, :], a[:, 0:TILES - s, :], ALU.add))
                    k = 1 - k
                step(dve.tensor_scalar(ti[:], run[k][:, TILES - 1, :], float(P - 1), None, ALU.add))
                step(dve.tensor_scalar(ti[:], ti[:], 7, None, ALU.arith_shift_right))
                step(dve.tensor_copy(tl[:], ti[:]))
                step(dve.tensor_copy(ends[0][:], tl[:]))
                j = 0
                for s in (1, 2, 4):
                    a, b = ends[j], ends[1 - j]
                    dve.tensor_copy(b[:, 0:s], a[:, 0:s])
                    step(dve.tensor_tensor(b[:, s:], a[:, s:], a[:, 0:NEXP - s], ALU.add))
                    j = 1 - j
                step(dve.tensor_tensor(ct[:], tau[:].unsqueeze(2).broadcast_to([1, RTILES, 6]),
                                       ends[j][0:1, 0:6].unsqueeze(1).broadcast_to([1, RTILES, 6]), ALU.is_ge))
                step(dve.tensor_reduce(tau[:], ct[:], AX.X, ALU.add))
                dve.memset(both[:, 0:2], 0.0)
                step(dve.tensor_scalar(both[:, 2:], tau[:], float(NEXP), None, ALU.mult))
                step(dve.tensor_tensor(both[:, 0:RTILES], both[:, 0:RTILES], tau[:], ALU.add))
                step(dve.tensor_copy(experts[:], both[:]))
                step(dve.tensor_tensor(tl[:], ends[j][:], tl[:], ALU.subtract))
                step(dve.tensor_scalar(tl[:], tl[:], float(P), None, ALU.mult))
                step(dve.tensor_tensor(run[k][:], run[k][:], pC[:], ALU.subtract))
                step(dve.tensor_tensor(run[k][:], run[k][:], pR[:], ALU.add))
                step(dve.tensor_tensor(run[k][:], run[k][:], tl[:].unsqueeze(1).broadcast_to(SH), ALU.add))
                step(dve.tensor_tensor(run[k][:], run[k][:], oh[:], ALU.mult))
                step(dve.tensor_reduce(sf[:], run[k][:], AX.X, ALU.add))
                dve.tensor_copy(slots[:], sf[:]).then_inc(s_slots, 1)
                each_chunk(dve, chunk)
                add(CH - 1)


def routed_experts(nc, WG, WU, WD, experts, YS, RO):
    with ExitStack() as ctx:
        def sb(name, shape, dt=F32):
            return ctx.enter_context(nc.sbuf_tensor("e_" + name, shape, dt))

        def sem(name):
            return ctx.enter_context(nc.semaphore("e_" + name))

        def two(name, shape):
            return [sb(f"{name}{i}", shape) for i in range(2)]

        HC = 4
        ident = sb("ident", [P, P])
        next_idx, idx = [[sb(f"{n}{i}", [P, 1], I32) for i in range(2)] for n in ("next_idx", "idx")]
        xin, xT, sg, h, hT, ro = (two(n, s) for n, s in (
            ("xin", [P, ROW]), ("xT", [P, P]), ("sg", [P, 512]), ("h", [P, HC, P]), ("hT", [P, HC, P]), ("ro", [P, D])))
        pX = ctx.enter_context(nc.psum_tensor("e_pX", [P, 512], F32))
        pG = [ctx.enter_context(nc.psum_tensor(f"e_pG{i}", [P, 512], F32)) for i in range(2)]
        pU = [ctx.enter_context(nc.psum_tensor(f"e_pU{i}", [P, 512], F32)) for i in range(2)]
        pH = ctx.enter_context(nc.psum_tensor("e_pH", [P, HC, P], F32))
        pO = ctx.enter_context(nc.psum_tensor("e_pO", [P, 512], F32))
        s_k = sem("const_steps")
        s_in, s_ro = [[sem(f"{n}{i}") for i in range(2)] for n in ("tile_loaded", "tile_stored")]
        s_tx, s_xt, s_g, s_u, s_sg, s_h = (sem("pX_made"), sem("xT_copied"), sem("gate_made"), sem("up_made"),
                                           sem("silu_done"), sem("h_done"))
        s_ni, s_ix, s_pass = sem("numbers_read"), sem("indices_moved"), sem("passed")
        s_th, s_ht, s_o, s_oc = sem("pH_made"), sem("hT_copied"), sem("pO_made"), sem("ro_copied")

        def each_turn(eng, turn):
            full = ("next", "this", "last", "before")
            turn(0, 0, 0, full[:2])
            turn(1, 1, 0, full[:3])
            turn(2, 0, 1, full)
            turn(3, 1, 1, full)
            turn(4, 0, 2, full)
            with eng.Fori(2, (RTILES - 4) // 2) as v:
                turn(v * 2 + 1, 1, v, full)
                turn(v * 2 + 2, 0, v + 1, full)
            for t in range((RTILES - 4) // 2 * 2 + 1, RTILES + 2):
                turn(t, t % 2, t // 2, [n for n, tile in zip(full, (t + 1, t, t - 1, t - 2)) if tile < RTILES])

        def uses(par, half, ahead):
            return half + (par + ahead) // 2 + 1

        with nc.Block() as block:
            @block.sync
            def _(sp):
                def load(t, k):
                    sp.dma_start(xin[k][:], YS[bass.ts(t, P), :]).then_inc(s_in[k], 16)

                load(0, 0)
                load(1, 1)

                def turn(t, par, half, which):
                    if isinstance(t, int) and t == 0:
                        sp.wait_ge(s_tx, 1)
                        sp.wait_ge(s_ni, 1)
                        load(2, 0)
                    if not (isinstance(t, int) and t + 3 >= RTILES):
                        sp.wait_ge(s_tx, t + 2)
                        sp.wait_ge(s_ni, t + 2)
                        load(t + 3, 1 - par)

                each_turn(sp, turn)

            @block.gpsimd
            def _(gp):
                gp.memset(ident[:], 0.0).then_inc(s_k, 1)
                gp.wait_ge(s_k, 1)
                gp.affine_select(out=ident[:], in_=ident[:], compare_op=ALU.not_equal, fill=1.0, base=0,
                                 pattern=[[-1, P]], channel_multiplier=1).then_inc(s_k, 1)

                def read_numbers(t, k, loads):
                    wait_apart(gp, s_in[k], loads * 16, s_pass)
                    gp.tensor_copy(next_idx[k][:], xin[k][:, D:D + 1]).then_inc(s_ni, 1)

                def turn(t, par, half, which):
                    if isinstance(t, int) and t == 0:
                        read_numbers(0, 0, 1)
                    if "last" in which:
                        wait_apart(gp, s_ni, t, s_pass)
                        if not (isinstance(t, int) and t < 3):
                            wait_apart(gp, s_ro[1 - par], (uses(par, half, -1) - 1) * 16, s_pass)
                        gp.tensor_copy(idx[1 - par][:], next_idx[1 - par][:]).then_inc(s_ix, 1)
                    if "next" in which:
                        if not (isinstance(t, int) and t < 1):
                            wait_apart(gp, s_ix, t, s_pass)
                        read_numbers(t + 1, 1 - par, uses(par, half, 1))
                    if "before" in which:
                        wait_apart(gp, s_oc, t - 1, s_pass)
                        wait_apart(gp, s_ix, t - 1, s_pass)
                        gp.indirect_dma_start(out=RO,
                                              out_offset=bass.IndirectOffsetOnAxis(ap=idx[par][:, 0:1], axis=0),
                                              in_=ro[par][:, :], in_offset=None).then_inc(s_ro[par], 16)

                each_turn(gp, turn)
                gp.wait_ge(s_ro[0], (RTILES + 1) // 2 * 16)
                gp.wait_ge(s_ro[1], RTILES // 2 * 16)

            @block.tensor
            def _(pe):
                pe.wait_ge(s_k, 2)

                def transpose_in(t, k, loads):
                    pe.wait_ge(s_in[k], loads * 16)
                    reached(pe, s_xt, t)
                    pe.transpose(pX[:, 0:P], xin[k][:, 0:D], ident[:]).then_inc(s_tx, 1)

                def turn(t, par, half, which):
                    both = pe.value_load(experts[0:1, bass.ds(t, 1)], min_val=0, max_val=8 * 6 + 6)
                    up_e, down_e = both % 8, both // 8
                    if isinstance(t, int) and t == 0:
                        transpose_in(0, 0, 1)
                    if "next" in which:
                        transpose_in(t + 1, 1 - par, uses(par, half, 1))
                    if "before" in which:
                        pe.wait_ge(s_ht, t - 1)
                        reached(pe, s_oc, t - 2)
                        for c in range(HC):
                            ins = pe.matmul(pO[:, 0:D], hT[par][:, c, :],
                                            WD[:, bass.ds(down_e, 1), c, :].rearrange("p e n -> p (e n)"),
                                            start=(c == 0), stop=(c == HC - 1))
                        ins.then_inc(s_o, 1)
                    if "last" in which:
                        pe.wait_ge(s_h, t)
                        reached(pe, s_ht, t - 1)
                        for c in range(HC):
                            ins = pe.transpose(pH[:, c, :], h[1 - par][:, c, :], ident[:])
                        ins.then_inc(s_th, 1)
                    if "this" in which:
                        pe.wait_ge(s_xt, t + 1)
                        reached(pe, s_h, t - 1)
                        pe.matmul(pG[par][:], xT[par][:], WG[:, bass.ds(up_e, 1), :].rearrange("p e n -> p (e n)"),
                                  start=True, stop=True).then_inc(s_g, 1)
                        pe.matmul(pU[par][:], xT[par][:], WU[:, bass.ds(up_e, 1), :].rearrange("p e n -> p (e n)"),
                                  start=True, stop=True).then_inc(s_u, 1)

                each_turn(pe, turn)

            @block.scalar
            def _(act):
                def copy_in(t, k):
                    act.wait_ge(s_tx, t + 1)
                    reached(act, s_u, t - 1)
                    act.activation(xT[k][:], pX[:, 0:P], ACT.Copy).then_inc(s_xt, 1)

                def turn(t, par, half, which):
                    if isinstance(t, int) and t == 0:
                        copy_in(0, 0)
                    if "next" in which:
                        copy_in(t + 1, 1 - par)
                    if "before" in which:
                        act.wait_ge(s_o, t - 1)
                        reached(act, s_ro[par], (uses(par, half, -2) - 1) * 16)
                        act.activation(ro[par][:], pO[:, 0:D], ACT.Copy).then_inc(s_oc, 1)
                    if "this" in which:
                        act.wait_ge(s_g, t + 1)
                        reached(act, s_h, t - 1)
                        act.activation(sg[par][:], pG[par][:], ACT.Silu).then_inc(s_sg, 1)

                each_turn(act, turn)

            @block.vector
            def _(dve):
                def turn(t, par, half, which):
                    if "last" in which:
                        dve.wait_ge(s_th, t)
                        reached(dve, s_o, t - 2)
                        dve.tensor_copy(hT[1 - par][:], pH[:]).then_inc(s_ht, 1)
                    if "this" in which:
                        dve.wait_ge(s_sg, t + 1)
                        dve.wait_ge(s_u, t + 1)
                        reached(dve, s_th, t - 1)
                        dve.tensor_tensor(h[par][:].rearrange("p c n -> p (c n)"), sg[par][:], pU[par][:],
                                          ALU.mult).then_inc(s_h, 1)

                each_turn(dve, turn)


def finish(nc, X, scale, RO, out):
    with ExitStack() as ctx:
        def sem(name):
            return ctx.enter_context(nc.semaphore("f_" + name))

        G = ctx.enter_context(nc.sbuf_tensor("f_routed", [P, TILES, D], F32))
        s_g = [sem(f"routed{i}_loaded") for i in range(TPB)]
        s_a, s_out = sem("added"), sem("stored")

        with nc.Block() as block:
            @block.scalar
            def _(act):
                for i in range(TPB):
                    act.dma_start(G[:, i * NBATCH:(i + 1) * NBATCH, :],
                                  RO[0:TOKENS, :].rearrange("(b i p) d -> i p b d", b=NBATCH, i=TPB)[i]).then_inc(s_g[i], 16)

            @block.vector
            def _(dve):
                for i in range(TPB):
                    dve.wait_ge(s_g[i], 16)
                    for b in range(NBATCH):
                        n = i * NBATCH + b
                        ins = dve.scalar_tensor_tensor(out=X[:, TPB * b + i, :], in0=G[:, n, :],
                                                       scalar=scale[:, n:n + 1], in1=X[:, TPB * b + i, :],
                                                       op0=ALU.mult, op1=ALU.add)
                    ins.then_inc(s_a, 1)

            @block.sync
            def _(sp):
                with sp.Fori(0, TPB) as i:
                    sp.wait_ge(s_a, i + 1)
                    sp.dma_start(out[:, bass.ts(i, P), :].rearrange("b p d -> p b d"),
                                 X[:, :, :].rearrange("p (b i) d -> p i b d", b=NBATCH)[:, bass.ds(i, 1), :, :]
                                 .rearrange("p i b d -> p (i b) d")).then_inc(s_out, 16)
                sp.wait_ge(s_out, TPB * 16)


def build(nc, w, out):
    QD = nc.dram_tensor("q_stacks", [QUADS, 4, ROWS, SEQ], BF16, kind="Internal").ap()
    KD = nc.dram_tensor("k_stacks", [QUADS, 4, ROWS, SEQ], BF16, kind="Internal").ap()
    MD = nc.dram_tensor("neg_maxima", [96, P], BF16, kind="Internal").ap()
    ND = nc.dram_tensor("attended", [QUADS, 4, HD + 1, SEQ], F32, kind="Internal").ap()
    RD = nc.dram_tensor("inverse_dens", [NBATCH * HEADS, SEQ], F32, kind="Internal").ap()
    YS = nc.dram_tensor("sorted_in", [RTILES * P, ROW], F32, kind="Internal").ap()
    RO = nc.dram_tensor("routed", [TOKENS + RTILES * P, D], F32, kind="Internal").ap()
    with ExitStack() as ctx:
        def sb(name, shape, dt=F32):
            return ctx.enter_context(nc.sbuf_tensor(name, shape, dt))

        X = sb("x", [P, TILES, D])
        mw = MiddleWeights(nc, ctx)
        with nc.sbuf_tensor("v_by_quads", [P, QUADS, TPB, 32], F32) as VS, ExitStack() as stacks:
            bufs = StackBuffers(nc, stacks)
            project_and_rotate(nc, X, VS, bufs, w["x"], w["cos"], w["sin"], w["qw"], w["qws"], w["kw"], w["kws"],
                               w["vw"], QD, KD)
            attend(nc, VS, bufs, lambda queue: mw.load(queue, w), QD, KD, MD, ND)
        WG, WU, WD = sb("WG", [P, NEXP, 512]), sb("WU", [P, NEXP, 512]), sb("WD", [P, NEXP, 4, D])
        Y4, L2 = sb("y4", [P, TILES, ROW]), sb("logits2", [P, TILES, NEXP])
        slots, scale = sb("slots", [P, TILES], I32), sb("scale", [P, TILES])
        experts = sb("experts", [1, RTILES + 2], I32)
        shared_loaded = ctx.enter_context(nc.semaphore("shared_weights_loaded"))
        experts_loaded = ctx.enter_context(nc.semaphore("expert_weights_loaded"))
        w = {**w, "WG": WG, "WU": WU, "WD": WD}
        with nc.sbuf_tensor("y4T", [P, TILES, P], F32) as YT4:
            middle_layers(nc, X, Y4, YT4, L2, ND, RD, mw, w, shared_loaded)
            order_tokens(nc, X, Y4, YT4, L2, slots, scale, experts, YS, w, shared_loaded, experts_loaded)
        routed_experts(nc, WG, WU, WD, experts, YS, RO)
        finish(nc, X, scale, RO, out)


def host_arrays(i):
    cos, sin = tables()
    swap = np.arange(D) ^ 1
    e = np.arange(8)
    sums, heads, spread = head_sums()
    tile = np.arange(TILES)
    numbers = tile[None, :] % NBATCH * SEQ + tile[None, :] // NBATCH * P + np.arange(P)[:, None]
    pads = np.zeros((RTILES * P, ROW), np.float32)
    pads[:, D] = TOKENS + np.arange(RTILES * P)
    return {
        "numbers": numbers.astype(np.float32), "pads": pads,
        "x": i["L0_attn_x"], "cos": cos, "sin": sin,
        "qw": i["L0_attn_qw"], "qws": i["L0_attn_qw"][:, swap],
        "kw": i["L0_attn_kw"], "kws": i["L0_attn_kw"][:, swap],
        "vw": i["L0_attn_vw"], "ow": i["L0_attn_ow"],
        "gate": i["L0_ffn_gate_w"], "Wu": i["L0_ffn_Wu"], "Wv": i["L0_ffn_Wv"], "Wo": i["L0_ffn_Wo"],
        "Win": i["L1_attn_in_proj_weight"].T, "bias": i["L1_attn_in_proj_bias"].reshape(3, D).T,
        "outw": i["L1_attn_out_w"].T, "outb": i["L1_attn_out_b"], "router": i["L1_ffn_router_w"],
        "up_w": i["L1_ffn_up_w"], "gate_w": i["L1_ffn_gate_w"], "down_w": i["L1_ffn_down_w"],
        "su": i["L1_ffn_shared_up_w"], "sg": i["L1_ffn_shared_gate_w"], "sd": i["L1_ffn_shared_down_w"],
        "sums": sums, "heads": heads, "spread": spread, "tri": (e[:, None] > e[None, :]).astype(np.float32).reshape(64),
        "down8": (8 - e).astype(np.float32), "tau": np.arange(RTILES, dtype=np.float32),
    }


def kernel(**inputs):
    import concourse.bacc as bacc
    from concourse.bass_utils import run_bass_kernel_spmd

    nc = bacc.Bacc("TRN2", target_bir_lowering=False, num_devices=1)
    arrays, args = {}, {}
    for name, a in host_arrays({k: np.asarray(v) for k, v in inputs.items()}).items():
        a = np.ascontiguousarray(a)
        arrays[f"in_{name}"] = a
        args[name] = nc.dram_tensor(f"in_{name}", a.shape, mybir.dt.from_np(a.dtype), kind="ExternalInput").ap()
    out = nc.dram_tensor("out", (NBATCH, SEQ, D), F32, kind="ExternalOutput").ap()
    build(nc, args, out)
    result = run_bass_kernel_spmd(nc, [arrays], core_ids=[0])
    return result.results[0]["out"]
```
